# Optimizing a Trainium2 kernel written in Bass

```python
import numpy as np
import jax
import jax.numpy as jnp

def _softmax(x, axis=-1):
    return jax.nn.softmax(x, axis=axis)

def _gelu(x):
    return jax.nn.gelu(x, approximate=True)

def _silu(x):
    return jax.nn.silu(x)

def _sigmoid(x):
    return jax.nn.sigmoid(x)

def _layernorm(x, axis=-1, eps=1e-05):
    m = jnp.mean(x, axis=axis, keepdims=True)
    v = jnp.var(x, axis=axis, keepdims=True)
    return (x - m) / jnp.sqrt(v + eps)

def _scatter_add(tgt, idx, src, axis=0):
    return tgt.at[idx].add(src)

def _segment_sum(src, seg, n):
    return jax.ops.segment_sum(src, seg, n)
kernel_name = 'mk_gps_d1_gnn_r8_dd13a8'

def setup_inputs(seed: int=0):
    np.random.seed(seed)
    _w = jnp.asarray

    def _rec_inputs():
        import jax
        import jax.numpy as jnp
        _gk = jax.random.key(seed)
        x = -0.0003713 + 1 * jax.random.normal(jax.random.fold_in(_gk, 1), (6250, 256), jnp.float32)
        src = jax.random.randint(jax.random.fold_in(_gk, 2), (100000,), 0, 6250, jnp.int32)
        dst = jax.random.randint(jax.random.fold_in(_gk, 3), (100000,), 0, 6250, jnp.int32)
        _o = jnp.argsort(dst, stable=True)
        src = src[_o]
        dst = dst[_o]
        return (x, src, dst)
    x, src, dst = _rec_inputs()

    def _L0_gnn_setup():
        import jax, jax.numpy as jnp
        import numpy as np
        N = 6250
        DIM = 256
        E = 100000

        def _srgnn_conv(x, W, b, src, dst, num_nodes):
            xl = x @ W.T + b
            msgs = xl[src]
            agg = jax.ops.segment_sum(msgs, dst, num_segments=num_nodes)
            cnt = jax.ops.segment_sum(jnp.ones((src.shape[0],), x.dtype), dst, num_segments=num_nodes)
            return agg / jnp.maximum(cnt, 1.0)[:, None]
        key = jax.random.key(seed)
        ks = jax.random.split(key, 11)
        stdv = 1.0 / np.sqrt(DIM)
        u = lambda k, shape: jax.random.uniform(k, shape, jnp.float32, -stdv, stdv)
        hidden = jax.random.normal(ks[0], (N, DIM), jnp.float32)
        edge_index = jax.random.randint(ks[1], (2, E), 0, N, jnp.int64)
        return {'hidden': hidden, 'edge_index': edge_index, 'W_in': u(ks[2], (DIM, DIM)), 'b_in': u(ks[3], (DIM,)), 'W_out': u(ks[4], (DIM, DIM)), 'b_out': u(ks[5], (DIM,)), 'W_ih': u(ks[6], (3 * DIM, 2 * DIM)), 'b_ih': u(ks[7], (3 * DIM,)), 'W_hh': u(ks[8], (3 * DIM, DIM)), 'b_hh': u(ks[9], (3 * DIM,))}
    _L0_gnn_all = _L0_gnn_setup()
    _L0_gnn_in = {k: v for k, v in _L0_gnn_all.items() if k in ('W_in', 'b_in', 'W_out', 'b_out', 'W_ih', 'b_ih', 'W_hh', 'b_hh')}
    del _L0_gnn_all

    def _L0_mix_setup():
        import jax, jax.numpy as jnp
        import numpy as np
        B, L, D, H = (4, 2048, 256, 8)
        DK = D // H

        def _heads(t):
            b, l, d = t.shape
            return t.reshape(b, l, H, DK).transpose(0, 2, 1, 3)
        key = jax.random.key(seed)
        ks = jax.random.split(key, 9)
        s = 0.02
        return {'x': jax.random.normal(ks[0], (B, L, D), dtype=jnp.float32), 'Wq': jax.random.normal(ks[1], (D, D), dtype=jnp.float32) * s, 'bq': jnp.zeros((D,), dtype=jnp.float32), 'Wk': jax.random.normal(ks[2], (D, D), dtype=jnp.float32) * s, 'bk': jnp.zeros((D,), dtype=jnp.float32), 'Wv': jax.random.normal(ks[3], (D, D), dtype=jnp.float32) * s, 'bv': jnp.zeros((D,), dtype=jnp.float32), 'Wfc': jax.random.normal(ks[4], (D, D), dtype=jnp.float32) * s, 'bfc': jnp.zeros((D,), dtype=jnp.float32)}
    _L0_mix_all = _L0_mix_setup()
    _L0_mix_in = {k: v for k, v in _L0_mix_all.items() if k in ('Wq', 'bq', 'Wk', 'bk', 'Wv', 'bv', 'Wfc', 'bfc')}
    del _L0_mix_all

    def _L0_ffn_setup():
        import jax, jax.numpy as jnp
        import numpy as np
        B, S, D, E, H, K = (4, 512, 256, 8, 512, 2)
        key = jax.random.key(seed)
        ks = jax.random.split(key, 6)
        x = jax.random.normal(ks[0], (B, S, D), jnp.float32)
        Wg = jax.random.normal(ks[1], (D, E), jnp.float32) * 0.02
        bg = jnp.zeros((E,), jnp.float32)
        W1 = jax.random.normal(ks[2], (E, D, H), jnp.float32) * 0.02
        b1 = jnp.zeros((E, H), jnp.float32)
        W2 = jax.random.normal(ks[3], (E, H, D), jnp.float32) * 0.02
        b2 = jnp.zeros((E, D), jnp.float32)
        return {'x': x, 'Wg': Wg, 'bg': bg, 'W1': W1, 'b1': b1, 'W2': W2, 'b2': b2}
    _L0_ffn_all = _L0_ffn_setup()
    _L0_ffn_in = {k: v for k, v in _L0_ffn_all.items() if k in ('Wg', 'bg', 'W1', 'b1', 'W2', 'b2')}
    del _L0_ffn_all
    return {'x': x, 'src': src, 'dst': dst, 'L0_gnn_W_in': _L0_gnn_in['W_in'], 'L0_gnn_b_in': _L0_gnn_in['b_in'], 'L0_gnn_W_out': _L0_gnn_in['W_out'], 'L0_gnn_b_out': _L0_gnn_in['b_out'], 'L0_gnn_W_ih': _L0_gnn_in['W_ih'], 'L0_gnn_b_ih': _L0_gnn_in['b_ih'], 'L0_gnn_W_hh': _L0_gnn_in['W_hh'], 'L0_gnn_b_hh': _L0_gnn_in['b_hh'], 'L0_mix_Wq': _L0_mix_in['Wq'], 'L0_mix_bq': _L0_mix_in['bq'], 'L0_mix_Wk': _L0_mix_in['Wk'], 'L0_mix_bk': _L0_mix_in['bk'], 'L0_mix_Wv': _L0_mix_in['Wv'], 'L0_mix_bv': _L0_mix_in['bv'], 'L0_mix_Wfc': _L0_mix_in['Wfc'], 'L0_mix_bfc': _L0_mix_in['bfc'], 'L0_ffn_Wg': _L0_ffn_in['Wg'], 'L0_ffn_bg': _L0_ffn_in['bg'], 'L0_ffn_W1': _L0_ffn_in['W1'], 'L0_ffn_b1': _L0_ffn_in['b1'], 'L0_ffn_W2': _L0_ffn_in['W2'], 'L0_ffn_b2': _L0_ffn_in['b2']}

def reference(x, src, dst, L0_gnn_W_in, L0_gnn_b_in, L0_gnn_W_out, L0_gnn_b_out, L0_gnn_W_ih, L0_gnn_b_ih, L0_gnn_W_hh, L0_gnn_b_hh, L0_mix_Wq, L0_mix_bq, L0_mix_Wk, L0_mix_bk, L0_mix_Wv, L0_mix_bv, L0_mix_Wfc, L0_mix_bfc, L0_ffn_Wg, L0_ffn_bg, L0_ffn_W1, L0_ffn_b1, L0_ffn_W2, L0_ffn_b2):
    import jax
    import jax.numpy as jnp

    def _L0_gnn_ref(hidden, edge_index, W_in, b_in, W_out, b_out, W_ih, b_ih, W_hh, b_hh):
        import jax, jax.numpy as jnp
        import numpy as np
        N = 6250
        DIM = 256
        E = 100000

        def _srgnn_conv(x, W, b, src, dst, num_nodes):
            xl = x @ W.T + b
            msgs = xl[src]
            agg = jax.ops.segment_sum(msgs, dst, num_segments=num_nodes)
            cnt = jax.ops.segment_sum(jnp.ones((src.shape[0],), x.dtype), dst, num_segments=num_nodes)
            return agg / jnp.maximum(cnt, 1.0)[:, None]
        src, dst = (edge_index[0], edge_index[1])
        n = hidden.shape[0]
        input_in = _srgnn_conv(hidden, W_in, b_in, src, dst, n)
        input_out = _srgnn_conv(hidden, W_out, b_out, dst, src, n)
        inputs = jnp.concatenate([input_in, input_out], axis=-1)
        gi = inputs @ W_ih.T + b_ih
        gh = hidden @ W_hh.T + b_hh
        i_r, i_i, i_n = jnp.split(gi, 3, axis=-1)
        h_r, h_i, h_n = jnp.split(gh, 3, axis=-1)
        reset_gate = jax.nn.sigmoid(i_r + h_r)
        input_gate = jax.nn.sigmoid(i_i + h_i)
        new_gate = jnp.tanh(i_n + reset_gate * h_n)
        return (1.0 - input_gate) * hidden + input_gate * new_gate

    def _L0_mix_ref(x, Wq, bq, Wk, bk, Wv, bv, Wfc, bfc):
        import jax, jax.numpy as jnp
        import numpy as np
        B, L, D, H = (4, 2048, 256, 8)
        DK = D // H

        def _heads(t):
            b, l, d = t.shape
            return t.reshape(b, l, H, DK).transpose(0, 2, 1, 3)
        q = _heads(x @ Wq.T + bq)
        k = _heads(x @ Wk.T + bk)
        v = _heads(x @ Wv.T + bv)
        seq_len = q.shape[-2]
        p_attn = jnp.einsum('bhnd,bhne->bhde', k, v) / seq_len
        out = jnp.einsum('bhnd,bhde->bhne', q, p_attn)
        out = out.transpose(0, 2, 1, 3).reshape(x.shape[0], seq_len, H * DK)
        return out @ Wfc.T + bfc

    def _L0_ffn_ref(x, Wg, bg, W1, b1, W2, b2):
        import jax, jax.numpy as jnp
        import numpy as np
        B, S, D, E, H, K = (4, 512, 256, 8, 512, 2)
        Bv, Sv, Dv = x.shape
        gate_scores = x @ Wg + bg
        _, idx = jax.lax.top_k(gate_scores, K)
        mask = jax.nn.one_hot(idx, E, dtype=x.dtype).sum(axis=-2)
        xf = x.reshape(-1, Dv)
        mf = mask.reshape(-1, E)
        h = jax.nn.gelu(jnp.einsum('td,edh->teh', xf, W1) + b1[None], approximate=False)
        y = jnp.einsum('teh,ehd->ted', h, W2) + b2[None]
        out = jnp.einsum('ted,te->td', y, mf)
        return out.reshape(Bv, Sv, Dv)
    edge_index = jnp.stack([src, dst])
    xn = _layernorm(x, axis=-1)
    x = x + _L0_gnn_ref(xn, edge_index, L0_gnn_W_in, L0_gnn_b_in, L0_gnn_W_out, L0_gnn_b_out, L0_gnn_W_ih, L0_gnn_b_ih, L0_gnn_W_hh, L0_gnn_b_hh) + _L0_mix_ref(xn[None], L0_mix_Wq, L0_mix_bq, L0_mix_Wk, L0_mix_bk, L0_mix_Wv, L0_mix_bv, L0_mix_Wfc, L0_mix_bfc)[0]
    x = x + _L0_ffn_ref(_layernorm(x, axis=-1)[None], L0_ffn_Wg, L0_ffn_bg, L0_ffn_W1, L0_ffn_b1, L0_ffn_W2, L0_ffn_b2)[0]
    return x

_drawn_inputs = setup_inputs


def setup_inputs(seed=0):
    import zlib

    import numpy as np

    out = dict(_drawn_inputs(seed))
    spreads = {'L0_mix_bq': (0.0, 0.8),
     'L0_mix_bk': (0.0, 0.8),
     'L0_mix_bv': (0.0, 0.8),
     'L0_mix_bfc': (0.0, 0.8),
     'L0_ffn_bg': (0.0, 0.8),
     'L0_ffn_b1': (0.0, 2.0),
     'L0_ffn_b2': (0.0, 0.8)}
    factors = {'L0_gnn_b_in': 36.64,
     'L0_gnn_b_out': 34.84,
     'L0_gnn_b_ih': 27.904,
     'L0_gnn_b_hh': 33.8,
     'L0_mix_Wq': 6.438,
     'L0_mix_Wk': 8.0,
     'L0_mix_Wv': 7.769,
     'L0_mix_Wfc': 6.402,
     'L0_gnn_W_in': 8.0,
     'L0_gnn_W_out': 8.0,
     'L0_gnn_W_ih': 8.0,
     'L0_gnn_W_hh': 5.471,
     'L0_ffn_Wg': 5.708,
     'L0_ffn_W1': 8.0,
     'L0_ffn_W2': 6.141}
    for name, (base, spread) in spreads.items():
        noise = np.random.default_rng([zlib.crc32(name.encode()), seed]).standard_normal(out[name].shape)
        drawn = base * np.exp(spread * noise) if base else spread * noise
        out[name] = jnp.asarray(drawn.astype(out[name].dtype))
    for name, factor in factors.items():
        out[name] = (out[name] * factor).astype(out[name].dtype)
    return out
```

```python
import concourse.bass as bass
from concourse import mybir
from contextlib import ExitStack

F32 = mybir.dt.float32
F32R = mybir.dt.float32r
F16 = mybir.dt.float16
I32 = mybir.dt.int32
U32 = mybir.dt.uint32
U16 = mybir.dt.uint16
ALU = mybir.AluOpType
ACT = mybir.ActivationFunctionType
AX = mybir.AxisListType

P = 128
NODES = 6250
D = 256
NBLK = -(-NODES // P)
TAIL = NODES - (NBLK - 1) * P
EDGES = 100000
EP = 125
EC = EDGES // EP
HEADS = 8
DK = D // HEADS
NEXP = 8
HID = 512
EPS = 1e-5

GROUP = 4
RING = 4


def whole(n, m):
    return -(-n // m) * m


ETILES = whole((EDGES + NBLK * (P - 1)) // P, GROUP * RING)
XTILES = whole((2 * NBLK * P + NEXP * (P - 1)) // P, RING)
SHIFT = 13
NONE_PAYLOAD = 255 << SHIFT
ACOLS = D + 2
WCOLS = 20 * D
GCOLS = 5 * D


class Count:

    def __init__(self, sem):
        self.sem, self.n = sem, 0

    def after(self, eng, ins):
        self.n += 1
        ins.then_inc(self.sem, 1)
        eng.wait_ge(self.sem, self.n)


def constants(nc, T, s):
    with nc.Block() as block:
        @block.gpsimd
        def _(pool):
            c = Count(s("const_chain"))
            for t, v in ((T.ident, 0.0), (T.ident1, 0.0), (T.ident128, 0.0), (T.upper, 1.0),
                         (T.colsel, 0.0), (T.ones16, 1.0), (T.zeros16, 0.0), (T.expo, 0.0)):
                c.after(pool, nc.gpsimd.memset(t[:, :], v))
            for t, v in ((T.ident, 1.0), (T.ident1, 1.0), (T.ident128, 128.0)):
                c.after(pool, nc.gpsimd.affine_select(
                    out=t[:, :], in_=t[:, :], pattern=[[-1, P]], compare_op=ALU.not_equal,
                    fill=v, base=0, channel_multiplier=1))
            c.after(pool, nc.gpsimd.affine_select(
                out=T.upper[:, :], in_=T.upper[:, :], pattern=[[1, P]], compare_op=ALU.is_gt,
                fill=0.0, base=0, channel_multiplier=-1))
            c.after(pool, nc.gpsimd.memset(T.colsel[:, 63:64], 1.0))
            c.after(pool, nc.gpsimd.iota(T.ramp_i[:, :], pattern=[[1, ETILES]], base=0,
                                         channel_multiplier=0))
            c.after(pool, nc.gpsimd.tensor_copy(T.ramp16[:, :], T.ramp_i[:, :]))
            c.after(pool, nc.gpsimd.tensor_copy(T.ramp32[:, :], T.ramp_i[:, 0:P]))


def rstd_steps(nc, dve, c, st, mean, rstd, tmp):
    me, ve = st[:, :, 1], st[:, :, 2]
    mo, vo = st[:, :, 4], st[:, :, 5]
    c.after(dve, nc.vector.tensor_tensor(mean, me, mo, ALU.add))
    c.after(dve, nc.vector.tensor_tensor(tmp, me, mo, ALU.subtract))
    c.after(dve, nc.vector.tensor_tensor(rstd, ve, vo, ALU.add))
    c.after(dve, nc.vector.tensor_scalar(mean, mean, 0.5, None, ALU.mult))
    c.after(dve, nc.vector.tensor_tensor(tmp, tmp, tmp, ALU.mult))
    c.after(dve, nc.vector.tensor_scalar(rstd, rstd, 1.0 / D, EPS, ALU.mult, ALU.add))
    c.after(dve, nc.vector.scalar_tensor_tensor(out=rstd, in0=tmp, scalar=0.25, in1=rstd,
                                                op0=ALU.mult, op1=ALU.add))


class Gate:

    def __init__(self, passed):
        self.passed = passed

    def wait(self, eng, sem, value):
        eng.wait_ge(sem, value)
        eng.sem_inc(self.passed, 1)


def behind(b, n):
    return not isinstance(b, int) or b >= n


def pairs(n, eng, body, first=0):
    m = (n - first) // 2
    if m:
        with eng.Fori(0, m) as j:
            for k in range(2):
                body(j * 2 + (first + k), k)
    if (n - first) % 2:
        body(n - 1, 0)


def normalise(nc, A, T, s):
    ctx = ExitStack()
    with ctx:
        def sb(name, shape, dt=F32):
            return ctx.enter_context(nc.sbuf_tensor(name, shape, dt))
        X = sb("X", [P, NBLK, D])
        XN = sb("XN", [P, NBLK, D])
        st = sb("st", [P, NBLK, 6])
        mean, rstd, tmp = sb("mean", [P, NBLK]), sb("rstd", [P, NBLK]), sb("tmp", [P, NBLK])
        xhi = sb("xhi", [P, 2, ACOLS], F32R)
        xlo = sb("xlo", [P, 2, D], F32R)
        pg = ctx.enter_context(nc.psum_tensor("pg", [P, 2, 512], F32))
        block = ctx.enter_context(nc.Block())
        NG = 7
        x_in = [s(f"x_in{g}") for g in range(NBLK // NG)]
        tail_clear, tail_in, stats, var_ok, sd_ok, xn_ok, xs_ok = (
            s(n) for n in ("tail_clear", "tail_in", "stats", "var_ok", "sd_ok", "xn_ok", "xs_ok"))
        stored, hi_ok, lo_ok, gram_used, chain, mm = (
            s(n) for n in ("stored", "hi_ok", "lo_ok", "gram_used", "n_chain", "gram_ok"))

        @block.sync
        def _(sp):
            for g in range(NBLK // NG):
                b0, n = g * NG, NG if g < NBLK // NG - 1 else NG - 1
                sp.dma_start(X[:, b0:b0 + n, :],
                             A.x[b0 * P:(b0 + n) * P, :].rearrange("(b p) f -> p b f", p=P)).then_inc(x_in[g], 16)
            sp.wait_ge(tail_clear, 1)
            sp.dma_start(X[0:TAIL, NBLK - 1, :], A.x[(NBLK - 1) * P:NODES, :]).then_inc(tail_in, 16)
            sp.wait_ge(xn_ok, NBLK)
            sp.dma_start(A.xn_dram.rearrange("(b p) f -> p b f", p=P), XN[:, :, :]).then_inc(stored, 16)
            sp.wait_ge(xs_ok, 1)
            sp.dma_start(A.xs_dram.rearrange("(b p) f -> p b f", p=P), X[:, :, :]).then_inc(stored, 16)
            sp.wait_ge(stored, 32)

        @block.scalar
        def _(act):
            act.wait_ge(var_ok, 1)
            nc.scalar.activation(tmp[:, :], tmp[:, :], ACT.Sqrt).then_inc(sd_ok, 1)

            def high(b, k):
                act.wait_ge(xn_ok, b + 1)
                act.wait_ge(gram_used, b + 1)
                nc.scalar.activation(xhi[:, k, 0:D], XN[:, bass.ds(b, 1), :].rearrange("p o f -> p (o f)"),
                                     ACT.Copy).then_inc(hi_ok, 1)
            pairs(NBLK, act, high)
        @block.gpsimd
        def _(pool):
            pool.wait_ge(xn_ok, NBLK)
            nc.gpsimd.tensor_tensor(X[:, :, :], X[:, :, :], XN[:, :, :], ALU.add).then_inc(xs_ok, 1)

        @block.vector
        def _(dve):
            c = Count(chain)
            nc.vector.memset(X[:, NBLK - 1, :], 0.0).then_inc(tail_clear, 1)
            nc.vector.tensor_scalar(xhi[:, :, D:ACOLS], T.ones16[:, 0:4].rearrange("p (a b) -> p a b", a=2),
                                    1.0, None, ALU.mult).then_inc(gram_used, 2)
            for g in range(NBLK // NG):
                dve.wait_ge(x_in[g], 16)
                if g == NBLK // NG - 1:
                    dve.wait_ge(tail_in, 16)
                with dve.Fori(g * NG, g * NG + NG) as b:
                    nc.vector.bn_stats(st[:, bass.ds(b, 1), :].rearrange("p o f -> p (o f)"),
                                       X[:, bass.ds(b, 1), :].rearrange("p o f -> p (o f)")).then_inc(stats, 1)
            dve.wait_ge(stats, NBLK)
            rstd_steps(nc, dve, c, st, mean[:, :], rstd[:, :], tmp[:, :])
            nc.vector.tensor_copy(tmp[:, :], rstd[:, :]).then_inc(var_ok, 1)
            dve.wait_ge(sd_ok, 1)
            c.after(dve, nc.vector.reciprocal(rstd[:, :], tmp[:, :]))
            with dve.Fori(0, NBLK) as b:
                nc.vector.tensor_scalar(XN[:, bass.ds(b, 1), :], X[:, bass.ds(b, 1), :],
                                        mean[:, bass.ds(b, 1)], rstd[:, bass.ds(b, 1)],
                                        ALU.subtract, ALU.mult).then_inc(xn_ok, 1)

            def low(b, k):
                dve.wait_ge(hi_ok, b + 1)
                nc.vector.tensor_tensor(xlo[:, k, :], XN[:, bass.ds(b, 1), :].rearrange("p o f -> p (o f)"),
                                        xhi[:, k, 0:D].bitcast(F32), ALU.subtract).then_inc(lo_ok, 1)
            pairs(NBLK, dve, low)

            dve.wait_ge(mm, 1)
            c.after(dve, nc.vector.tensor_copy(T.gram[:, 0:2, :], pg[:, :, 0:D + 1]))

        @block.tensor
        def _(pe):
            for f in range(2):
                nc.tensor.matmul(pg[:, f, 0:ACOLS], T.zeros16[:, 0:P], T.zeros16[:, 0:ACOLS], start=True, stop=False)

            def gram(b, k):
                pe.wait_ge(lo_ok, b + 1)
                for f in range(2):
                    hi, lo = xhi[:, k, f * P:(f + 1) * P], xlo[:, k, f * P:(f + 1) * P]
                    nc.tensor.matmul(pg[:, f, 0:ACOLS], hi, xhi[:, k, :], start=False, stop=False)
                    nc.tensor.matmul(pg[:, f, 0:ACOLS], lo, xhi[:, k, :], start=False, stop=False)
                    last = nc.tensor.matmul(pg[:, f, 0:D], hi, xlo[:, k, :], start=False, stop=False)
                last.then_inc(gram_used, 1)
            pairs(NBLK, pe, gram)
            for f in range(2):
                last = nc.tensor.matmul(pg[:, f, 0:ACOLS], T.zeros16[:, 0:P], T.zeros16[:, 0:ACOLS], start=False, stop=True)
            last.then_inc(mm, 1)


def part(w, o, q, n=1):
    start, width, first = ((0, 2 * D, 0), (12 * D, D, 0), (16 * D, 2 * D, 4))[o]
    v = w[:, start + (q - first) * width:start + (q - first + n) * width]
    return v.rearrange("p (q c) -> p q c", q=n) if n > 1 else v


def weights(nc, A, T, W, s):
    ctx = ExitStack()
    with ctx:
        def sb(name, shape, dt=F32):
            return ctx.enter_context(nc.sbuf_tensor(name, shape, dt))
        G = T.gram
        mark = sb("mark", [1, 2])
        wv = sb("wv", [P, 3, D])
        wk = sb("wk", [P, 3, D])
        wq = sb("wq", [P, 2, D + 1])
        wfc = sb("wfc", [P, 2, D])
        win = sb("win", [P, 2, 2, D + 1])
        wih = sb("wih", [P, 4, 3 * D])
        whh = sb("whh", [P, 2, 3 * D])
        T1 = sb("T1", [P, 3, D])
        KV = sb("KV", [P, 2, D])
        M1 = sb("M1", [P, 2, D + 1])
        row = sb("row", [1, 3, GCOLS])
        rhi = sb("rhi", [1, 3, GCOLS], F32R)
        rlo = sb("rlo", [1, 3, GCOLS], F32R)
        bfc = sb("bfc", [1, D])
        bhh = sb("bhh", [1, 3 * D])
        WF = sb("WF", [P, WCOLS])
        pw = ctx.enter_context(nc.psum_tensor("pw", [P, 4, 512], F32))
        NPIECE = 5
        PIECE = WCOLS // NPIECE
        block = ctx.enter_context(nc.Block())
        w_in, mm, ev, rows_ok, aux_in, split_hi, chain = (
            s(n) for n in ("w_in", "mm", "ev", "rows_ok", "aux_in", "split_hi", "w_chain"))
        NLOAD = 19

        @block.sync
        def _(sp):
            sp.wait_ge(rows_ok, 6)
            for d in range(3):
                sp.dma_start(W.aux[2 * d:2 * d + 1, :].bitcast(F32), rhi[0:1, d, :].bitcast(F32)).then_inc(aux_in, 16)
                sp.dma_start(W.aux[2 * d + 1:2 * d + 2, :].bitcast(F32), rlo[0:1, d, :].bitcast(F32)).then_inc(aux_in, 16)
            sp.wait_ge(aux_in, 96)

        @block.scalar
        def _(act):
            def load(dst, src):
                act.dma_start(dst, src).then_inc(w_in, 16)
            for t, w, b in ((wv, A.wv_t, A.bv), (wk, A.wk_t, A.bk)):
                load(t[:, 0:2, :], w.rearrange("(c p) n -> p c n", p=P))
                load(t[0:1, 2, :], b.rearrange("(o n) -> o n", o=1))
            load(wq[:, :, 0:D], A.wq.rearrange("(c p) n -> p c n", p=P))
            for c in range(2):
                load(wq[:, c, D:D + 1], A.bq[c * P:(c + 1) * P].rearrange("(p o) -> p o", o=1))
            load(wfc[:, :, :], A.wfc_t.rearrange("(c p) n -> p c n", p=P))
            for d, (w, b) in enumerate(((A.w_in, A.b_in), (A.w_out, A.b_out))):
                load(win[:, d, :, 0:D], w.rearrange("(c p) n -> p c n", p=P))
                for c in range(2):
                    load(win[:, d, c, D:D + 1], b[c * P:(c + 1) * P].rearrange("(p o) -> p o", o=1))
            load(wih[:, :, :], A.wih_t.rearrange("(c p) n -> p c n", p=P))
            load(whh[:, :, :], A.whh_t.rearrange("(c p) n -> p c n", p=P))
            load(bfc[:, :], A.bfc.rearrange("(o n) -> o n", o=1))
            load(row[0:1, 0, 0:3 * D], A.b_ih.rearrange("(o n) -> o n", o=1))
            load(bhh[:, :], A.b_hh.rearrange("(o n) -> o n", o=1))
            act.wait_ge(ev, 13)
            for q in range(NPIECE):
                cols = slice(q * PIECE, (q + 1) * PIECE)
                nc.scalar.activation(W.hi[:, cols], WF[:, cols], ACT.Copy).then_inc(split_hi, 1)

        @block.vector
        def _(dve):
            c = Count(chain)
            dve.wait_ge(w_in, 16 * NLOAD)
            c.after(dve, nc.vector.memset(row[0:1, 1:3, :], 0.0))
            c.after(dve, nc.vector.memset(G[0:1, 2, D:D + 1], float(NODES)))
            c.after(dve, nc.vector.memset(KV[:, :, :], 0.0))
            ev_n = [0]

            def evict(after_mm, *copies):
                dve.wait_ge(mm, after_mm)
                for ins in copies:
                    last = ins()
                last.then_inc(ev, 1)
                ev_n[0] += 1
            nc.vector.memset(mark[:, :], 0.0).then_inc(ev, 1)
            evict(1, lambda: nc.vector.tensor_copy(G[0:1, 2, 0:D], pw[0:1, 0, 0:D]))
            evict(2, lambda: nc.vector.tensor_copy(T1[:, 0:2, :], pw[:, 0:2, 0:D]),
                  lambda: nc.vector.tensor_copy(T1[0:1, 2, :], pw[0:1, 2, 0:D]))
            heads = [(h // 4, (h % 4) * DK, h * DK) for h in range(HEADS)]
            evict(3, *[lambda a=a, p=p, q=q: nc.vector.tensor_scalar(
                KV[p:p + DK, a, q:q + DK], pw[p:p + DK, a, q:q + DK], 1.0 / NODES, None, ALU.mult)
                for a, p, q in heads])
            evict(4, lambda: nc.vector.tensor_copy(M1[:, :, :], pw[:, 0:2, 0:D + 1]))
            evict(5, lambda: nc.vector.tensor_copy(part(WF, 2, 4, 2)[:, :, D:2 * D], pw[:, 0:2, 0:D]),
                  lambda: nc.vector.tensor_tensor(row[0:1, 0, 4 * D:5 * D], pw[0:1, 2, 0:D], bfc[0:1, :], ALU.add))
            n = 6
            for d in range(2):
                for j in range(3):
                    evict(n, lambda: nc.vector.tensor_copy(part(WF, j // 2, 2 * d, 2)[:, :, (j % 2) * D:(j % 2 + 1) * D], pw[:, 0:2, 0:D]),
                          lambda: nc.vector.tensor_copy(row[0:1, 1 + d, j * D:(j + 1) * D], pw[0:1, 2, 0:D]))
                    n += 1
            c.after(dve, nc.vector.tensor_copy(part(WF, 0, 4, 2), whh[:, :, 0:2 * D]))
            c.after(dve, nc.vector.tensor_copy(part(WF, 2, 4, 2)[:, :, 0:D], whh[:, :, 2 * D:3 * D]))
            c.after(dve, nc.vector.tensor_tensor(row[0:1, 0, 0:2 * D], row[0:1, 0, 0:2 * D], bhh[0:1, 0:2 * D], ALU.add))
            c.after(dve, nc.vector.tensor_copy(row[0:1, 0, 3 * D:4 * D], bhh[0:1, 2 * D:3 * D]))
            nc.vector.memset(mark[:, :], 0.0).then_inc(ev, 1)
            for d in range(3):
                nc.vector.tensor_copy(rhi[0:1, d, :], row[0:1, d, :]).then_inc(rows_ok, 1)
                dve.wait_ge(rows_ok, 2 * d + 1)
                nc.vector.tensor_tensor(rlo[0:1, d, :], row[0:1, d, :], rhi[0:1, d, :].bitcast(F32),
                                        ALU.subtract).then_inc(rows_ok, 1)
            for q in range(NPIECE):
                dve.wait_ge(split_hi, q + 1)
                cols = slice(q * PIECE, (q + 1) * PIECE)
                nc.vector.tensor_tensor(W.lo[:, cols], WF[:, cols], W.hi[:, cols].bitcast(F32), ALU.subtract)

        @block.tensor
        def _(pe):
            def product(out_parts, lhs, rhs):
                for a, out in enumerate(out_parts):
                    for k, r in enumerate(rhs):
                        last = nc.tensor.matmul(out, lhs[k][a], r, start=k == 0, stop=k == len(rhs) - 1)
                last.then_inc(mm, 1)
            cut = ((0, P), (P, 2 * P), (2 * P, 2 * P + 1))
            three = [pw[:, 0, 0:D], pw[:, 1, 0:D], pw[0:1, 2, 0:D]]
            pe.wait_ge(w_in, 16 * NLOAD)
            pe.wait_ge(ev, 1)
            for f in range(2):
                last = nc.tensor.matmul(pw[0:1, 0, f * P:(f + 1) * P], G[:, f, D:D + 1], T.ident[:, :], start=True, stop=True)
            last.then_inc(mm, 1)
            pe.wait_ge(ev, 2)
            kp = (P, P, 1)
            product(three, [[G[0:kp[c], c, a:b] for a, b in cut] for c in range(3)],
                    [wv[0:kp[c], c, :] for c in range(3)])
            pe.wait_ge(ev, 3)
            product(three[:2], [[wk[0:kp[c], c, a:b] for a, b in cut[:2]] for c in range(3)],
                    [T1[0:kp[c], c, :] for c in range(3)])
            pe.wait_ge(ev, 4)
            product([pw[:, 0, 0:D + 1], pw[:, 1, 0:D + 1]],
                    [[KV[:, c, a:b] for a, b in cut[:2]] for c in range(2)], [wq[:, c, :] for c in range(2)])
            pe.wait_ge(ev, 5)
            product(three, [[M1[:, c, a:b] for a, b in cut] for c in range(2)], [wfc[:, c, :] for c in range(2)])
            n = 6
            for d in range(2):
                for j in range(3):
                    pe.wait_ge(ev, n)
                    product(three, [[win[:, d, c, a:b] for a, b in cut] for c in range(2)],
                            [wih[:, 2 * d + c, j * D:(j + 1) * D] for c in range(2)])
                    n += 1


class Rank:

    def __init__(self, nc, ctx, s, name, parts, cols, bins, tiles):
        def sb(n, shape, dt=F32):
            return ctx.enter_context(nc.sbuf_tensor(f"{name}_{n}", shape, dt))
        self.parts, self.cols, self.bins, self.tiles = parts, cols, bins, tiles
        self.halves = 2 if cols > 512 else 1
        self.key = sb("key", [P, cols], F16)
        self.mask = sb("mask", [P, 2, cols], F16)
        self.colsum = sb("colsum", [P, cols])
        self.zero = sb("zero", [P, cols])
        self.before = sb("before", [P, cols])
        self.slot_i = sb("slot_i", [P, cols], I32)
        self.tile_i = sb("tile_i", [P, cols], I32)
        self.tile16 = sb("tile16", [P, cols], F16)
        self.rest16 = sb("rest16", [P, cols], F16)
        self.pos = sb("pos", [P, cols])
        self.pos_i = sb("pos_i", [P, cols], I32)
        self.low_i = sb("low_i", [P, cols], I32)
        self.addr = sb("addr", [P, cols], I32)
        self.total_i = sb("total_i", [P, 1], I32)
        self.ntiles = sb("ntiles", [P, 1])
        self.ntiles16 = sb("ntiles16", [P, 1], F16)
        self.base = sb("base", [P, 1])
        self.end = sb("end", [P, 1])
        self.past = sb("past", [P, tiles], F16)
        self.masked, self.used, self.counted, self.tiled, self.based, self.split, self.placed, \
            self.merged, self.pasts, self.tabled, self.chain = (
                s(f"{name}_{n}") for n in ("masked", "used", "counted", "tiled", "based", "split",
                                           "placed", "merged", "pasts", "tabled", "chain"))

    def col(self, t):
        return t.rearrange("p (h c) -> p h c", h=self.halves)


def rank_dve(nc, dve, T, R, table):
    c = Count(R.chain)
    n, cols = R.parts, R.cols

    def mask(b, k):
        return nc.vector.tensor_scalar(R.mask[0:n, k, :], R.key[0:n, :], T.ramp32[0:n, bass.ds(b, 1)],
                                       None, ALU.is_equal)
    nc.vector.memset(R.zero[:, :], 0.0).then_inc(R.used, 2)
    nc.vector.memset(R.pos[:, :], 0.0).then_inc(R.merged, 2)
    dve.wait_ge(R.merged, 2)

    def count(b, k):
        dve.wait_ge(R.used, b + 1)
        mask(b, k).then_inc(R.masked, 1)
    pairs(R.bins, dve, count)
    dve.wait_ge(R.counted, 1)
    c.after(dve, nc.vector.tensor_copy(R.col(R.colsum), R.pa[:, 0:R.halves, 0:cols // R.halves]))
    c.after(dve, nc.vector.tensor_tensor_scan(R.before[:, :], R.colsum[:, :], R.zero[:, :], 0.0, ALU.add, ALU.add))
    c.after(dve, nc.vector.tensor_scalar(R.total_i[:, :], R.before[:, cols - 1:cols], float(P - 1), None, ALU.add))
    c.after(dve, nc.vector.tensor_scalar(R.total_i[:, :], R.total_i[:, :], 7, None, ALU.arith_shift_right))
    c.after(dve, nc.vector.tensor_copy(R.ntiles[:, :], R.total_i[:, :]))
    nc.vector.tensor_copy(R.ntiles16[:, :], R.ntiles[:, :]).then_inc(R.tiled, 1)
    c.after(dve, nc.vector.tensor_tensor(R.before[:, :], R.before[:, :], R.colsum[:, :], ALU.subtract))
    dve.wait_ge(R.based, 1)
    c.after(dve, nc.vector.tensor_scalar(R.base[:, :], R.pa[:, 0, 0:1], float(P), None, ALU.mult))
    c.after(dve, nc.vector.tensor_tensor(R.end[:, :], R.pa[:, 0, 0:1], R.ntiles[:, :], ALU.add))
    nc.vector.tensor_scalar(R.past[:, :], T.ramp16[:, 0:R.tiles], R.end[:, 0:1], None, ALU.is_ge).then_inc(R.pasts, 1)
    c.after(dve, nc.vector.tensor_scalar(R.slot_i[:, :], R.before[:, :], R.base[:, 0:1], None, ALU.add))
    c.after(dve, nc.vector.tensor_scalar(R.tile_i[:, :], R.slot_i[:, :], 7, None, ALU.arith_shift_right))
    c.after(dve, nc.vector.tensor_scalar(R.slot_i[:, :], R.slot_i[:, :], P - 1, None, ALU.bitwise_and))
    c.after(dve, nc.vector.tensor_copy(R.tile16[:, :], R.tile_i[:, :]))
    nc.vector.tensor_copy(R.rest16[:, :], R.slot_i[:, :]).then_inc(R.split, 1)
    dve.wait_ge(R.tabled, 1)
    c.after(dve, nc.vector.tensor_scalar(table, R.pt, float(R.bins - 1), float(R.table_base), ALU.min, ALU.add))
    mask(0, 0).then_inc(R.masked, 1)

    def merge(b, k):
        dve.wait_ge(R.merged, b + 2)
        mask(b + 1, 1 - k).then_inc(R.masked, 1)
        T.gate_dve.wait(dve, R.placed, b + 1)
        nc.vector.copy_predicated(R.col(R.pos)[0:n], R.col(R.mask[0:n, k, :]).bitcast(U16),
                                  R.pp[k][0:n, 0:R.halves, 0:cols // R.halves]).then_inc(R.merged, 1)
    pairs(R.bins, dve, merge)
    dve.wait_ge(R.merged, R.bins + 2)
    c.after(dve, nc.vector.tensor_copy(R.pos_i[:, :], R.pos[:, :]))
    c.after(dve, nc.vector.tensor_scalar(R.low_i[:, :], R.pos_i[:, :], P - 1, None, ALU.bitwise_and))
    c.after(dve, nc.vector.tensor_scalar(R.slot_i[:, :], R.pos_i[:, :], 7, None, ALU.arith_shift_right))
    c.after(dve, nc.vector.scalar_tensor_tensor(out=R.addr[:, :], in0=R.low_i[:, :], scalar=float(R.tiles),
                                                in1=R.slot_i[:, :], op0=ALU.mult, op1=ALU.add))


def rank_pe(nc, pe, T, R):
    n, w = R.parts, R.cols // R.halves

    def half(t, h):
        return t[:, h * w:(h + 1) * w]
    for h in range(R.halves):
        nc.tensor.matmul(R.pa[:, h, 0:w], T.zeros16[:, 0:P], T.zeros16[:, 0:w], start=True, stop=False)

    def count(b, k):
        T.gate_pe.wait(pe, R.masked, b + 1)
        for h in range(R.halves):
            last = nc.tensor.matmul(R.pa[:, h, 0:w], T.colsel[0:n, bass.ds(63 - b, P)],
                                    half(R.mask[0:n, k, :], h), start=False, stop=False)
        last.then_inc(R.used, 1)
    pairs(R.bins, pe, count)
    for h in range(R.halves):
        last = nc.tensor.matmul(R.pa[:, h, 0:w], T.zeros16[:, 0:P], T.zeros16[:, 0:w], start=False, stop=True)
    last.then_inc(R.counted, 1)
    pe.wait_ge(R.tiled, 1)
    nc.tensor.matmul(R.pa[:, 0, 0:1], T.upper[:, :], R.ntiles16[:, :], start=True, stop=True).then_inc(R.based, 1)
    pe.wait_ge(R.pasts, 1)
    tw = R.tiles // R.halves
    for h in range(R.halves):
        last = nc.tensor.matmul(R.ptb[0:1, h, 0:tw], T.ones16[0:R.bins, 0:1],
                                R.past[0:R.bins, h * tw:(h + 1) * tw], start=True, stop=True)
    last.then_inc(R.tabled, 1)
    pe.wait_ge(R.split, 1)

    def place(b, k):
        pe.wait_ge(R.masked, R.bins + 1 + b)
        pe.wait_ge(R.merged, b + 1)
        for h in range(R.halves):
            out = R.pp[k][0:n, h, 0:w]
            nc.tensor.matmul(out, T.ident128[:, bass.ds(b, 1)].to_broadcast([P, n]), half(R.tile16, h), start=True, stop=False)
            nc.tensor.matmul(out, T.ident1[:, bass.ds(b, 1)].to_broadcast([P, n]), half(R.rest16, h), start=False, stop=False)
            last = nc.tensor.matmul(out, T.upper[0:n, 0:n], half(R.mask[0:n, k, :], h), start=False, stop=True)
        last.then_inc(R.placed, 1)
    pairs(R.bins, pe, place)


def sort_edges(nc, A, T, s):
    ctx = ExitStack()
    with ctx:
        def sb(name, shape, dt=F32):
            return ctx.enter_context(nc.sbuf_tensor(name, shape, dt))
        ends = [sb(f"ends{d}", [P, EC], I32) for d in range(2)]
        pay = [sb(f"pay{d}", [P, EC], I32) for d in range(2)]
        key_i = sb("key_i", [P, EC], I32)
        fill = sb("fill", [P, ETILES], I32)
        SC = 16
        addr_st = sb("addr_st", [P, 2, SC], I32)
        pay_st = sb("pay_st", [P, 2, SC], I32)
        R = [Rank(nc, ctx, s, f"e{d}", EP, EC, NBLK, ETILES) for d in range(2)]
        pa = ctx.enter_context(nc.psum_tensor("pa", [P, 2, 512], F32))
        pp = [ctx.enter_context(nc.psum_tensor(f"pp{k}", [P, 2, 512], F32)) for k in range(2)]
        ptb = ctx.enter_context(nc.psum_tensor("ptb", [P, 2, 512], F32))
        for d in range(2):
            R[d].pa, R[d].pp, R[d].ptb = pa, pp, ptb
            R[d].pt = ptb[0:1, 0:2, 0:ETILES // 2]
            R[d].table_base = d * NBLK
        block = ctx.enter_context(nc.Block())
        ends_in, filled, fill_ok, key_ok, ranked, chain = (
            s(n) for n in ("ends_in", "filled", "fill_ok", "key_ok", "ranked", "sort_chain"))
        staged, sorted_in, decoded = (s(n) for n in ("staged", "sorted_in", "decoded"))
        scattered = [s(f"scattered{k}") for k in range(2)]

        @block.sync
        def _(sp):
            for d, a in enumerate((A.dst, A.src)):
                sp.dma_start(ends[d][0:EP, :], a.rearrange("(p c) -> p c", p=EP)).then_inc(ends_in, 16)
            sp.wait_ge(fill_ok, 1)
            for d in range(2):
                sp.dma_start(A.perm[d].rearrange("(p t) o -> p (t o)", p=P), fill[:, :]).then_inc(filled, 16)
            for d in range(2):
                for k in range(2):
                    sp.wait_ge(scattered[k], (d + 1) * (EC // SC // 2) * SC * 16)
                sp.dma_start(T.slots[:, d * ETILES:(d + 1) * ETILES],
                             A.perm[d].rearrange("(p t) o -> p (t o)", p=P)).then_inc(sorted_in, 16)
            sp.wait_ge(sorted_in, 32)

        @block.vector
        def _(dve):
            c = Count(chain)
            nc.vector.memset(fill[:, :], NONE_PAYLOAD).then_inc(fill_ok, 1)
            dve.wait_ge(ends_in, 32)
            for d in range(2):
                tgt, oth = ends[d][0:EP, :], ends[1 - d][0:EP, :]
                c.after(dve, nc.vector.tensor_scalar(pay[d][0:EP, :], tgt, P - 1, SHIFT,
                                                     ALU.bitwise_and, ALU.logical_shift_left))
                c.after(dve, nc.vector.tensor_tensor(pay[d][0:EP, :], pay[d][0:EP, :], oth, ALU.bitwise_or))
                c.after(dve, nc.vector.tensor_scalar(key_i[0:EP, :], tgt, 7, None, ALU.arith_shift_right))
                c.after(dve, nc.vector.tensor_copy(R[d].key[0:EP, :], key_i[0:EP, :]))
                rank_dve(nc, dve, T, R[d], T.table[0:1, d * ETILES:(d + 1) * ETILES].rearrange("p (h c) -> p h c", h=2))
                dve.sem_inc(ranked, 1)
            for d in range(2):
                dve.wait_ge(sorted_in, 16 * (d + 1))
            c.after(dve, nc.vector.tensor_scalar(T.other[:, 0:2 * ETILES], T.slots[:, 0:2 * ETILES],
                                                 (1 << SHIFT) - 1, None, ALU.bitwise_and))
            c.after(dve, nc.vector.tensor_scalar(T.slots[:, 0:2 * ETILES], T.slots[:, 0:2 * ETILES],
                                                 SHIFT, None, ALU.arith_shift_right))
            nc.vector.tensor_copy(T.local[:, 0:2 * ETILES], T.slots[:, 0:2 * ETILES]).then_inc(decoded, 1)
            nc.vector.memset(T.other[:, 2 * ETILES:], 0).then_inc(decoded, 1)
            dve.wait_ge(decoded, 2)

        @block.tensor
        def _(pe):
            for d in range(2):
                rank_pe(nc, pe, T, R[d])

        @block.scalar
        def _(act):
            for d in range(2):
                act.wait_ge(ranked, d + 1)
                base = d * (EC // SC // 2)

                def stage(i, k):
                    if d or behind(i, 1):
                        act.wait_ge(scattered[k], (i + base) * (SC * 16))
                    nc.scalar.copy(addr_st[0:EP, k, :], R[d].addr[0:EP, bass.ds((i * 2 + k) * SC, SC)])
                    nc.scalar.copy(pay_st[0:EP, k, :], pay[d][0:EP, bass.ds((i * 2 + k) * SC, SC)]).then_inc(staged, 1)
                stage(0, 0)
                stage(0, 1)
                with act.Fori(1, EC // SC // 2) as i:
                    for k in range(2):
                        stage(i, k)

        @block.gpsimd
        def _(pool):
            pool.wait_ge(filled, 32)
            for d in range(2):
                base = d * (EC // SC)
                with pool.Fori(0, EC // SC // 2) as i:
                    for k in range(2):
                        T.gate_pool.wait(pool, staged, i * 2 + (base + k + 1))
                        for q in range(SC):
                            nc.gpsimd.indirect_dma_start(
                                out=A.perm[d][:, :], out_offset=bass.IndirectOffsetOnAxis(ap=addr_st[0:EP, k, q:q + 1], axis=0),
                                in_=pay_st[0:EP, k, q:q + 1], in_offset=None).then_inc(scattered[k], 16)


def aggregate(nc, A, T, acc, s):
    ctx = ExitStack()
    with ctx:
        def sb(name, shape, dt=F32):
            return ctx.enter_context(nc.sbuf_tensor(name, shape, dt))
        rows = sb("rows", [P, RING, GROUP, D])
        idx_st = sb("idx_st", [P, RING, GROUP], I32)
        hi = sb("ghi", [P, 2, GROUP, ACOLS], F32R)
        lo = sb("glo", [P, 2, GROUP, D], F32R)
        hot = sb("hot", [P, 2, GROUP, P], F32R)
        ps = ctx.enter_context(nc.psum_tensor("gps", [P, 2, GROUP, 512], F32))
        block = ctx.enter_context(nc.Block())
        idx_ok, hi_ok, lo_ok, hot_ok, pe_done, added = (
            s(n) for n in ("g_idx", "g_hi", "g_lo", "g_hot", "g_pe", "g_added"))
        cleared = s("g_cleared")
        got = [s(f"g_got{q}") for q in range(RING)]
        ROUNDS = 2 * ETILES // (GROUP * RING)
        ones_v = T.ones16[:, 0:16].rearrange("p (a b c) -> p a b c", a=2, b=4)

        @block.gpsimd
        def _(pool):
            with pool.Fori(0, ROUNDS) as i:
                for q in range(RING):
                    n = i * RING + q
                    T.gate_pool.wait(pool, idx_ok, n + 1)
                    T.gate_pool.wait(pool, lo_ok, n + 1)
                    for g in range(GROUP):
                        nc.gpsimd.indirect_dma_start(
                            out=rows[:, q, g, :], out_offset=None, in_=A.xn_dram[:, :],
                            in_offset=bass.IndirectOffsetOnAxis(ap=idx_st[:, q, g:g + 1], axis=0)).then_inc(got[q], 16)

        @block.scalar
        def _(act):
            nc.scalar.copy(idx_st[:, :, :], T.other[:, 0:RING * GROUP].rearrange("p (a b) -> p a b", a=RING)).then_inc(idx_ok, RING)
            with act.Fori(0, ROUNDS) as i:
                for q in range(RING):
                    n = i * RING + q
                    act.wait_ge(got[q], (i + 1) * (GROUP * 16))
                    nc.scalar.copy(idx_st[:, q, :], T.other[:, bass.ds((n + RING) * GROUP, GROUP)]).then_inc(idx_ok, 1)
                    act.wait_ge(pe_done, n + 1)
                    nc.scalar.activation(hi[:, q % 2, :, 0:D], rows[:, q, :, :], ACT.Copy).then_inc(hi_ok, 1)

        @block.vector
        def _(dve):
            nc.vector.tensor_scalar(hi[:, :, :, D:ACOLS], ones_v, 1.0, None, ALU.mult).then_inc(pe_done, 2)
            nc.vector.memset(acc[:, 0:NBLK * ACOLS], 0.0).then_inc(cleared, 1)
            nc.vector.memset(acc[:, NBLK * ACOLS:], 0.0).then_inc(cleared, 1)
            dve.sem_inc(lo_ok, RING)
            dve.wait_ge(cleared, 2)
            dve.sem_inc(added, 2 * GROUP)

            def prepare(n, q):
                dve.wait_ge(hi_ok, n + 1)
                nc.vector.tensor_tensor(lo[:, q % 2, :, :], rows[:, q, :, :], hi[:, q % 2, :, 0:D].bitcast(F32),
                                        ALU.subtract).then_inc(lo_ok, 1)
                nc.vector.tensor_tensor(
                    hot[:, q % 2, :, :], T.ramp32[:, :].unsqueeze(1).to_broadcast([P, GROUP, P]),
                    T.local[:, bass.ds(n * GROUP, GROUP)].unsqueeze(2).to_broadcast([P, GROUP, P]),
                    ALU.is_equal).then_inc(hot_ok, 1)

            def add(n, q):
                _, blks = nc.values_load_multi_w_load_instructions(
                    T.table[0:1, bass.ds(n * GROUP, GROUP)], engines=(mybir.EngineType.DVE,),
                    min_val=0, max_val=2 * NBLK - 1, skip_runtime_bounds_check_because="the table's values are clamped when it is made")
                dve.wait_ge(pe_done, n + 3)
                for g in range(GROUP):
                    dve.wait_ge(added, n * GROUP + (g + 2 * GROUP))
                    a = acc[:, bass.ds(blks[g] * ACOLS, ACOLS)]
                    nc.vector.tensor_tensor(a, a, ps[:, q % 2, g, 0:ACOLS], ALU.add).then_inc(added, 1)

            for q in range(RING):
                prepare(q, q)
                if q:
                    add(q - 1, q - 1)
            with dve.Fori(1, ROUNDS) as i:
                for q in range(RING):
                    n = i * RING + q
                    prepare(n, q)
                    add(n - 1, (q - 1) % RING)
            add(ROUNDS * RING - 1, RING - 1)

        @block.tensor
        def _(pe):
            with pe.Fori(0, ROUNDS) as i:
                for q in range(RING):
                    n = i * RING + q
                    pe.wait_ge(hot_ok, n + 1)
                    pe.wait_ge(added, (n + 1) * GROUP)
                    for g in range(GROUP):
                        w = hot[:, q % 2, g, :]
                        nc.tensor.matmul(ps[:, q % 2, g, 0:ACOLS], w, hi[:, q % 2, g, :], start=True, stop=False)
                        last = nc.tensor.matmul(ps[:, q % 2, g, 0:D], w, lo[:, q % 2, g, :], start=False, stop=True)
                    last.then_inc(pe_done, 1)


def update(nc, A, T, W, acc, s):
    ctx = ExitStack()
    with ctx:
        def sb(name, shape, dt=F32):
            return ctx.enter_context(nc.sbuf_tensor(name, shape, dt))
        rc = sb("rc", [P, 2 * NBLK])
        aux = sb("auxv", [P, NBLK, 6])
        aux_st = sb("aux_st", [P, 2, 6])
        ag = sb("ag", [P, 2, 2, D])
        xn = sb("uxn", [P, 2, D])
        xs = sb("uxs", [P, 2, D])
        thi = sb("thi", [P, 2, 7, P], F32R)
        tlo = sb("tlo", [P, 2, 6, P], F32R)
        rz = sb("rz", [P, 2, 2 * D])
        nn = sb("nn", [P, 2, D])
        x1 = sb("ux1", [P, 2, D])
        st2 = sb("st2", [P, NBLK, 6])
        pt = ctx.enter_context(nc.psum_tensor("upt", [P, 2, 512], F32))
        po = ctx.enter_context(nc.psum_tensor("upo", [P, 2, 3, 512], F32))
        acc_v = acc[:, :].rearrange("p (d b c) -> p d b c", d=2, b=NBLK)
        block = ctx.enter_context(nc.Block())
        chain, aux_ok, mean_ok, tr_ok, hi_ok, lo_ok, gates, sig_ok, pre_ok, tanh_ok, x1_ok = (
            s(n) for n in ("u_chain", "u_aux", "u_mean", "u_tr", "u_hi", "u_lo", "u_gates", "u_sig",
                           "u_pre", "u_tanh", "u_x1"))
        rows_in = [s(f"u_rows{k}") for k in range(2)]
        x1_out = [s(f"u_out{k}") for k in range(2)]
        dchain, st_ok, stg_ok = s("u_dchain"), s("u_stats"), s("u_staged")

        @block.sync
        def _(sp):
            def load(b, k):
                sp.wait_ge(x1_ok, b + 1)
                for t, src in ((xn, A.xn_dram), (xs, A.xs_dram)):
                    sp.dma_start(t[:, k, :], src[bass.ds(b * P, P), :]).then_inc(rows_in[k], 16)
            pairs(NBLK, sp, load)

        @block.scalar
        def _(act):
            act.wait_ge(aux_ok, 1)

            def means(b, k):
                act.wait_ge(tr_ok, b + 1)
                for d in range(2):
                    last = nc.scalar.activation(ag[:, k, d, :], acc_v[:, d, bass.ds(b, 1), 0:D].rearrange("p o f -> p (o f)"),
                                                ACT.Copy, scale=rc[:, bass.ds(b + d * NBLK, 1)])
                last.then_inc(mean_ok, 1)

            def split(b, k):
                act.wait_ge(tr_ok, b + 3)
                act.wait_ge(gates, b + 1)
                nc.scalar.activation(thi[:, k, 0:4, :].rearrange("p a b -> p (a b)"), pt[:, 0, :], ACT.Copy)
                nc.scalar.activation(thi[:, k, 4:6, :].rearrange("p a b -> p (a b)"), pt[:, 1, 0:2 * P], ACT.Copy)
                nc.scalar.activation(thi[0:6, k, 6, :], pt[0:6, 1, 2 * P:3 * P], ACT.Copy).then_inc(hi_ok, 1)

            def gate(b, k):
                act.wait_ge(gates, b + 3)
                nc.scalar.activation(rz[:, k, :], po[:, k, 0, :], ACT.Sigmoid).then_inc(sig_ok, 1)
                act.wait_ge(pre_ok, b + 1)
                nc.scalar.activation(nn[:, k, :], nn[:, k, :], ACT.Tanh).then_inc(tanh_ok, 1)
                act.wait_ge(x1_ok, b + 3)
                act.dma_start(A.x1_dram[bass.ds(b * P, P), :], x1[:, k, :]).then_inc(x1_out[k], 16)
            means(0, 0)
            split(0, 0)

            def step(b, k):
                means(b + 1, 1 - k)
                split(b + 1, 1 - k)
                gate(b, k)
            with act.Fori(0, NBLK // 2) as j:
                for k in range(2):
                    step(j * 2 + k, k)
            gate(NBLK - 1, 0)
            act.wait_ge(x1_out[0], 16 * (NBLK - NBLK // 2))
            act.wait_ge(x1_out[1], 16 * (NBLK // 2))

        @block.vector
        def _(dve):
            c = Count(chain)
            cnt = acc_v[:, :, :, D]
            rcv = rc[:, :].rearrange("p (d b) -> p d b", d=2)
            c.after(dve, nc.vector.tensor_scalar(rcv, cnt, 1.0, None, ALU.max))
            c.after(dve, nc.vector.memset(aux[:, :, 0:2], 1.0))
            for d in range(2):
                for j in range(2):
                    c.after(dve, nc.vector.tensor_scalar(aux[:, :, 2 + 2 * d + j], acc_v[:, d, :, D], 1.0, None, ALU.min))
            nc.vector.reciprocal(rc[:, :], rc[:, :]).then_inc(aux_ok, 1)
            for sem in (x1_ok, tr_ok, gates):
                dve.sem_inc(sem, 2)

            def low(b, k):
                dve.wait_ge(hi_ok, b + 1)
                nc.vector.tensor_tensor(tlo[:, k, 0:4, :].rearrange("p a b -> p (a b)"), pt[:, 0, :],
                                        thi[:, k, 0:4, :].rearrange("p a b -> p (a b)").bitcast(F32), ALU.subtract)
                nc.vector.tensor_tensor(tlo[:, k, 4:6, :].rearrange("p a b -> p (a b)"), pt[:, 1, 0:2 * P],
                                        thi[:, k, 4:6, :].rearrange("p a b -> p (a b)").bitcast(F32),
                                        ALU.subtract).then_inc(lo_ok, 1)

            def stage(b, k):
                dve.wait_ge(tr_ok, b + 1)
                nc.vector.tensor_copy(aux_st[:, k, :], aux[:, bass.ds(b, 1), :].rearrange("p o f -> p (o f)")).then_inc(stg_ok, 1)

            def gru(b, k):
                n = nn[:, k, :]
                z = rz[:, k, D:2 * D]
                dve.wait_ge(sig_ok, b + 1)
                nc.vector.tensor_tensor(n, rz[:, k, 0:D], po[:, k, 2, 0:D], ALU.mult).then_inc(dchain, 1)
                dve.wait_ge(dchain, b * 4 + 1)
                nc.vector.tensor_tensor(n, n, po[:, k, 1, 0:D], ALU.add).then_inc(pre_ok, 1)
                dve.wait_ge(tanh_ok, b + 1)
                dve.wait_ge(rows_in[k], b_wait(b, k))
                nc.vector.tensor_tensor(n, n, xn[:, k, :], ALU.subtract).then_inc(dchain, 1)
                dve.wait_ge(dchain, b * 4 + 2)
                nc.vector.tensor_tensor(n, n, z, ALU.mult).then_inc(dchain, 1)
                dve.wait_ge(dchain, b * 4 + 3)
                nc.vector.tensor_tensor(n, n, xs[:, k, :], ALU.add).then_inc(dchain, 1)
                dve.wait_ge(dchain, b * 4 + 4)
                xo(b, k)
                y = x1[:, k, :]
                nc.vector.tensor_tensor(y, n, po[:, k, 2, D:2 * D], ALU.add).then_inc(x1_ok, 1)
                dve.wait_ge(x1_ok, b + 3)
                nc.vector.tensor_copy(acc_v[:, 0, bass.ds(b, 1), 0:D].rearrange("p o f -> p (o f)"), y)
                nc.vector.bn_stats(st2[:, bass.ds(b, 1), :].rearrange("p o f -> p (o f)"), y).then_inc(st_ok, 1)

            def b_wait(b, k):
                return (b - k) * 16 + 32

            def xo(b, k):
                if behind(b, 2):
                    dve.wait_ge(x1_out[k], (b - k) * 8)
            stage(0, 0)
            low(0, 0)

            def step(b, k):
                stage(b + 1, 1 - k)
                low(b + 1, 1 - k)
                gru(b, k)
            step(0, 0)
            step(1, 1)
            with dve.Fori(1, NBLK // 2) as j:
                for k in range(2):
                    step(j * 2 + k, k)
            gru(NBLK - 1, 0)
            dve.wait_ge(st_ok, NBLK)
            rstd_steps(nc, dve, c, st2, T.mean2[:, :], T.rstd2[:, :], T.tmp2[:, :])

        @block.tensor
        def _(pe):
            def transposes(b, k):
                pe.wait_ge(mean_ok, b + 1)
                pe.wait_ge(stg_ok, b + 1)
                pe.wait_ge(rows_in[k], (b - k) * 16 + 32)
                pe.wait_ge(lo_ok, b + 1)
                for q in range(6):
                    src = (ag[:, k, q // 2, :] if q < 4 else xn[:, k, :])[:, (q % 2) * P:(q % 2 + 1) * P]
                    nc.tensor.transpose(pt[:, q // 4, (q % 4) * P:(q % 4 + 1) * P], src, T.ident[:, :])
                nc.tensor.matmul(pt[0:6, 1, 2 * P:3 * P], aux_st[:, k, :], T.ident[:, :], start=True, stop=True).then_inc(tr_ok, 1)

            def products(b, k):
                pe.wait_ge(lo_ok, b + 2)
                pe.wait_ge(x1_ok, b + 1)
                for o, c0, c1, p0, p1 in ((0, 0, 2 * D, 0, 6), (1, 2 * D, 3 * D, 0, 4), (2, 3 * D, 5 * D, 4, 6)):
                    out = po[:, k, o, 0:c1 - c0]
                    nc.tensor.matmul(out, thi[0:6, k, 6, :], W.aux[:, c0:c1], start=True, stop=False)
                    for q in range(p0, p1):
                        nc.tensor.matmul(out, thi[:, k, q, :], part(W.hi, o, q), start=False, stop=False)
                        nc.tensor.matmul(out, thi[:, k, q, :], part(W.lo, o, q), start=False, stop=False)
                        last = nc.tensor.matmul(out, tlo[:, k, q, :], part(W.hi, o, q), start=False, stop=q == p1 - 1)
                last.then_inc(gates, 1)
            transposes(0, 0)

            def step(b, k):
                transposes(b + 1, 1 - k)
                products(b, k)
            with pe.Fori(0, NBLK // 2) as j:
                for k in range(2):
                    step(j * 2 + k, k)
            products(NBLK - 1, 0)

        @block.gpsimd
        def _(pool):
            pool.sem_inc(lo_ok, 1)


def route(nc, A, T, acc, s):
    ctx = ExitStack()
    with ctx:
        def sb(name, shape, dt=F32):
            return ctx.enter_context(nc.sbuf_tensor(name, shape, dt))
        x2 = sb("x2", [P, 2, D])
        x2t = sb("x2t", [P, 2, 2, P])
        wg = sb("wg", [P, 2, NEXP])
        bg = sb("bg", [1, NEXP])
        one = sb("one", [1, P])
        score = sb("score", [P, 2, NEXP])
        best = sb("best", [P, 2, 8])
        bidx = sb("bidx", [P, 2, 8], U32)
        pt = ctx.enter_context(nc.psum_tensor("rpt", [P, 2, 512], F32))
        pg = ctx.enter_context(nc.psum_tensor("rpg", [P, 2, 512], F32))
        acc_v = acc[:, :].rearrange("p (d b c) -> p d b c", d=2, b=NBLK)
        block = ctx.enter_context(nc.Block())
        w_in, sd_ok, chain, x2_ok, tr_ok, t_ok, sc_ok, dch = (
            s(n) for n in ("r_w", "r_sd", "r_chain", "r_x2", "r_tr", "r_t", "r_sc", "r_dch"))
        x2_out = [s(f"r_out{k}") for k in range(2)]
        one_ok = s("r_one")

        @block.sync
        def _(sp):
            sp.dma_start(wg[:, :, :], A.wg.rearrange("(c p) n -> p c n", p=P)).then_inc(w_in, 16)
            sp.dma_start(bg[:, :], A.bg.rearrange("(o n) -> o n", o=1)).then_inc(w_in, 16)

            def store(b, k):
                sp.wait_ge(x2_ok, b + 1)
                sp.dma_start(A.x2_dram[bass.ds(b * P, P), :], x2[:, k, :]).then_inc(x2_out[k], 16)
            pairs(NBLK, sp, store)
            sp.wait_ge(x2_out[0], 16 * (NBLK - NBLK // 2))
            sp.wait_ge(x2_out[1], 16 * (NBLK // 2))

        @block.scalar
        def _(act):
            nc.scalar.activation(T.tmp2[:, :], T.rstd2[:, :], ACT.Sqrt).then_inc(sd_ok, 1)

            def out(b, k):
                act.wait_ge(tr_ok, b + 3)
                act.wait_ge(sc_ok, b + 1)
                nc.scalar.copy(x2t[:, k, :, :].rearrange("p a b -> p (a b)"), pt[:, k, 0:2 * P]).then_inc(t_ok, 1)
            pairs(NBLK, act, out)

        @block.vector
        def _(dve):
            c = Count(chain)
            nc.vector.memset(one[:, :], 1.0).then_inc(one_ok, 1)
            dve.sem_inc(tr_ok, 2)
            dve.sem_inc(sc_ok, 2)
            dve.wait_ge(sd_ok, 1)
            c.after(dve, nc.vector.reciprocal(T.rstd2[:, :], T.tmp2[:, :]))

            def norm(b, k):
                if behind(b, 2):
                    dve.wait_ge(x2_out[k], (b - k) * 8)
                dve.wait_ge(tr_ok, b + 1)
                nc.vector.tensor_scalar(x2[:, k, :], acc_v[:, 0, bass.ds(b, 1), 0:D].rearrange("p o f -> p (o f)"),
                                        T.mean2[:, bass.ds(b, 1)], T.rstd2[:, bass.ds(b, 1)],
                                        ALU.subtract, ALU.mult).then_inc(x2_ok, 1)

            def pick(b, k):
                dve.wait_ge(sc_ok, b + 3)
                nc.vector.tensor_copy(score[:, k, :], pg[:, k, 0:NEXP]).then_inc(dch, 1)
                T.gate_dve.wait(dve, dch, b * 3 + 1)
                nc.vector.max(best[:, k, :], score[:, k, :]).then_inc(dch, 1)
                T.gate_dve.wait(dve, dch, b * 3 + 2)
                nc.vector.max_index(bidx[:, k, :], best[:, k, :], score[:, k, :]).then_inc(dch, 1)
                dve.wait_ge(dch, b * 3 + 3)
                nc.vector.tensor_copy(T.expert[:, :].rearrange("p (j b) -> p j b", j=2)[:, :, bass.ds(b, 1)],
                                      bidx[:, k, 0:2].unsqueeze(2))
            norm(0, 0)

            def step(b, k):
                norm(b + 1, 1 - k)
                pick(b, k)
            step(0, 0)
            step(1, 1)
            with dve.Fori(1, NBLK // 2) as j:
                for k in range(2):
                    step(j * 2 + k, k)
            pick(NBLK - 1, 0)

        @block.tensor
        def _(pe):
            pe.wait_ge(w_in, 32)
            pe.wait_ge(one_ok, 1)

            def gate(b, k):
                pe.wait_ge(x2_ok, b + 1)
                for q in range(2):
                    last = nc.tensor.transpose(pt[:, k, q * P:(q + 1) * P], x2[:, k, q * P:(q + 1) * P], T.ident[:, :])
                last.then_inc(tr_ok, 1)
                pe.wait_ge(t_ok, b + 1)
                nc.tensor.matmul(pg[:, k, 0:NEXP], one[:, :], bg[:, :], start=True, stop=False)
                for q in range(2):
                    last = nc.tensor.matmul(pg[:, k, 0:NEXP], x2t[:, k, q, :], wg[:, q, :], start=False, stop=q == 1)
                last.then_inc(sc_ok, 1)
            pairs(NBLK, pe, gate)


def sort_tokens(nc, A, T, s):
    ctx = ExitStack()
    with ctx:
        def sb(name, shape, dt=F32):
            return ctx.enter_context(nc.sbuf_tensor(name, shape, dt))
        token = sb("token", [P, 2 * NBLK], I32)
        fill = sb("xfill", [P, XTILES], I32)
        R = Rank(nc, ctx, s, "x", P, 2 * NBLK, NEXP, XTILES)
        R.pa = ctx.enter_context(nc.psum_tensor("xpa", [P, 1, 512], F32))
        R.pp = [ctx.enter_context(nc.psum_tensor(f"xpp{k}", [P, 1, 512], F32)) for k in range(2)]
        R.ptb = ctx.enter_context(nc.psum_tensor("xptb", [P, 1, 512], F32))
        R.pt = R.ptb[0:1, 0, 0:XTILES]
        R.table_base = 0
        SC = 14
        addr_st = sb("xaddr_st", [P, SC], I32)
        tok_st = sb("xtok_st", [P, SC], I32)
        block = ctx.enter_context(nc.Block())
        tok_ok, filled, fill_ok, ranked, staged, scattered, sorted_in, chain = (
            s(n) for n in ("x_tok", "x_filled", "x_fill", "x_ranked", "x_staged", "x_scat", "x_sorted", "x_ch"))

        @block.sync
        def _(sp):
            sp.wait_ge(fill_ok, 1)
            sp.dma_start(A.perm_x.rearrange("(p t) o -> p (t o)", p=P), fill[:, :]).then_inc(filled, 16)
            sp.wait_ge(scattered, 2 * NBLK * 16)
            sp.dma_start(T.tokens[:, 0:XTILES], A.perm_x.rearrange("(p t) o -> p (t o)", p=P)).then_inc(sorted_in, 16)
            sp.wait_ge(sorted_in, 16)

        @block.vector
        def _(dve):
            c = Count(chain)
            nc.vector.memset(fill[:, :], 0).then_inc(fill_ok, 1)
            nc.vector.memset(T.tokens[:, XTILES:], 0)
            c.after(dve, nc.vector.tensor_copy(R.key[:, :], T.expert[:, :]))
            rank_dve(nc, dve, T, R, T.xtable[0:1, 0:XTILES])
            nc.vector.tensor_copy(T.slot_of[:, :], R.pos_i[:, :]).then_inc(ranked, 1)

        @block.tensor
        def _(pe):
            rank_pe(nc, pe, T, R)

        @block.scalar
        def _(act):
            act.wait_ge(ranked, 1)
            act.wait_ge(tok_ok, 1)

            def stage(i):
                if behind(i, 1):
                    act.wait_ge(scattered, i * (SC * 16))
                nc.scalar.copy(addr_st[:, :], R.addr[:, bass.ds(i * SC, SC)])
                nc.scalar.copy(tok_st[:, :], token[:, bass.ds(i * SC, SC)]).then_inc(staged, 1)
            stage(0)
            with act.Fori(1, 2 * NBLK // SC) as i:
                stage(i)

        @block.gpsimd
        def _(pool):
            nc.gpsimd.iota(token[:, :], pattern=[[0, 2], [P, NBLK]], base=0, channel_multiplier=1).then_inc(tok_ok, 1)
            pool.wait_ge(filled, 16)
            with pool.Fori(0, 2 * NBLK // SC) as i:
                T.gate_pool.wait(pool, staged, i + 1)
                for q in range(SC):
                    nc.gpsimd.indirect_dma_start(
                        out=A.perm_x[:, :], out_offset=bass.IndirectOffsetOnAxis(ap=addr_st[:, q:q + 1], axis=0),
                        in_=tok_st[:, q:q + 1], in_offset=None).then_inc(scattered, 16)


def experts(nc, A, T, s):
    ctx = ExitStack()
    with ctx:
        def sb(name, shape, dt=F32):
            return ctx.enter_context(nc.sbuf_tensor(name, shape, dt))
        KD, KH = D // P, HID // P
        w1 = [sb(f"w1{n}", [P, NEXP * KD * HID], F32R) for n in "hl"]
        w2 = [sb(f"w2{n}", [P, NEXP * KH * D], F32R) for n in "hl"]
        raw = sb("raw", [P, 2, KD * HID])
        b1 = sb("b1", [2, NEXP * HID], F32R)
        b2 = sb("b2", [2, NEXP * D], F32R)
        NB1 = NEXP * (HID + D)
        braw = sb("braw", [1, HID + D])
        bhi = sb("bhi", [1, HID + D], F32R)
        blo = sb("blo", [1, HID + D], F32R)
        twos = sb("twos", [2, P], F32R)
        rows = sb("xrows", [P, RING, D])
        idx_st = sb("xidx", [P, RING], I32)
        xt = [sb(f"xt{n}", [P, 2, KD * P], F32R) for n in "hl"]
        act_h = sb("act_h", [P, 2, HID])
        ht = [sb(f"ht{n}", [P, 2, HID], F32R) for n in "hl"]
        y = sb("y", [P, 2, D])
        px = ctx.enter_context(nc.psum_tensor("epx", [P, 2, 512], F32))
        ph = ctx.enter_context(nc.psum_tensor("eph", [P, 2, 512], F32))
        pg = ctx.enter_context(nc.psum_tensor("epg", [P, 2, 512], F32))
        py = ctx.enter_context(nc.psum_tensor("epy", [P, 2, 512], F32))
        block = ctx.enter_context(nc.Block())
        raw_in = [s(f"e_raw{k}") for k in range(2)]
        whi, wlo, b_in, b_hi, b_lo, b_out, w_ok, y_ok = (
            s(f"e_{n}") for n in ("whi", "wlo", "bin", "bhi", "blo", "bout", "wok", "yok"))
        idx_ok, tx, xhi, xlo, h_ok, g_ok, tg, hhi, hlo, y_mm = (
            s(f"e_{n}") for n in ("idx", "tx", "xhi", "xlo", "h", "g", "tg", "hhi", "hlo", "ymm"))
        got = [s(f"e_got{q}") for q in range(RING)]
        y_out = [s(f"e_yout{k}") for k in range(2)]
        NWT = 2 * NEXP
        ROUNDS = XTILES // RING

        def skewed(eng, *stages):
            lag = max(n for _, n in stages)
            for t in range(RING):
                for f, n in stages:
                    if t >= n:
                        f(t - n, (t - n) % RING)
            with eng.Fori(1, ROUNDS) as i:
                for q in range(RING):
                    for f, n in stages:
                        f(i * RING + (q - n), (q - n) % RING)
            for t in range(XTILES, XTILES + lag):
                for f, n in stages:
                    if t - n < XTILES:
                        f(t - n, (t - n) % RING)

        @block.sync
        def _(sp):
            for n in range(NWT):
                e, second = divmod(n, 2)
                if n >= 2:
                    sp.wait_ge(wlo, n - 1)
                src = (A.w2 if second else A.w1)[e, :, :].rearrange("(c p) n -> p c n", p=P)
                sp.dma_start(raw[:, n % 2, :].rearrange("p (c n) -> p c n", c=KH if second else KD), src).then_inc(raw_in[n % 2], 16)
            for e in range(NEXP):
                if e:
                    sp.wait_ge(b_lo, e)
                sp.dma_start(braw[0:1, 0:HID], A.b1[e:e + 1, :]).then_inc(b_in, 16)
                sp.dma_start(braw[0:1, HID:], A.b2[e:e + 1, :]).then_inc(b_in, 16)
                sp.wait_ge(b_lo, e + 1)
                for r, t in enumerate((bhi, blo)):
                    sp.dma_start(b1[r:r + 1, e * HID:(e + 1) * HID].bitcast(F32), t[0:1, 0:HID].bitcast(F32)).then_inc(b_out, 16)
                    sp.dma_start(b2[r:r + 1, e * D:(e + 1) * D].bitcast(F32), t[0:1, HID:].bitcast(F32)).then_inc(b_out, 16)
                sp.wait_ge(b_out, 64 * (e + 1))

            def store(t, k):
                sp.wait_ge(y_ok, t + 3)
                sp.dma_start(A.y_dram[bass.ds(t * P, P), :], y[:, k, :]).then_inc(y_out[k], 16)
            pairs(XTILES, sp, store)
            for k in range(2):
                sp.wait_ge(y_out[k], 16 * (XTILES // 2))

        @block.gpsimd
        def _(pool):
            with pool.Fori(0, ROUNDS) as i:
                for q in range(RING):
                    t = i * RING + q
                    T.gate_pool.wait(pool, idx_ok, t + 1)
                    T.gate_pool.wait(pool, tx, t + 1)
                    nc.gpsimd.indirect_dma_start(
                        out=rows[:, q, :], out_offset=None, in_=A.x2_dram[:, :],
                        in_offset=bass.IndirectOffsetOnAxis(ap=idx_st[:, q:q + 1], axis=0)).then_inc(got[q], 16)

        @block.scalar
        def _(act):
            nc.scalar.copy(idx_st[:, :], T.tokens[:, 0:RING]).then_inc(idx_ok, RING)
            for n in range(NWT):
                e, second = divmod(n, 2)
                act.wait_ge(raw_in[n % 2], 16 * (n // 2 + 1))
                nc.scalar.activation((w2 if second else w1)[0][:, e * KD * HID:(e + 1) * KD * HID],
                                     raw[:, n % 2, :], ACT.Copy).then_inc(whi, 1)

            def split_x(t, q):
                act.wait_ge(tx, t + (RING + 1))
                act.wait_ge(h_ok, t + 1)
                nc.scalar.activation(xt[0][:, q % 2, :], px[:, q % 2, 0:KD * P], ACT.Copy).then_inc(xhi, 1)
                nc.scalar.copy(idx_st[:, q:q + 1], T.tokens[:, bass.ds(t + RING, 1)]).then_inc(idx_ok, 1)

            def gelu(t, q):
                act.wait_ge(h_ok, t + 3)
                act.wait_ge(tg, t + 1)
                nc.scalar.activation(act_h[:, q % 2, :], ph[:, q % 2, :], ACT.Gelu).then_inc(g_ok, 1)

            def split_h(t, q):
                act.wait_ge(tg, t + 3)
                act.wait_ge(y_mm, t + 1)
                nc.scalar.activation(ht[0][:, q % 2, :], pg[:, q % 2, :], ACT.Copy).then_inc(hhi, 1)
            skewed(act, (split_x, 0), (gelu, 0), (split_h, 1))

        @block.vector
        def _(dve):
            nc.vector.tensor_scalar(twos[:, :], T.ident[0:2, :], 0.0, 1.0, ALU.mult, ALU.add).then_inc(w_ok, 1)
            dve.sem_inc(tx, RING)
            for sem in (h_ok, tg, y_mm, xlo, g_ok, hlo, y_ok):
                dve.sem_inc(sem, 2)
            for n in range(NWT):
                e, second = divmod(n, 2)
                w = w2 if second else w1
                cols = slice(e * KD * HID, (e + 1) * KD * HID)
                dve.wait_ge(whi, n + 1)
                nc.vector.tensor_tensor(w[1][:, cols], raw[:, n % 2, :], w[0][:, cols].bitcast(F32),
                                        ALU.subtract).then_inc(wlo, 1)
            for e in range(NEXP):
                dve.wait_ge(b_in, 32 * (e + 1))
                if e:
                    dve.wait_ge(b_out, 64 * e)
                nc.vector.tensor_copy(bhi[:, :], braw[:, :]).then_inc(b_hi, 1)
                dve.wait_ge(b_hi, e + 1)
                nc.vector.tensor_tensor(blo[:, :], braw[:, :], bhi[:, :].bitcast(F32), ALU.subtract).then_inc(b_lo, 1)

            def low_x(t, q):
                dve.wait_ge(xhi, t + 1)
                nc.vector.tensor_tensor(xt[1][:, q % 2, :], px[:, q % 2, 0:KD * P],
                                        xt[0][:, q % 2, :].bitcast(F32), ALU.subtract).then_inc(xlo, 1)

            def low_h(t, q):
                dve.wait_ge(hhi, t + 1)
                nc.vector.tensor_tensor(ht[1][:, q % 2, :], pg[:, q % 2, :],
                                        ht[0][:, q % 2, :].bitcast(F32), ALU.subtract).then_inc(hlo, 1)

            def out(t, q):
                dve.wait_ge(y_mm, t + 3)
                if behind(t, 2):
                    dve.wait_ge(y_out[q % 2], (t - q % 2) * 8)
                nc.vector.tensor_copy(y[:, q % 2, :], py[:, q % 2, 0:D]).then_inc(y_ok, 1)
            skewed(dve, (low_x, 0), (low_h, 1), (out, 2))

        @block.tensor
        def _(pe):
            pe.wait_ge(w_ok, 1)
            pe.wait_ge(wlo, NWT)
            pe.wait_ge(b_out, 64 * NEXP)
            expert = {}

            def load_expert(t):
                _, v = nc.values_load_multi_w_load_instructions(
                    T.xtable[0:1, bass.ds(t, 1)], engines=(mybir.EngineType.PE,), min_val=0, max_val=NEXP - 1,
                    skip_runtime_bounds_check_because="the table's values are clamped when it is made")
                return v[0]

            def turn_x(t, q):
                pe.wait_ge(got[q], got_value(t, q))
                pe.wait_ge(xlo, t + 1)
                for c in range(KD):
                    last = nc.tensor.transpose(px[:, q % 2, c * P:(c + 1) * P], rows[:, q, c * P:(c + 1) * P], T.ident[:, :])
                last.then_inc(tx, 1)

            def got_value(t, q):
                return (t - q) * (16 // RING) + 16

            def hidden(t, q):
                e = load_expert(t)
                pe.wait_ge(xlo, t + 3)
                pe.wait_ge(g_ok, t + 1)
                out, k = ph[:, q % 2, :], q % 2
                nc.tensor.matmul(out, twos[:, :], b1[:, bass.ds(e * HID, HID)], start=True, stop=False)
                for c in range(KD):
                    x_h, x_l = (xt[m][:, k, c * P:(c + 1) * P] for m in range(2))
                    w_h, w_l = (w1[m][:, bass.ds(e * (KD * HID) + c * HID, HID)] for m in range(2))
                    nc.tensor.matmul(out, x_h, w_h, start=False, stop=False)
                    nc.tensor.matmul(out, x_h, w_l, start=False, stop=False)
                    last = nc.tensor.matmul(out, x_l, w_h, start=False, stop=c == KD - 1)
                last.then_inc(h_ok, 1)

            def turn_h(t, q):
                pe.wait_ge(g_ok, t + 3)
                pe.wait_ge(hlo, t + 1)
                for c in range(KH):
                    last = nc.tensor.transpose(pg[:, q % 2, c * P:(c + 1) * P], act_h[:, q % 2, c * P:(c + 1) * P], T.ident[:, :])
                last.then_inc(tg, 1)

            def outputs(t, q):
                e = load_expert(t)
                pe.wait_ge(hlo, t + 3)
                pe.wait_ge(y_ok, t + 1)
                out, k = py[:, q % 2, 0:D], q % 2
                nc.tensor.matmul(out, twos[:, :], b2[:, bass.ds(e * D, D)], start=True, stop=False)
                for c in range(KH):
                    h_h, h_l = (ht[m][:, k, c * P:(c + 1) * P] for m in range(2))
                    w_h, w_l = (w2[m][:, bass.ds(e * (KH * D) + c * D, D)] for m in range(2))
                    nc.tensor.matmul(out, h_h, w_h, start=False, stop=False)
                    nc.tensor.matmul(out, h_h, w_l, start=False, stop=False)
                    last = nc.tensor.matmul(out, h_l, w_h, start=False, stop=c == KH - 1)
                last.then_inc(y_mm, 1)
            skewed(pe, (turn_x, 0), (hidden, 0), (turn_h, 1), (outputs, 2))


def combine(nc, A, T, s):
    ctx = ExitStack()
    with ctx:
        def sb(name, shape, dt=F32):
            return ctx.enter_context(nc.sbuf_tensor(name, shape, dt))
        NG = 7
        idx_st = sb("cidx", [P, 2, NG], I32)
        yy = sb("cy", [P, 2, NG, D])
        x1 = sb("cx1", [P, NG, D])
        block = ctx.enter_context(nc.Block())
        idx_ok, got, x_in, sum_ok, done, out_ok = (
            s(f"c_{n}") for n in ("idx", "got", "xin", "sum", "done", "out"))
        slots = T.slot_of[:, :].rearrange("p (j b) -> p j b", j=2)
        rounds = NBLK // NG

        @block.scalar
        def _(act):
            for i in range(rounds):
                if i:
                    act.wait_ge(got, i * 2 * NG * 16)
                nc.scalar.copy(idx_st[:, :, :], slots[:, :, i * NG:(i + 1) * NG]).then_inc(idx_ok, 1)

        @block.gpsimd
        def _(pool):
            for i in range(rounds):
                pool.wait_ge(idx_ok, i + 1)
                if i:
                    pool.wait_ge(done, i)
                for j in range(2):
                    for q in range(NG):
                        nc.gpsimd.indirect_dma_start(
                            out=yy[:, j, q, :], out_offset=None, in_=A.y_dram[:, :],
                            in_offset=bass.IndirectOffsetOnAxis(ap=idx_st[:, j, q:q + 1], axis=0)).then_inc(got, 16)

        @block.vector
        def _(dve):
            for i in range(rounds):
                dve.wait_ge(got, (i + 1) * 2 * NG * 16)
                dve.wait_ge(x_in, 16 * (i + 1))
                nc.vector.tensor_tensor(x1[:, :, :], x1[:, :, :], yy[:, 0, :, :], ALU.add).then_inc(sum_ok, 1)
                dve.wait_ge(sum_ok, i + 1)
                nc.vector.tensor_tensor(x1[:, :, :], x1[:, :, :], yy[:, 1, :, :], ALU.add).then_inc(done, 1)

        @block.sync
        def _(sp):
            n_out = 0
            for i in range(rounds):
                if i:
                    sp.wait_ge(out_ok, 16 * n_out)
                r = slice(i * NG * P, (i + 1) * NG * P)
                sp.dma_start(x1[:, :, :], A.x1_dram[r, :].rearrange("(b p) f -> p b f", p=P)).then_inc(x_in, 16)
                sp.wait_ge(done, i + 1)
                full = NG if i < rounds - 1 else NG - 1
                sp.dma_start(A.out[i * NG * P:(i * NG + full) * P, :].rearrange("(b p) f -> p b f", p=P),
                             x1[:, 0:full, :]).then_inc(out_ok, 16)
                n_out += 1
            sp.dma_start(A.out[(NBLK - 1) * P:NODES, :], x1[0:TAIL, NG - 1, :]).then_inc(out_ok, 16)
            sp.wait_ge(out_ok, 16 * (n_out + 1))


class Names:
    pass


def gps_layer(nc, args):
    ctx = ExitStack()
    with ctx:
        A, T, W = Names(), Names(), Names()
        (A.x, A.src, A.dst, A.w_in, A.b_in, A.w_out, A.b_out, A.wih_t, A.b_ih, A.whh_t, A.b_hh) = (
            args[n] for n in "x src dst w_in b_in w_out b_out wih_t b_ih whh_t b_hh".split())
        (A.wq, A.bq, A.wk_t, A.bk, A.wv_t, A.bv, A.wfc_t, A.bfc, A.wg, A.bg, A.w1, A.b1, A.w2, A.b2, A.out) = (
            args[n] for n in "wq bq wk_t bk wv_t bv wfc_t bfc wg bg w1 b1 w2 b2 out".split())

        def sb(name, shape, dt=F32):
            return ctx.enter_context(nc.sbuf_tensor(name, shape, dt))

        def s(name):
            return ctx.enter_context(nc.semaphore(name))
        NP = NBLK * P
        T.gate_dve, T.gate_pe, T.gate_pool = (Gate(s(f"passed_{n}")) for n in ("dve", "pe", "pool"))
        A.xn_dram, A.xs_dram, A.x1_dram, A.x2_dram = (
            nc.dram_tensor(f"{n}_rows", [NP, D], F32).ap() for n in ("xn", "xs", "x1", "x2"))
        A.y_dram = nc.dram_tensor("y_rows", [XTILES * P, D], F32).ap()
        A.perm = [nc.dram_tensor(f"perm{d}", [P * ETILES, 1], I32).ap() for d in range(2)]
        A.perm_x = nc.dram_tensor("perm_x", [P * XTILES, 1], I32).ap()
        T.ident = sb("ident", [P, P])
        T.ident1 = sb("ident1", [P, P], F16)
        T.ident128 = sb("ident128", [P, P], F16)
        T.upper = sb("upper", [P, P], F16)
        T.colsel = sb("colsel", [P, 192], F16)
        T.ones16 = sb("ones16", [P, 16], F16)
        T.zeros16 = sb("zeros16", [P, 512], F16)
        T.expo = sb("expo", [P, 2])
        T.ramp16 = sb("ramp16", [P, ETILES], F16)
        T.ramp32 = sb("ramp32", [P, P])
        T.mean2, T.rstd2, T.tmp2 = (sb(n, [P, NBLK]) for n in ("mean2", "rstd2", "tmp2"))
        T.expert = sb("expert", [P, 2 * NBLK])
        T.slot_of = sb("slot_of", [P, 2 * NBLK], I32)
        T.tokens = sb("tokens", [P, XTILES + RING], I32)
        T.xtable = sb("xtable", [1, XTILES], I32)
        with ExitStack() as blocks:
            def sb2(name, shape, dt=F32):
                return blocks.enter_context(nc.sbuf_tensor(name, shape, dt))
            W.hi = sb2("whi", [P, WCOLS], F32R)
            W.lo = sb2("wlo", [P, WCOLS], F32R)
            W.aux = sb2("waux", [6, GCOLS], F32R)
            with ExitStack() as first:
                T.ramp_i = first.enter_context(nc.sbuf_tensor("ramp_i", [P, ETILES], I32))
                T.gram = first.enter_context(nc.sbuf_tensor("gram", [P, 3, D + 1], F32))
                constants(nc, T, s)
                normalise(nc, A, T, s)
                weights(nc, A, T, W, s)
            with ExitStack() as edges:
                def sb3(name, shape, dt=F32):
                    return edges.enter_context(nc.sbuf_tensor(name, shape, dt))
                T.other = sb3("other", [P, 2 * ETILES + GROUP * RING], I32)
                T.local = sb3("local", [P, 2 * ETILES], F16)
                T.table = sb3("table", [1, 2 * ETILES], I32)
                with ExitStack() as raw:
                    T.slots = raw.enter_context(nc.sbuf_tensor("slots", [P, 2 * ETILES], I32))
                    sort_edges(nc, A, T, s)
                acc = edges.enter_context(nc.sbuf_tensor("acc", [P, 2 * NBLK * ACOLS], F32))
                aggregate(nc, A, T, acc, s)
                update(nc, A, T, W, acc, s)
                route(nc, A, T, acc, s)
        sort_tokens(nc, A, T, s)
        experts(nc, A, T, s)
        combine(nc, A, T, s)


def kernel(**inputs):
    import numpy as _np
    import concourse.bacc as _bacc
    from concourse import mybir as _mybir
    from concourse.bass_utils import run_bass_kernel_spmd as _run

    names = {
        "x": ("x", 0), "src": ("src", 0), "dst": ("dst", 0),
        "w_in": ("L0_gnn_W_in", 0), "b_in": ("L0_gnn_b_in", 0), "w_out": ("L0_gnn_W_out", 0), "b_out": ("L0_gnn_b_out", 0),
        "wih_t": ("L0_gnn_W_ih", 1), "b_ih": ("L0_gnn_b_ih", 0), "whh_t": ("L0_gnn_W_hh", 1), "b_hh": ("L0_gnn_b_hh", 0),
        "wq": ("L0_mix_Wq", 0), "bq": ("L0_mix_bq", 0), "wk_t": ("L0_mix_Wk", 1), "bk": ("L0_mix_bk", 0),
        "wv_t": ("L0_mix_Wv", 1), "bv": ("L0_mix_bv", 0), "wfc_t": ("L0_mix_Wfc", 1), "bfc": ("L0_mix_bfc", 0),
        "wg": ("L0_ffn_Wg", 0), "bg": ("L0_ffn_bg", 0), "w1": ("L0_ffn_W1", 0), "b1": ("L0_ffn_b1", 0),
        "w2": ("L0_ffn_W2", 0), "b2": ("L0_ffn_b2", 0),
    }
    nc = _bacc.Bacc("TRN2", target_bir_lowering=False, num_devices=1)
    arrays, args = {}, {}
    for name, (given, turned) in names.items():
        a = _np.asarray(inputs[given])
        a = _np.ascontiguousarray(a.T if turned else a)
        arrays[f"in_{name}_dram"] = a
        args[name] = nc.dram_tensor(f"in_{name}_dram", a.shape, _mybir.dt.from_np(a.dtype), kind="ExternalInput").ap()
    args["out"] = nc.dram_tensor("out_0_dram", (NODES, D), _mybir.dt.float32, kind="ExternalOutput").ap()
    gps_layer(nc, args)
    r = _run(nc, [arrays], core_ids=[0])
    return r.results[0]["out_0_dram"]
```

```python
import concourse.bass as bass
from concourse import mybir
from contextlib import ExitStack

F32 = mybir.dt.float32
F32R = mybir.dt.float32r
F16 = mybir.dt.float16
I32 = mybir.dt.int32
U32 = mybir.dt.uint32
U16 = mybir.dt.uint16
ALU = mybir.AluOpType
ACT = mybir.ActivationFunctionType
AX = mybir.AxisListType

P = 128
NODES = 6250
D = 256
NBLK = -(-NODES // P)
TAIL = NODES - (NBLK - 1) * P
EDGES = 100000
EP = 125
EC = EDGES // EP
HEADS = 8
DK = D // HEADS
NEXP = 8
HID = 512
EPS = 1e-5

UNIT = 2
RING = 4


def whole(n, m):
    return -(-n // m) * m


CHUNKS = 2
CC = EC // CHUNKS
ETILES = whole((EP * CC + NBLK * (UNIT * P - 1)) // P, UNIT * RING)
ROUNDS = ETILES // (UNIT * RING)
XTILES = whole((2 * NBLK * P + NEXP * (P - 1)) // P, RING)
LOW = 11
ACOLS = D + 2
SPLIT = ACOLS + D
WCOLS = 20 * D
GCOLS = 5 * D


class Count:

    def __init__(self, sem):
        self.sem, self.n = sem, 0

    def after(self, eng, ins):
        self.n += 1
        ins.then_inc(self.sem, 1)
        eng.wait_ge(self.sem, self.n)


def constants(nc, T, s):
    with nc.Block() as block:
        @block.gpsimd
        def _(pool):
            c = Count(s("const_chain"))
            for t, v in ((T.ident, 0.0), (T.ident1, 0.0), (T.ident128, 0.0), (T.upper, 1.0),
                         (T.colsel, 0.0), (T.ones16, 1.0), (T.zeros16, 0.0)):
                c.after(pool, nc.gpsimd.memset(t[:, :], v))
            for t, v in ((T.ident, 1.0), (T.ident1, 1.0), (T.ident128, 128.0)):
                c.after(pool, nc.gpsimd.affine_select(
                    out=t[:, :], in_=t[:, :], pattern=[[-1, P]], compare_op=ALU.not_equal,
                    fill=v, base=0, channel_multiplier=1))
            c.after(pool, nc.gpsimd.affine_select(
                out=T.upper[:, :], in_=T.upper[:, :], pattern=[[1, P]], compare_op=ALU.is_gt,
                fill=0.0, base=0, channel_multiplier=-1))
            c.after(pool, nc.gpsimd.memset(T.colsel[:, 63:64], 1.0))
            c.after(pool, nc.gpsimd.iota(T.ramp_i[:, :], pattern=[[1, ETILES]], base=0,
                                         channel_multiplier=0))
            c.after(pool, nc.gpsimd.tensor_copy(T.ramp16[:, :], T.ramp_i[:, :]))
            c.after(pool, nc.gpsimd.tensor_copy(T.ramp32[:, :], T.ramp_i[:, 0:P]))


def rstd_steps(nc, dve, c, st, mean, rstd, tmp):
    me, ve = st[:, :, 1], st[:, :, 2]
    mo, vo = st[:, :, 4], st[:, :, 5]
    c.after(dve, nc.vector.tensor_tensor(mean, me, mo, ALU.add))
    c.after(dve, nc.vector.tensor_tensor(tmp, me, mo, ALU.subtract))
    c.after(dve, nc.vector.tensor_tensor(rstd, ve, vo, ALU.add))
    c.after(dve, nc.vector.tensor_scalar(mean, mean, 0.5, None, ALU.mult))
    c.after(dve, nc.vector.tensor_tensor(tmp, tmp, tmp, ALU.mult))
    c.after(dve, nc.vector.tensor_scalar(rstd, rstd, 1.0 / D, EPS, ALU.mult, ALU.add))
    c.after(dve, nc.vector.scalar_tensor_tensor(out=rstd, in0=tmp, scalar=0.25, in1=rstd,
                                                op0=ALU.mult, op1=ALU.add))


class Gate:

    def __init__(self, passed):
        self.passed = passed

    def wait(self, eng, sem, value):
        eng.wait_ge(sem, value)
        eng.sem_inc(self.passed, 1)


def behind(b, n):
    return not isinstance(b, int) or b >= n


def pairs(n, eng, body, first=0):
    m = (n - first) // 2
    if m:
        with eng.Fori(0, m) as j:
            for k in range(2):
                body(j * 2 + (first + k), k)
    if (n - first) % 2:
        body(n - 1, 0)


def normalise(nc, A, T, s):
    ctx = ExitStack()
    with ctx:
        def sb(name, shape, dt=F32):
            return ctx.enter_context(nc.sbuf_tensor(name, shape, dt))
        X = sb("X", [P, NBLK, D])
        XN = sb("XN", [P, NBLK, D])
        st = sb("st", [P, NBLK, 6])
        mean, rstd, tmp = sb("mean", [P, NBLK]), sb("rstd", [P, NBLK]), sb("tmp", [P, NBLK])
        both = sb("both", [P, 2, SPLIT], F32R)
        xhi, xlo = both[:, :, 0:ACOLS], both[:, :, ACOLS:]
        pg = ctx.enter_context(nc.psum_tensor("pg", [P, 2, 512], F32))
        block = ctx.enter_context(nc.Block())
        NG = 7
        x_in = [s(f"x_in{g}") for g in range(NBLK // NG)]
        tail_clear, tail_in, stats, var_ok, sd_ok, xn_ok, xs_ok = (
            s(n) for n in ("tail_clear", "tail_in", "stats", "var_ok", "sd_ok", "xn_ok", "xs_ok"))
        both_out = [s(f"both_out{k}") for k in range(2)]
        stored, hi_ok, lo_ok, gram_used, chain, mm = (
            s(n) for n in ("stored", "hi_ok", "lo_ok", "gram_used", "n_chain", "gram_ok"))

        @block.sync
        def _(sp):
            for g in range(NBLK // NG):
                b0, n = g * NG, NG if g < NBLK // NG - 1 else NG - 1
                sp.dma_start(X[:, b0:b0 + n, :],
                             A.x[b0 * P:(b0 + n) * P, :].rearrange("(b p) f -> p b f", p=P)).then_inc(x_in[g], 16)
            sp.wait_ge(tail_clear, 1)
            sp.dma_start(X[0:TAIL, NBLK - 1, :], A.x[(NBLK - 1) * P:NODES, :]).then_inc(tail_in, 16)

            def store(b, k):
                sp.wait_ge(lo_ok, b + 1)
                sp.dma_start(A.split_dram[bass.ds(b * P, P), :], both[:, k, :].bitcast(F32)).then_inc(both_out[k], 16)
            pairs(NBLK, sp, store)
            sp.wait_ge(both_out[0], 16 * (NBLK - NBLK // 2))
            sp.wait_ge(both_out[1], 16 * (NBLK // 2))
            sp.wait_ge(xn_ok, NBLK)
            sp.dma_start(A.xn_dram.rearrange("(b p) f -> p b f", p=P), XN[:, :, :]).then_inc(stored, 16)
            sp.wait_ge(xs_ok, 1)
            sp.dma_start(A.xs_dram.rearrange("(b p) f -> p b f", p=P), X[:, :, :]).then_inc(stored, 16)
            sp.wait_ge(stored, 32)

        @block.scalar
        def _(act):
            act.wait_ge(var_ok, 1)
            nc.scalar.activation(tmp[:, :], tmp[:, :], ACT.Sqrt).then_inc(sd_ok, 1)

            def high(b, k):
                act.wait_ge(xn_ok, b + 1)
                act.wait_ge(gram_used, b + 1)
                if behind(b, 2):
                    act.wait_ge(both_out[k], (b - k) * 8)
                nc.scalar.activation(xhi[:, k, 0:D], XN[:, bass.ds(b, 1), :].rearrange("p o f -> p (o f)"),
                                     ACT.Copy).then_inc(hi_ok, 1)
            high(0, 0)
            high(1, 1)
            pairs(NBLK, act, high, first=2)
        @block.gpsimd
        def _(pool):
            pool.wait_ge(xn_ok, NBLK)
            nc.gpsimd.tensor_tensor(X[:, :, :], X[:, :, :], XN[:, :, :], ALU.add).then_inc(xs_ok, 1)

        @block.vector
        def _(dve):
            c = Count(chain)
            nc.vector.memset(X[:, NBLK - 1, :], 0.0).then_inc(tail_clear, 1)
            nc.vector.tensor_scalar(xhi[:, :, D:ACOLS], T.ones16[:, 0:4].rearrange("p (a b) -> p a b", a=2),
                                    1.0, None, ALU.mult).then_inc(gram_used, 2)
            for g in range(NBLK // NG):
                dve.wait_ge(x_in[g], 16)
                if g == NBLK // NG - 1:
                    dve.wait_ge(tail_in, 16)
                with dve.Fori(g * NG, g * NG + NG) as b:
                    nc.vector.bn_stats(st[:, bass.ds(b, 1), :].rearrange("p o f -> p (o f)"),
                                       X[:, bass.ds(b, 1), :].rearrange("p o f -> p (o f)")).then_inc(stats, 1)
            dve.wait_ge(stats, NBLK)
            rstd_steps(nc, dve, c, st, mean[:, :], rstd[:, :], tmp[:, :])
            nc.vector.tensor_copy(tmp[:, :], rstd[:, :]).then_inc(var_ok, 1)
            dve.wait_ge(sd_ok, 1)
            c.after(dve, nc.vector.reciprocal(rstd[:, :], tmp[:, :]))
            with dve.Fori(0, NBLK) as b:
                nc.vector.tensor_scalar(XN[:, bass.ds(b, 1), :], X[:, bass.ds(b, 1), :],
                                        mean[:, bass.ds(b, 1)], rstd[:, bass.ds(b, 1)],
                                        ALU.subtract, ALU.mult).then_inc(xn_ok, 1)

            def low(b, k):
                dve.wait_ge(hi_ok, b + 1)
                nc.vector.tensor_tensor(xlo[:, k, :], XN[:, bass.ds(b, 1), :].rearrange("p o f -> p (o f)"),
                                        xhi[:, k, 0:D].bitcast(F32), ALU.subtract).then_inc(lo_ok, 1)
            pairs(NBLK, dve, low)

            dve.wait_ge(mm, 1)
            c.after(dve, nc.vector.tensor_copy(T.gram[:, 0:2, :], pg[:, :, 0:D + 1]))

        @block.tensor
        def _(pe):
            for f in range(2):
                nc.tensor.matmul(pg[:, f, 0:ACOLS], T.zeros16[:, 0:P], T.zeros16[:, 0:ACOLS], start=True, stop=False)

            def gram(b, k):
                pe.wait_ge(lo_ok, b + 1)
                for f in range(2):
                    hi, lo = xhi[:, k, f * P:(f + 1) * P], xlo[:, k, f * P:(f + 1) * P]
                    nc.tensor.matmul(pg[:, f, 0:ACOLS], hi, xhi[:, k, :], start=False, stop=False)
                    nc.tensor.matmul(pg[:, f, 0:ACOLS], lo, xhi[:, k, :], start=False, stop=False)
                    last = nc.tensor.matmul(pg[:, f, 0:D], hi, xlo[:, k, :], start=False, stop=False)
                last.then_inc(gram_used, 1)
            pairs(NBLK, pe, gram)
            for f in range(2):
                last = nc.tensor.matmul(pg[:, f, 0:ACOLS], T.zeros16[:, 0:P], T.zeros16[:, 0:ACOLS], start=False, stop=True)
            last.then_inc(mm, 1)


def part(w, o, q, n=1):
    start, width, first = ((0, 2 * D, 0), (12 * D, D, 0), (16 * D, 2 * D, 4))[o]
    v = w[:, start + (q - first) * width:start + (q - first + n) * width]
    return v.rearrange("p (q c) -> p q c", q=n) if n > 1 else v


def weights(nc, A, T, W, s):
    ctx = ExitStack()
    with ctx:
        def sb(name, shape, dt=F32):
            return ctx.enter_context(nc.sbuf_tensor(name, shape, dt))
        G = T.gram
        mark = sb("mark", [1, 2])
        wv = sb("wv", [P, 3, D])
        wk = sb("wk", [P, 3, D])
        wq = sb("wq", [P, 2, D + 1])
        wfc = sb("wfc", [P, 2, D])
        win = sb("win", [P, 2, 2, D + 1])
        wih = sb("wih", [P, 4, 3 * D])
        whh = sb("whh", [P, 2, 3 * D])
        T1 = sb("T1", [P, 3, D])
        KV = sb("KV", [P, 2, D])
        M1 = sb("M1", [P, 2, D + 1])
        row = sb("row", [1, 3, GCOLS])
        rhi = sb("rhi", [1, 3, GCOLS], F32R)
        rlo = sb("rlo", [1, 3, GCOLS], F32R)
        bfc = sb("bfc", [1, D])
        bhh = sb("bhh", [1, 3 * D])
        WF = sb("WF", [P, WCOLS])
        pw = ctx.enter_context(nc.psum_tensor("pw", [P, 4, 512], F32))
        NPIECE = 5
        PIECE = WCOLS // NPIECE
        block = ctx.enter_context(nc.Block())
        w_in, mm, ev, rows_ok, aux_in, split_hi, chain = (
            s(n) for n in ("w_in", "mm", "ev", "rows_ok", "aux_in", "split_hi", "w_chain"))
        NLOAD = 19

        @block.sync
        def _(sp):
            sp.wait_ge(rows_ok, 6)
            for d in range(3):
                sp.dma_start(W.aux[2 * d:2 * d + 1, :].bitcast(F32), rhi[0:1, d, :].bitcast(F32)).then_inc(aux_in, 16)
                sp.dma_start(W.aux[2 * d + 1:2 * d + 2, :].bitcast(F32), rlo[0:1, d, :].bitcast(F32)).then_inc(aux_in, 16)
            sp.wait_ge(aux_in, 96)

        @block.scalar
        def _(act):
            def load(dst, src):
                act.dma_start(dst, src).then_inc(w_in, 16)
            for t, w, b in ((wv, A.wv_t, A.bv), (wk, A.wk_t, A.bk)):
                load(t[:, 0:2, :], w.rearrange("(c p) n -> p c n", p=P))
                load(t[0:1, 2, :], b.rearrange("(o n) -> o n", o=1))
            load(wq[:, :, 0:D], A.wq.rearrange("(c p) n -> p c n", p=P))
            for c in range(2):
                load(wq[:, c, D:D + 1], A.bq[c * P:(c + 1) * P].rearrange("(p o) -> p o", o=1))
            load(wfc[:, :, :], A.wfc_t.rearrange("(c p) n -> p c n", p=P))
            for d, (w, b) in enumerate(((A.w_in, A.b_in), (A.w_out, A.b_out))):
                load(win[:, d, :, 0:D], w.rearrange("(c p) n -> p c n", p=P))
                for c in range(2):
                    load(win[:, d, c, D:D + 1], b[c * P:(c + 1) * P].rearrange("(p o) -> p o", o=1))
            load(wih[:, :, :], A.wih_t.rearrange("(c p) n -> p c n", p=P))
            load(whh[:, :, :], A.whh_t.rearrange("(c p) n -> p c n", p=P))
            load(bfc[:, :], A.bfc.rearrange("(o n) -> o n", o=1))
            load(row[0:1, 0, 0:3 * D], A.b_ih.rearrange("(o n) -> o n", o=1))
            load(bhh[:, :], A.b_hh.rearrange("(o n) -> o n", o=1))
            act.wait_ge(ev, 13)
            for q in range(NPIECE):
                cols = slice(q * PIECE, (q + 1) * PIECE)
                nc.scalar.activation(W.hi[:, cols], WF[:, cols], ACT.Copy).then_inc(split_hi, 1)

        @block.vector
        def _(dve):
            c = Count(chain)
            dve.wait_ge(w_in, 16 * NLOAD)
            c.after(dve, nc.vector.memset(row[0:1, 1:3, :], 0.0))
            c.after(dve, nc.vector.memset(G[0:1, 2, D:D + 1], float(NODES)))
            c.after(dve, nc.vector.memset(KV[:, :, :], 0.0))
            ev_n = [0]

            def evict(after_mm, *copies):
                dve.wait_ge(mm, after_mm)
                for ins in copies:
                    last = ins()
                last.then_inc(ev, 1)
                ev_n[0] += 1
            nc.vector.memset(mark[:, :], 0.0).then_inc(ev, 1)
            evict(1, lambda: nc.vector.tensor_copy(G[0:1, 2, 0:D], pw[0:1, 0, 0:D]))
            evict(2, lambda: nc.vector.tensor_copy(T1[:, 0:2, :], pw[:, 0:2, 0:D]),
                  lambda: nc.vector.tensor_copy(T1[0:1, 2, :], pw[0:1, 2, 0:D]))
            heads = [(h // 4, (h % 4) * DK, h * DK) for h in range(HEADS)]
            evict(3, *[lambda a=a, p=p, q=q: nc.vector.tensor_scalar(
                KV[p:p + DK, a, q:q + DK], pw[p:p + DK, a, q:q + DK], 1.0 / NODES, None, ALU.mult)
                for a, p, q in heads])
            evict(4, lambda: nc.vector.tensor_copy(M1[:, :, :], pw[:, 0:2, 0:D + 1]))
            evict(5, lambda: nc.vector.tensor_copy(part(WF, 2, 4, 2)[:, :, D:2 * D], pw[:, 0:2, 0:D]),
                  lambda: nc.vector.tensor_tensor(row[0:1, 0, 4 * D:5 * D], pw[0:1, 2, 0:D], bfc[0:1, :], ALU.add))
            n = 6
            for d in range(2):
                for j in range(3):
                    evict(n, lambda: nc.vector.tensor_copy(part(WF, j // 2, 2 * d, 2)[:, :, (j % 2) * D:(j % 2 + 1) * D], pw[:, 0:2, 0:D]),
                          lambda: nc.vector.tensor_copy(row[0:1, 1 + d, j * D:(j + 1) * D], pw[0:1, 2, 0:D]))
                    n += 1
            c.after(dve, nc.vector.tensor_copy(part(WF, 0, 4, 2), whh[:, :, 0:2 * D]))
            c.after(dve, nc.vector.tensor_copy(part(WF, 2, 4, 2)[:, :, 0:D], whh[:, :, 2 * D:3 * D]))
            c.after(dve, nc.vector.tensor_tensor(row[0:1, 0, 0:2 * D], row[0:1, 0, 0:2 * D], bhh[0:1, 0:2 * D], ALU.add))
            c.after(dve, nc.vector.tensor_copy(row[0:1, 0, 3 * D:4 * D], bhh[0:1, 2 * D:3 * D]))
            nc.vector.memset(mark[:, :], 0.0).then_inc(ev, 1)
            for d in range(3):
                nc.vector.tensor_copy(rhi[0:1, d, :], row[0:1, d, :]).then_inc(rows_ok, 1)
                dve.wait_ge(rows_ok, 2 * d + 1)
                nc.vector.tensor_tensor(rlo[0:1, d, :], row[0:1, d, :], rhi[0:1, d, :].bitcast(F32),
                                        ALU.subtract).then_inc(rows_ok, 1)
            for q in range(NPIECE):
                dve.wait_ge(split_hi, q + 1)
                cols = slice(q * PIECE, (q + 1) * PIECE)
                nc.vector.tensor_tensor(W.lo[:, cols], WF[:, cols], W.hi[:, cols].bitcast(F32), ALU.subtract)

        @block.tensor
        def _(pe):
            def product(out_parts, lhs, rhs):
                for a, out in enumerate(out_parts):
                    for k, r in enumerate(rhs):
                        last = nc.tensor.matmul(out, lhs[k][a], r, start=k == 0, stop=k == len(rhs) - 1)
                last.then_inc(mm, 1)
            cut = ((0, P), (P, 2 * P), (2 * P, 2 * P + 1))
            three = [pw[:, 0, 0:D], pw[:, 1, 0:D], pw[0:1, 2, 0:D]]
            pe.wait_ge(w_in, 16 * NLOAD)
            pe.wait_ge(ev, 1)
            for f in range(2):
                last = nc.tensor.matmul(pw[0:1, 0, f * P:(f + 1) * P], G[:, f, D:D + 1], T.ident[:, :], start=True, stop=True)
            last.then_inc(mm, 1)
            pe.wait_ge(ev, 2)
            kp = (P, P, 1)
            product(three, [[G[0:kp[c], c, a:b] for a, b in cut] for c in range(3)],
                    [wv[0:kp[c], c, :] for c in range(3)])
            pe.wait_ge(ev, 3)
            product(three[:2], [[wk[0:kp[c], c, a:b] for a, b in cut[:2]] for c in range(3)],
                    [T1[0:kp[c], c, :] for c in range(3)])
            pe.wait_ge(ev, 4)
            product([pw[:, 0, 0:D + 1], pw[:, 1, 0:D + 1]],
                    [[KV[:, c, a:b] for a, b in cut[:2]] for c in range(2)], [wq[:, c, :] for c in range(2)])
            pe.wait_ge(ev, 5)
            product(three, [[M1[:, c, a:b] for a, b in cut] for c in range(2)], [wfc[:, c, :] for c in range(2)])
            n = 6
            for d in range(2):
                for j in range(3):
                    pe.wait_ge(ev, n)
                    product(three, [[win[:, d, c, a:b] for a, b in cut] for c in range(2)],
                            [wih[:, 2 * d + c, j * D:(j + 1) * D] for c in range(2)])
                    n += 1


class Sort:

    def __init__(self, nc, ctx, s, name, parts, cols, bins, tiles, counted, merged, per, groups, ring=2, together=1):
        def sb(n, shape, dt=F32):
            return ctx.enter_context(nc.sbuf_tensor(f"{name}_{n}", shape, dt))
        self.parts, self.cols, self.bins, self.tiles = parts, cols, bins, tiles
        self.n_count, self.n_merge, self.per, self.n_group = counted, merged, per, groups
        self.ring = ring
        self.together = together
        self.key = sb("key", [P, cols], F16)
        self.mask = sb("mask", [P, 2, cols], F16)
        self.colsum = sb("colsum", [P, cols])
        self.before = sb("before", [P, cols])
        self.slot_i = sb("slot_i", [P, cols], I32)
        self.tile_i = sb("tile_i", [P, cols], I32)
        self.tile16 = sb("tile16", [P, cols], F16)
        self.rest16 = sb("rest16", [P, cols], F16)
        self.pos = sb("pos", [P, cols])
        self.parts16 = sb("parts16", [P, cols, 2], F16)
        self.part0, self.part1 = self.parts16[:, :, 0], self.parts16[:, :, 1]
        self.low, self.col = self.colsum, self.before
        self.total_i = sb("total_i", [P, 1], I32)
        self.ntiles = sb("ntiles", [P, 1])
        self.ntiles16 = sb("ntiles16", [P, 1], F16)
        self.base = sb("base", [P, 1])
        self.end = sb("end", [P, 1])
        self.past = sb("past", [P, tiles], F16)
        self.to_slot = sb("to_slot", [P, ring, per, 2, P], F16)
        self.to_tile = sb("to_tile", [P, ring, per, tiles], F16)
        self.pa = ctx.enter_context(nc.psum_tensor(f"{name}_pa", [P, 512], F32))
        self.pt = ctx.enter_context(nc.psum_tensor(f"{name}_pt", [P, 512], F32))
        self.pp = [ctx.enter_context(nc.psum_tensor(f"{name}_pp{k}", [P, 512], F32)) for k in range(2)]
        self.masked, self.used, self.counted, self.tiled, self.based, self.split, self.placed, \
            self.merged, self.pasts, self.tabled, self.chain, self.cleared, self.hots, self.hot_used, self.done = (
                s(f"{name}_{n}") for n in ("masked", "used", "counted", "tiled", "based", "split",
                                           "placed", "merged", "pasts", "tabled", "chain", "cleared",
                                           "hots", "hot_used", "done"))


class SortDVE:

    def __init__(self, nc, dve, T, R):
        self.nc, self.dve, self.T, self.R, self.c = nc, dve, T, R, Count(R.chain)
        nc.vector.memset(R.pos[:, :], 0.0).then_inc(R.cleared, 1)
        dve.wait_ge(R.cleared, 1)
        for sem, ahead in ((R.used, 2), (R.merged, 2), (R.hot_used, R.ring)):
            dve.sem_inc(sem, ahead)

    def mask(self, b, k):
        R = self.R
        n = R.parts
        return self.nc.vector.tensor_scalar(R.mask[0:n, k, :], R.key[0:n, :], self.T.ramp32[0:n, bass.ds(b, 1)],
                                            None, ALU.is_equal).then_inc(R.masked, 1)

    def count(self, ch, b, k):
        R = self.R
        self.dve.wait_ge(R.used, b + (ch * R.n_count + 1))
        self.mask(b, k)

    def bases(self, ch, table, table_base):
        nc, dve, R, T, c = self.nc, self.dve, self.R, self.T, self.c
        dve.wait_ge(R.counted, ch + 1)
        c.after(dve, nc.vector.tensor_copy(R.colsum[:, :], R.pa[:, 0:R.cols]))
        zero = R.slot_i[:, :].bitcast(F32)
        c.after(dve, nc.vector.memset(zero, 0.0))
        c.after(dve, nc.vector.tensor_tensor_scan(R.before[:, :], R.colsum[:, :], zero, 0.0, ALU.add, ALU.add))
        c.after(dve, nc.vector.tensor_scalar(R.total_i[:, :], R.before[:, R.cols - 1:R.cols],
                                              float(R.together * P - 1), None, ALU.add))
        c.after(dve, nc.vector.tensor_scalar(R.total_i[:, :], R.total_i[:, :], 6 + R.together, None,
                                              ALU.arith_shift_right))
        c.after(dve, nc.vector.tensor_scalar(R.ntiles[:, :], R.total_i[:, :], float(R.together), None, ALU.mult))
        nc.vector.tensor_copy(R.ntiles16[:, :], R.ntiles[:, :]).then_inc(R.tiled, 1)
        c.after(dve, nc.vector.tensor_tensor(R.before[:, :], R.before[:, :], R.colsum[:, :], ALU.subtract))
        dve.wait_ge(R.based, ch + 1)
        c.after(dve, nc.vector.tensor_scalar(R.base[:, :], R.pa[:, 0:1], float(P), None, ALU.mult))
        c.after(dve, nc.vector.tensor_tensor(R.end[:, :], R.pa[:, 0:1], R.ntiles[:, :], ALU.add))
        nc.vector.tensor_scalar(R.past[:, :], T.ramp16[:, 0:R.tiles], R.end[:, 0:1], None, ALU.is_ge).then_inc(R.pasts, 1)
        c.after(dve, nc.vector.tensor_scalar(R.slot_i[:, :], R.before[:, :], R.base[:, 0:1], None, ALU.add))
        c.after(dve, nc.vector.tensor_scalar(R.tile_i[:, :], R.slot_i[:, :], 7, None, ALU.arith_shift_right))
        c.after(dve, nc.vector.tensor_scalar(R.slot_i[:, :], R.slot_i[:, :], P - 1, None, ALU.bitwise_and))
        c.after(dve, nc.vector.tensor_copy(R.tile16[:, :], R.tile_i[:, :]))
        nc.vector.tensor_copy(R.rest16[:, :], R.slot_i[:, :]).then_inc(R.split, 1)
        self.mask(0, 0)
        dve.wait_ge(R.tabled, ch + 1)
        c.after(dve, nc.vector.tensor_scalar(table, R.pt[0:1, 0:R.tiles], float(R.bins - 1), float(table_base), ALU.min, ALU.add))

    def merge(self, ch, b, k):
        R = self.R
        n, done = R.parts, ch * R.n_merge
        self.dve.wait_ge(R.merged, b + (done + 2))
        self.mask(b + 1, 1 - k)
        self.T.gate_dve.wait(self.dve, R.placed, b + (done + 1))
        self.nc.vector.copy_predicated(R.pos[0:n, :], R.mask[0:n, k, :].bitcast(U16),
                                       R.pp[k][0:n, 0:R.cols]).then_inc(R.merged, 1)

    def slots(self, ch):
        nc, dve, R, c = self.nc, self.dve, self.R, self.c
        dve.wait_ge(R.merged, (ch + 1) * R.n_merge + 2)
        c.after(dve, nc.vector.tensor_copy(R.slot_i[:, :], R.pos[:, :]))
        c.after(dve, nc.vector.tensor_scalar(R.tile_i[:, :], R.slot_i[:, :], P - 1, None, ALU.bitwise_and))
        c.after(dve, nc.vector.tensor_copy(R.low[:, :], R.tile_i[:, :]))
        c.after(dve, nc.vector.tensor_scalar(R.tile_i[:, :], R.slot_i[:, :], 7, None, ALU.arith_shift_right))
        c.after(dve, nc.vector.tensor_copy(R.col[:, :], R.tile_i[:, :]))

    def spread(self, ch, g, n, k):
        nc, R, T = self.nc, self.R, self.T
        m = R.parts
        self.dve.wait_ge(R.hot_used, g + (ch * R.n_group + 1))
        for j in range(n):
            e = bass.ds(g * n + j, 1)
            nc.vector.scalar_tensor_tensor(
                out=R.to_slot[0:m, k, j, :, :], in0=T.ramp16[0:m, 0:P].unsqueeze(1).to_broadcast([m, 2, P]),
                scalar=R.low[0:m, e],
                in1=R.parts16[0:m, e, :].rearrange("p o q -> p (o q)").unsqueeze(2).to_broadcast([m, 2, P]),
                op0=ALU.is_equal, op1=ALU.mult)
            last = nc.vector.tensor_scalar(R.to_tile[0:m, k, j, :], T.ramp16[0:m, 0:R.tiles], R.col[0:m, e],
                                           None, ALU.is_equal)
        last.then_inc(R.hots, 1)


class SortPE:

    def __init__(self, nc, pe, T, R):
        self.nc, self.pe, self.T, self.R = nc, pe, T, R

    def empty(self, out, start):
        w = out.shape[-1]
        return self.nc.tensor.matmul(out, self.T.zeros16[:, 0:P], self.T.zeros16[:, 0:w], start=start, stop=not start)

    def open_count(self):
        self.empty(self.R.pa[:, 0:self.R.cols], True)

    def count(self, ch, b, k):
        R, n = self.R, self.R.parts
        self.T.gate_pe.wait(self.pe, R.masked, b + (self.masks(ch) + 1))
        self.nc.tensor.matmul(R.pa[:, 0:R.cols], self.T.colsel[0:n, bass.ds(63 - b, P)],
                              R.mask[0:n, k, :], start=False, stop=False).then_inc(R.used, 1)

    def masks(self, ch):
        return ch * (self.R.n_count + 1 + self.R.n_merge)

    def bases(self, ch):
        nc, pe, R, T = self.nc, self.pe, self.R, self.T
        self.empty(R.pa[:, 0:R.cols], False).then_inc(R.counted, 1)
        pe.wait_ge(R.tiled, ch + 1)
        nc.tensor.matmul(R.pa[:, 0:1], T.upper[:, :], R.ntiles16[:, :], start=True, stop=True).then_inc(R.based, 1)
        pe.wait_ge(R.pasts, ch + 1)
        nc.tensor.matmul(R.pt[0:1, 0:R.tiles], T.ones16[0:R.bins, 0:1], R.past[0:R.bins, :],
                         start=True, stop=True).then_inc(R.tabled, 1)
        pe.wait_ge(R.split, ch + 1)

    def merge(self, ch, b, k):
        nc, pe, R, T = self.nc, self.pe, self.R, self.T
        n = R.parts
        pe.wait_ge(R.masked, b + (self.masks(ch) + R.n_count + 1))
        pe.wait_ge(R.merged, b + (ch * R.n_merge + 1))
        out = R.pp[k][0:n, 0:R.cols]
        nc.tensor.matmul(out, T.ident128[:, bass.ds(b, 1)].to_broadcast([P, n]), R.tile16[:, :], start=True, stop=False)
        nc.tensor.matmul(out, T.ident1[:, bass.ds(b, 1)].to_broadcast([P, n]), R.rest16[:, :], start=False, stop=False)
        nc.tensor.matmul(out, T.upper[0:n, 0:n], R.mask[0:n, k, :], start=False, stop=True).then_inc(R.placed, 1)

    def open_spread(self, ch):
        R = self.R
        self.pe.wait_ge(R.merged, (ch + 1) * R.n_merge + 2)
        for q in range(2):
            self.empty(R.pp[q][:, 0:R.tiles], True)

    def spread(self, ch, g, n, k):
        R, m = self.R, self.R.parts
        self.pe.wait_ge(R.hots, g + (ch * R.n_group + 1))
        for j in range(n):
            for q in range(2):
                last = self.nc.tensor.matmul(R.pp[q][:, 0:R.tiles], R.to_slot[0:m, k, j, q, :],
                                             R.to_tile[0:m, k, j, :], start=False, stop=False)
        last.then_inc(R.hot_used, 1)

    def close_spread(self):
        for q in range(2):
            last = self.empty(self.R.pp[q][:, 0:self.R.tiles], False)
        last.then_inc(self.R.done, 1)


BINS_COUNTED = 7
BINS_MERGED = 2
R_RING = 4
COUNT_ROUNDS = -(-NBLK // (BINS_COUNTED * RING))
MERGE_ROUNDS = -(-NBLK // (BINS_MERGED * RING))
SPREAD_ROUNDS = CC // (UNIT * RING)
SORT_ROUNDS = COUNT_ROUNDS + MERGE_ROUNDS + SPREAD_ROUNDS
assert CC == SPREAD_ROUNDS * UNIT * RING and SORT_ROUNDS < ROUNDS


def beside(eng, first, unit, steps, ch):
    def loop(a, n, step):
        start = first + a

        def one_round(i):
            for q in range(RING):
                u = i * RING + (q - start * RING)
                for g in range(UNIT):
                    step(u, q, g)
                    if unit:
                        unit(i * RING + q, q, g)
        peeled = 1 if unit and not a else 0
        if peeled:
            one_round(start)
        with eng.Fori(start + peeled, start + n) as i:
            one_round(i)
        return a + n

    def share(bins, g):
        return range(g * -(-bins // UNIT), min(bins, (g + 1) * -(-bins // UNIT)))

    def count(u, q, g):
        for j in share(BINS_COUNTED, g):
            steps.count(ch, u * BINS_COUNTED + j, (q * BINS_COUNTED + j) % 2)

    def merge(u, q, g):
        for j in share(BINS_MERGED, g):
            steps.merge(ch, u * BINS_MERGED + j, (q * BINS_MERGED + j) % 2)
    steps.begin(ch)
    a = loop(0, COUNT_ROUNDS, count)
    steps.bases(ch)
    a = loop(a, MERGE_ROUNDS, merge)
    steps.slots(ch)
    a = loop(a, SPREAD_ROUNDS, lambda u, q, g: steps.spread(ch, u * UNIT + g, 1, (q * UNIT + g) % R_RING))
    steps.end(ch)
    if unit and a < ROUNDS:
        loop(a, ROUNDS - a, lambda u, q, g: None)


def aggregate(nc, A, T, acc, s):
    ctx = ExitStack()
    with ctx:
        def sb(name, shape, dt=F32):
            return ctx.enter_context(nc.sbuf_tensor(name, shape, dt))
        NCH = 2 * CHUNKS
        UNITS = ROUNDS * RING
        ends = [sb(f"ends{d}", [P, CC], I32) for d in range(2)]
        R = Sort(nc, ctx, s, "e", EP, CC, NBLK, ETILES, BINS_COUNTED * RING * COUNT_ROUNDS,
                 BINS_MERGED * RING * MERGE_ROUNDS, 1, CC, R_RING, UNIT)
        table = sb("table", [1, 2, ETILES], I32)
        other = sb("other", [P, 2, ETILES], I32)
        minus = sb("minus", [P, 2, ETILES])
        rows = sb("rows", [P, RING, UNIT, SPLIT], F32R)
        idx_st = sb("idx_st", [P, RING, UNIT], I32)
        apart = sb("apart", [P, 2, UNIT, P])
        hot = sb("hot", [P, 2, UNIT, P], F32R)
        one = sb("g_one", [P, 1])
        work = sb("work", [P, ETILES], I32)
        ps = ctx.enter_context(nc.psum_tensor("gps", [P, 2, 512], F32))
        block = ctx.enter_context(nc.Block())
        keyed = s("g_keyed")
        ends_in, decoded, idx_ok, apart_ok, hot_ok, pe_done, added, cleared, chain = (
            s(f"g_{n}") for n in ("ends", "decoded", "idx", "apart", "hot", "pe", "added", "cleared", "chain"))
        got = [s(f"g_got{q}") for q in range(RING)]

        @block.sync
        def _(sp):
            for ch in range(NCH):
                if ch:
                    sp.wait_ge(keyed, ch)
                cols = slice((ch % CHUNKS) * CC, (ch % CHUNKS + 1) * CC)
                for t, a in zip(ends, (A.dst, A.src) if ch < CHUNKS else (A.src, A.dst)):
                    sp.dma_start(t[0:EP, :], a.rearrange("(p c) -> p c", p=EP)[:, cols]).then_inc(ends_in, 16)
            sp.wait_ge(ends_in, 32 * NCH)

        @block.gpsimd
        def _(pool):
            with pool.Fori(0, NCH * ROUNDS) as i:
                for q in range(RING):
                    n = i * RING + q
                    T.gate_pool.wait(pool, idx_ok, n + 1)
                    T.gate_pool.wait(pool, pe_done, n + 1)
                    for g in range(UNIT):
                        nc.gpsimd.indirect_dma_start(
                            out=rows[:, q, g, :].bitcast(F32), out_offset=None, in_=A.split_dram[:, :],
                            in_offset=bass.IndirectOffsetOnAxis(ap=idx_st[:, q, g:g + 1], axis=0)).then_inc(got[q], 16)

        @block.scalar
        def _(act):
            act.wait_ge(decoded, 1)
            act.wait_ge(cleared, 3)
            nc.scalar.copy(idx_st[:, :, :], other[:, 0, 0:RING * UNIT].rearrange("p (a b) -> p a b", a=RING)).then_inc(idx_ok, RING)

            def stage(i, q, src):
                act.wait_ge(got[q], i * (UNIT * 16) + UNIT * 16)
                nc.scalar.copy(idx_st[:, q, :], src).then_inc(idx_ok, 1)

            def one_hot(ch, n, q):
                act.wait_ge(pe_done, n + (RING - 1))
                for g in range(UNIT):
                    t = n * UNIT + (g - ch * ETILES)
                    last = nc.scalar.activation(apart[:, q % 2, g, :], T.ramp32[:, :], ACT.Square,
                                                bias=minus[:, ch % 2, bass.ds(t, 1)])
                last.then_inc(apart_ok, 1)
                act.wait_ge(apart_ok, n + 1)
                nc.scalar.activation(hot[:, q % 2, :, :], apart[:, q % 2, :, :], ACT.Relu, bias=one[:, :],
                                     scale=-1.0).then_inc(hot_ok, 1)

            for ch in range(NCH):
                with act.Fori(ch * ROUNDS, (ch + 1) * ROUNDS - 1) as i:
                    for q in range(RING):
                        n = i * RING + q
                        one_hot(ch, n, q)
                        t = (n + RING) * UNIT - ch * ETILES
                        stage(i, q, other[:, ch % 2, bass.ds(t, UNIT)])
                i = (ch + 1) * ROUNDS - 1
                if ch + 1 < NCH:
                    act.wait_ge(decoded, ch + 2)
                for q in range(RING):
                    one_hot(ch, i * RING + q, q)
                    if ch + 1 < NCH:
                        stage(i, q, other[:, 1 - ch % 2, q * UNIT:(q + 1) * UNIT])

        @block.vector
        def _(dve):
            c = Count(chain)
            nc.vector.memset(one[:, :], 1.0).then_inc(cleared, 1)
            half = NBLK * ACOLS
            nc.vector.memset(acc[:, 0:half], 0.0).then_inc(cleared, 1)
            nc.vector.memset(acc[:, half:], 0.0).then_inc(cleared, 1)
            sort = SortDVE(nc, dve, T, R)
            dve.wait_ge(cleared, 3)
            dve.sem_inc(pe_done, RING)
            dve.sem_inc(added, 2)

            class Steps:
                count, merge, slots, spread = sort.count, sort.merge, sort.slots, sort.spread

                @staticmethod
                def begin(ch):
                    dve.wait_ge(ends_in, 32 * (ch + 1))
                    tgt, oth = ends[0][0:EP, :], ends[1][0:EP, :]
                    u, v = R.slot_i[0:EP, :], R.tile_i[0:EP, :]
                    c.after(dve, nc.vector.tensor_scalar(u, tgt, 7, None, ALU.arith_shift_right))
                    c.after(dve, nc.vector.tensor_copy(R.key[0:EP, :], u))
                    c.after(dve, nc.vector.tensor_scalar(u, oth, (1 << LOW) - 1, None, ALU.bitwise_and))
                    c.after(dve, nc.vector.tensor_copy(R.part0[0:EP], u))
                    c.after(dve, nc.vector.tensor_scalar(u, tgt, P - 1, 2, ALU.bitwise_and, ALU.logical_shift_left))
                    c.after(dve, nc.vector.tensor_scalar(v, oth, LOW, None, ALU.arith_shift_right))
                    c.after(dve, nc.vector.tensor_tensor(u, u, v, ALU.bitwise_or))
                    c.after(dve, nc.vector.tensor_scalar(R.part1[0:EP], u, 4.0 * P, None, ALU.add))
                    dve.sem_inc(keyed, 1)

                @staticmethod
                def bases(ch):
                    sort.bases(ch, table[0:1, ch % 2, :], (ch // CHUNKS) * NBLK)

                @staticmethod
                def end(ch):
                    u, v = work[:, :], other[:, ch % 2, :]
                    dve.wait_ge(R.done, ch + 1)
                    if ch >= 2:
                        dve.wait_ge(idx_ok, (ch - 1) * UNITS + RING)
                        dve.wait_ge(hot_ok, (ch - 1) * UNITS)
                    c.after(dve, nc.vector.tensor_copy(u, R.pp[1][:, 0:ETILES]))
                    c.after(dve, nc.vector.tensor_scalar(v, u, 3, None, ALU.bitwise_and))
                    c.after(dve, nc.vector.scalar_tensor_tensor(
                        out=other[:, ch % 2, :], in0=v, scalar=float(1 << LOW), in1=R.pp[0][:, 0:ETILES],
                        op0=ALU.mult, op1=ALU.add))
                    c.after(dve, nc.vector.tensor_scalar(u, u, 2, None, ALU.arith_shift_right))
                    nc.vector.tensor_scalar(minus[:, ch % 2, :], u, -1.0, float(P), ALU.mult, ALU.add).then_inc(decoded, 1)
                    dve.wait_ge(decoded, ch + 1)

            def adder(ch):
                def add(n, q):
                    _, blk = nc.values_load_multi_w_load_instructions(
                        table[0:1, ch % 2, bass.ds(n * UNIT - ch * ETILES, 1)], engines=(mybir.EngineType.DVE,),
                        min_val=0, max_val=2 * NBLK - 1,
                        skip_runtime_bounds_check_because="the table's values are clamped when it is made")
                    dve.wait_ge(pe_done, n + (RING + 1))
                    dve.wait_ge(added, n + 2)
                    a = acc[:, bass.ds(blk[0] * ACOLS, ACOLS)]
                    nc.vector.tensor_tensor(a, a, ps[:, q % 2, 0:ACOLS], ALU.add).then_inc(added, 1)

                def lagged(n, q, g):
                    if not g and behind(n, ch * UNITS + 1):
                        add(n - 1, (q - 1) % RING)
                return lagged, lambda: add((ch + 1) * UNITS - 1, RING - 1)
            beside(dve, 0, None, Steps, 0)
            for ch in range(NCH - 1):
                lagged, last_add = adder(ch)
                beside(dve, ch * ROUNDS, lagged, Steps, ch + 1)
                last_add()
            lagged, last_add = adder(NCH - 1)
            for q in range(RING):
                lagged((NCH - 1) * UNITS + q, q, 0)
            with dve.Fori((NCH - 1) * ROUNDS + 1, NCH * ROUNDS) as i:
                for q in range(RING):
                    lagged(i * RING + q, q, 0)
            last_add()

        @block.tensor
        def _(pe):
            sort = SortPE(nc, pe, T, R)

            class Steps:
                count, merge, bases, spread = sort.count, sort.merge, sort.bases, sort.spread
                slots = sort.open_spread

                @staticmethod
                def begin(ch):
                    sort.open_count()

                @staticmethod
                def end(ch):
                    sort.close_spread()

            def total(n, q, g):
                if g:
                    return
                pe.wait_ge(hot_ok, n + 1)
                pe.wait_ge(got[q], n * (UNIT * 16 // RING) + (RING - q) * (UNIT * 16 // RING))
                pe.wait_ge(added, n + 1)
                for g in range(UNIT):
                    w = hot[:, q % 2, g, :]
                    nc.tensor.matmul(ps[:, q % 2, 0:ACOLS], w, rows[:, q, g, 0:ACOLS], start=g == 0, stop=False)
                    last = nc.tensor.matmul(ps[:, q % 2, 0:D], w, rows[:, q, g, ACOLS:], start=False, stop=g == UNIT - 1)
                last.then_inc(pe_done, 1)
            beside(pe, 0, None, Steps, 0)
            for ch in range(NCH - 1):
                beside(pe, ch * ROUNDS, total, Steps, ch + 1)
            with pe.Fori((NCH - 1) * ROUNDS, NCH * ROUNDS) as i:
                for q in range(RING):
                    total(i * RING + q, q, 0)


def update(nc, A, T, W, acc, s):
    ctx = ExitStack()
    with ctx:
        def sb(name, shape, dt=F32):
            return ctx.enter_context(nc.sbuf_tensor(name, shape, dt))
        rc = sb("rc", [P, 2 * NBLK])
        aux = sb("auxv", [P, NBLK, 6])
        aux_st = sb("aux_st", [P, 2, 6])
        ag = sb("ag", [P, 2, 2, D])
        xn = sb("uxn", [P, 4, D])
        xs = sb("uxs", [P, 4, D])
        thi = sb("thi", [P, 2, 7, P], F32R)
        tlo = sb("tlo", [P, 2, 6, P], F32R)
        rz = sb("rz", [P, 2, 2 * D])
        nn = sb("nn", [P, 2, D])
        x1 = sb("ux1", [P, 2, D])
        st2 = sb("st2", [P, NBLK, 6])
        pt = ctx.enter_context(nc.psum_tensor("upt", [P, 2, 512], F32))
        po = ctx.enter_context(nc.psum_tensor("upo", [P, 2, 3, 512], F32))
        acc_v = acc[:, :].rearrange("p (d b c) -> p d b c", d=2, b=NBLK)
        block = ctx.enter_context(nc.Block())
        chain, mean_ok, tr_ok, hi_ok, lo_ok, gates, sig_ok, pre_ok, tanh_ok, x1_ok = (
            s(n) for n in ("u_chain", "u_mean", "u_tr", "u_hi", "u_lo", "u_gates", "u_sig",
                           "u_pre", "u_tanh", "u_x1"))
        rows_in = [s(f"u_rows{k}") for k in range(4)]
        x1_out = [s(f"u_out{k}") for k in range(2)]
        dchain, st_ok = s("u_dchain"), s("u_stats")

        @block.sync
        def _(sp):
            def load(b, k):
                for t, src in ((xn, A.xn_dram), (xs, A.xs_dram)):
                    sp.dma_start(t[:, k, :], src[bass.ds(b * P, P), :]).then_inc(rows_in[k], 16)

            def store(b, k):
                sp.wait_ge(x1_ok, b + 3)
                sp.dma_start(A.x1_dram[bass.ds(b * P, P), :], x1[:, k % 2, :]).then_inc(x1_out[k % 2], 16)
            for b in range(4):
                load(b, b)
            with sp.Fori(0, (NBLK - 4) // 4) as j:
                for k in range(4):
                    store(j * 4 + k, k)
                    load(j * 4 + (k + 4), k)
            for b in range((NBLK - 4) // 4 * 4, NBLK):
                store(b, b % 4)
                if b + 4 < NBLK:
                    load(b + 4, b % 4)
            sp.wait_ge(x1_out[0], 16 * (NBLK - NBLK // 2))
            sp.wait_ge(x1_out[1], 16 * (NBLK // 2))

        @block.scalar
        def _(act):
            def split(b, k):
                act.wait_ge(tr_ok, b + 3)
                act.wait_ge(gates, b + 1)
                nc.scalar.copy(thi[:, k, 0:4, :].rearrange("p a b -> p (a b)"), pt[:, 0, :])
                nc.scalar.copy(thi[:, k, 4:6, :].rearrange("p a b -> p (a b)"), pt[:, 1, 0:2 * P])
                nc.scalar.copy(thi[0:6, k, 6, :], pt[0:6, 1, 2 * P:3 * P]).then_inc(hi_ok, 1)

            def gate(b, k):
                act.wait_ge(gates, b + 3)
                nc.scalar.activation(rz[:, k, :], po[:, k, 0, :], ACT.Sigmoid).then_inc(sig_ok, 1)
                act.wait_ge(pre_ok, b + 1)
                nc.scalar.activation(nn[:, k, :], nn[:, k, :], ACT.Tanh).then_inc(tanh_ok, 1)
            split(0, 0)
            split(1, 1)

            def step(b, k):
                gate(b, k)
                split(b + 2, k)
            with act.Fori(0, (NBLK - 2) // 2) as j:
                for k in range(2):
                    step(j * 2 + k, k)
            step(NBLK - 3, (NBLK - 3) % 2)
            gate(NBLK - 2, (NBLK - 2) % 2)
            gate(NBLK - 1, (NBLK - 1) % 2)

        @block.vector
        def _(dve):
            c = Count(chain)
            cnt = acc_v[:, :, :, D]
            rcv = rc[:, :].rearrange("p (d b) -> p d b", d=2)
            c.after(dve, nc.vector.tensor_scalar(rcv, cnt, 1.0, None, ALU.max))
            c.after(dve, nc.vector.memset(aux[:, :, 0:2], 1.0))
            for d in range(2):
                for j in range(2):
                    c.after(dve, nc.vector.tensor_scalar(aux[:, :, 2 + 2 * d + j], acc_v[:, d, :, D], 1.0, None, ALU.min))
            c.after(dve, nc.vector.reciprocal(rc[:, :], rc[:, :]))
            for sem in (x1_ok, tr_ok, gates):
                dve.sem_inc(sem, 2)
            dve.sem_inc(lo_ok, 1)

            def means(b, k):
                dve.wait_ge(tr_ok, b + 1)
                for d in range(2):
                    nc.vector.tensor_scalar(ag[:, k, d, :], acc_v[:, d, bass.ds(b, 1), 0:D].rearrange("p o f -> p (o f)"),
                                            rc[:, bass.ds(b + d * NBLK, 1)], None, ALU.mult).then_inc(mean_ok, 1)
                nc.vector.tensor_copy(aux_st[:, k, :], aux[:, bass.ds(b, 1), :].rearrange("p o f -> p (o f)")).then_inc(mean_ok, 1)

            def low(b, k):
                dve.wait_ge(hi_ok, b + 1)
                nc.vector.tensor_tensor(tlo[:, k, 0:4, :].rearrange("p a b -> p (a b)"), pt[:, 0, :],
                                        thi[:, k, 0:4, :].rearrange("p a b -> p (a b)").bitcast(F32), ALU.subtract)
                nc.vector.tensor_tensor(tlo[:, k, 4:6, :].rearrange("p a b -> p (a b)"), pt[:, 1, 0:2 * P],
                                        thi[:, k, 4:6, :].rearrange("p a b -> p (a b)").bitcast(F32),
                                        ALU.subtract).then_inc(lo_ok, 1)

            def before_tanh(b, k):
                n = nn[:, k % 2, :]
                dve.wait_ge(sig_ok, b + 1)
                nc.vector.tensor_tensor(n, rz[:, k % 2, 0:D], po[:, k % 2, 2, 0:D], ALU.mult).then_inc(dchain, 1)
                dve.wait_ge(dchain, b * 4 + 1)
                nc.vector.tensor_tensor(n, n, po[:, k % 2, 1, 0:D], ALU.add).then_inc(pre_ok, 1)

            def after_tanh(b, k):
                n = nn[:, k % 2, :]
                z = rz[:, k % 2, D:2 * D]
                dve.wait_ge(tanh_ok, b + 1)
                dve.wait_ge(rows_in[k], (b - k) * 8 + 32)
                nc.vector.tensor_tensor(n, n, xn[:, k, :], ALU.subtract).then_inc(dchain, 1)
                dve.wait_ge(dchain, b * 4 + 2)
                nc.vector.tensor_tensor(n, n, z, ALU.mult).then_inc(dchain, 1)
                dve.wait_ge(dchain, b * 4 + 3)
                nc.vector.tensor_tensor(n, n, xs[:, k, :], ALU.add).then_inc(dchain, 1)
                dve.wait_ge(dchain, b * 4 + 4)
                if behind(b, 2):
                    dve.wait_ge(x1_out[k % 2], (b - k % 2) * 8)
                y = x1[:, k % 2, :]
                nc.vector.tensor_tensor(y, n, po[:, k % 2, 2, D:2 * D], ALU.add).then_inc(x1_ok, 1)
                T.gate_dve.wait(dve, x1_ok, b + 3)
                nc.vector.tensor_copy(acc_v[:, 0, bass.ds(b, 1), 0:D].rearrange("p o f -> p (o f)"), y)
                nc.vector.bn_stats(st2[:, bass.ds(b, 1), :].rearrange("p o f -> p (o f)"), y).then_inc(st_ok, 1)
            means(0, 0)
            means(1, 1)
            low(0, 0)
            means(2, 0)
            low(1, 1)

            def step(b, k):
                before_tanh(b, k)
                if not isinstance(b, int) or b + 3 < NBLK:
                    means(b + 3, (k + 1) % 2)
                if not isinstance(b, int) or b + 2 < NBLK:
                    low(b + 2, k % 2)
                after_tanh(b, k)
            for b in range(4):
                step(b, b)
            with dve.Fori(1, (NBLK - 3) // 4) as j:
                for k in range(4):
                    step(j * 4 + k, k)
            for b in range((NBLK - 3) // 4 * 4, NBLK):
                step(b, b % 4)
            dve.wait_ge(st_ok, NBLK)
            rstd_steps(nc, dve, c, st2, T.mean2[:, :], T.rstd2[:, :], T.tmp2[:, :])

        @block.tensor
        def _(pe):
            def transposes(b, k):
                pe.wait_ge(mean_ok, b * 3 + 3)
                pe.wait_ge(rows_in[k], (b - k) * 8 + 32)
                pe.wait_ge(lo_ok, b + 1)
                for q in range(6):
                    src = (ag[:, k % 2, q // 2, :] if q < 4 else xn[:, k, :])[:, (q % 2) * P:(q % 2 + 1) * P]
                    nc.tensor.transpose(pt[:, q // 4, (q % 4) * P:(q % 4 + 1) * P], src, T.ident[:, :])
                nc.tensor.matmul(pt[0:6, 1, 2 * P:3 * P], aux_st[:, k % 2, :], T.ident[:, :], start=True, stop=True).then_inc(tr_ok, 1)

            def products(b, k):
                pe.wait_ge(lo_ok, b + 2)
                pe.wait_ge(x1_ok, b + 1)
                for o, c0, c1, p0, p1 in ((0, 0, 2 * D, 0, 6), (1, 2 * D, 3 * D, 0, 4), (2, 3 * D, 5 * D, 4, 6)):
                    out = po[:, k, o, 0:c1 - c0]
                    nc.tensor.matmul(out, thi[0:6, k, 6, :], W.aux[:, c0:c1], start=True, stop=False)
                    for q in range(p0, p1):
                        nc.tensor.matmul(out, thi[:, k, q, :], part(W.hi, o, q), start=False, stop=False)
                        nc.tensor.matmul(out, thi[:, k, q, :], part(W.lo, o, q), start=False, stop=False)
                        last = nc.tensor.matmul(out, tlo[:, k, q, :], part(W.hi, o, q), start=False, stop=q == p1 - 1)
                last.then_inc(gates, 1)
            transposes(0, 0)
            transposes(1, 1)

            def step(b, k):
                products(b, k % 2)
                if not isinstance(b, int) or b + 2 < NBLK:
                    transposes(b + 2, (k + 2) % 4)
            with pe.Fori(0, (NBLK - 2) // 4) as j:
                for k in range(4):
                    step(j * 4 + k, k)
            for b in range((NBLK - 2) // 4 * 4, NBLK):
                step(b, b % 4)


def route(nc, A, T, acc, s):
    ctx = ExitStack()
    with ctx:
        def sb(name, shape, dt=F32):
            return ctx.enter_context(nc.sbuf_tensor(name, shape, dt))
        x2 = sb("x2", [P, 2, D])
        x2t = sb("x2t", [P, 2, 2, P])
        wg = sb("wg", [P, 2, NEXP])
        bg = sb("bg", [1, NEXP])
        one = sb("one", [1, P])
        score = sb("score", [P, 2, NEXP])
        best = sb("best", [P, 2, 8])
        bidx = sb("bidx", [P, 2, 8], U32)
        pt = ctx.enter_context(nc.psum_tensor("rpt", [P, 2, 512], F32))
        pg = ctx.enter_context(nc.psum_tensor("rpg", [P, 2, 512], F32))
        acc_v = acc[:, :].rearrange("p (d b c) -> p d b c", d=2, b=NBLK)
        block = ctx.enter_context(nc.Block())
        w_in, sd_ok, chain, x2_ok, tr_ok, t_ok, sc_ok, dch = (
            s(n) for n in ("r_w", "r_sd", "r_chain", "r_x2", "r_tr", "r_t", "r_sc", "r_dch"))
        x2_out = [s(f"r_out{k}") for k in range(2)]
        one_ok = s("r_one")

        @block.sync
        def _(sp):
            sp.dma_start(wg[:, :, :], A.wg.rearrange("(c p) n -> p c n", p=P)).then_inc(w_in, 16)
            sp.dma_start(bg[:, :], A.bg.rearrange("(o n) -> o n", o=1)).then_inc(w_in, 16)

            def store(b, k):
                sp.wait_ge(x2_ok, b + 1)
                sp.dma_start(A.x2_dram[bass.ds(b * P, P), :], x2[:, k, :]).then_inc(x2_out[k], 16)
            pairs(NBLK, sp, store)
            sp.wait_ge(x2_out[0], 16 * (NBLK - NBLK // 2))
            sp.wait_ge(x2_out[1], 16 * (NBLK // 2))

        @block.scalar
        def _(act):
            nc.scalar.activation(T.tmp2[:, :], T.rstd2[:, :], ACT.Sqrt).then_inc(sd_ok, 1)

            def out(b, k):
                act.wait_ge(tr_ok, b + 3)
                act.wait_ge(sc_ok, b + 1)
                nc.scalar.copy(x2t[:, k, :, :].rearrange("p a b -> p (a b)"), pt[:, k, 0:2 * P]).then_inc(t_ok, 1)
            pairs(NBLK, act, out)

        @block.vector
        def _(dve):
            c = Count(chain)
            nc.vector.memset(one[:, :], 1.0).then_inc(one_ok, 1)
            dve.sem_inc(tr_ok, 2)
            dve.sem_inc(sc_ok, 2)
            dve.wait_ge(sd_ok, 1)
            c.after(dve, nc.vector.reciprocal(T.rstd2[:, :], T.tmp2[:, :]))

            def norm(b, k):
                if behind(b, 2):
                    dve.wait_ge(x2_out[k], (b - k) * 8)
                dve.wait_ge(tr_ok, b + 1)
                nc.vector.tensor_scalar(x2[:, k, :], acc_v[:, 0, bass.ds(b, 1), 0:D].rearrange("p o f -> p (o f)"),
                                        T.mean2[:, bass.ds(b, 1)], T.rstd2[:, bass.ds(b, 1)],
                                        ALU.subtract, ALU.mult).then_inc(x2_ok, 1)

            def pick(b, k):
                dve.wait_ge(sc_ok, b + 3)
                nc.vector.tensor_copy(score[:, k, :], pg[:, k, 0:NEXP]).then_inc(dch, 1)
                T.gate_dve.wait(dve, dch, b * 3 + 1)
                nc.vector.max(best[:, k, :], score[:, k, :]).then_inc(dch, 1)
                T.gate_dve.wait(dve, dch, b * 3 + 2)
                nc.vector.max_index(bidx[:, k, :], best[:, k, :], score[:, k, :]).then_inc(dch, 1)
                dve.wait_ge(dch, b * 3 + 3)
                nc.vector.tensor_copy(T.expert[:, :].rearrange("p (j b) -> p j b", j=2)[:, :, bass.ds(b, 1)],
                                      bidx[:, k, 0:2].unsqueeze(2))
            norm(0, 0)

            def step(b, k):
                norm(b + 1, 1 - k)
                pick(b, k)
            step(0, 0)
            step(1, 1)
            with dve.Fori(1, NBLK // 2) as j:
                for k in range(2):
                    step(j * 2 + k, k)
            pick(NBLK - 1, 0)

        @block.tensor
        def _(pe):
            pe.wait_ge(w_in, 32)
            pe.wait_ge(one_ok, 1)

            def gate(b, k):
                pe.wait_ge(x2_ok, b + 1)
                for q in range(2):
                    last = nc.tensor.transpose(pt[:, k, q * P:(q + 1) * P], x2[:, k, q * P:(q + 1) * P], T.ident[:, :])
                last.then_inc(tr_ok, 1)
                pe.wait_ge(t_ok, b + 1)
                nc.tensor.matmul(pg[:, k, 0:NEXP], one[:, :], bg[:, :], start=True, stop=False)
                for q in range(2):
                    last = nc.tensor.matmul(pg[:, k, 0:NEXP], x2t[:, k, q, :], wg[:, q, :], start=False, stop=q == 1)
                last.then_inc(sc_ok, 1)
            pairs(NBLK, pe, gate)


def sort_tokens(nc, A, T, s):
    ctx = ExitStack()
    with ctx:
        def sb(name, shape, dt=F32):
            return ctx.enter_context(nc.sbuf_tensor(name, shape, dt))
        token = sb("token", [P, 2 * NBLK], I32)
        high = sb("high", [P, 2 * NBLK], I32)
        low_part = sb("low_part", [P, XTILES])
        PERX = 7
        R = Sort(nc, ctx, s, "x", P, 2 * NBLK, NEXP, XTILES, NEXP, NEXP, PERX, 2 * NBLK // PERX)
        block = ctx.enter_context(nc.Block())
        tok_ok, chain = s("x_tok"), s("x_ch")

        @block.gpsimd
        def _(pool):
            nc.gpsimd.iota(token[:, :], pattern=[[0, 2], [P, NBLK]], base=0, channel_multiplier=1).then_inc(tok_ok, 1)

        @block.vector
        def _(dve):
            c = Count(chain)
            sort = SortDVE(nc, dve, T, R)
            nc.vector.memset(T.tokens[:, XTILES:], 0)
            c.after(dve, nc.vector.tensor_copy(R.key[:, :], T.expert[:, :]))
            pairs(NEXP, dve, lambda b, k: sort.count(0, b, k))
            dve.wait_ge(tok_ok, 1)
            c.after(dve, nc.vector.tensor_scalar(high[:, :], token[:, :], LOW, None, ALU.arith_shift_right))
            c.after(dve, nc.vector.tensor_copy(R.part1, high[:, :]))
            c.after(dve, nc.vector.tensor_scalar(token[:, :], token[:, :], (1 << LOW) - 1, None, ALU.bitwise_and))
            c.after(dve, nc.vector.tensor_copy(R.part0, token[:, :]))
            sort.bases(0, T.xtable[0:1, 0:XTILES], 0)
            pairs(NEXP, dve, lambda b, k: sort.merge(0, b, k))
            sort.slots(0)
            c.after(dve, nc.vector.tensor_copy(T.slot_of[:, :], R.slot_i[:, :]))
            pairs(R.n_group, dve, lambda g, k: sort.spread(0, g, PERX, k))
            dve.wait_ge(R.done, 1)
            c.after(dve, nc.vector.tensor_copy(low_part[:, :], R.pp[0][:, 0:XTILES]))
            c.after(dve, nc.vector.scalar_tensor_tensor(out=T.tokens[:, 0:XTILES], in0=R.pp[1][:, 0:XTILES],
                                                        scalar=float(1 << LOW), in1=low_part[:, :],
                                                        op0=ALU.mult, op1=ALU.add))

        @block.tensor
        def _(pe):
            sort = SortPE(nc, pe, T, R)
            sort.open_count()
            pairs(NEXP, pe, lambda b, k: sort.count(0, b, k))
            sort.bases(0)
            pairs(NEXP, pe, lambda b, k: sort.merge(0, b, k))
            sort.open_spread(0)
            pairs(R.n_group, pe, lambda g, k: sort.spread(0, g, PERX, k))
            sort.close_spread()


def experts(nc, A, T, s):
    ctx = ExitStack()
    with ctx:
        def sb(name, shape, dt=F32):
            return ctx.enter_context(nc.sbuf_tensor(name, shape, dt))
        KD, KH = D // P, HID // P
        w1 = [sb(f"w1{n}", [P, NEXP * KD * HID], F32R) for n in "hl"]
        w2 = [sb(f"w2{n}", [P, NEXP * KH * D], F32R) for n in "hl"]
        raw = sb("raw", [P, 2, KD * HID])
        b1 = sb("b1", [2, NEXP * HID], F32R)
        b2 = sb("b2", [2, NEXP * D], F32R)
        NB1 = NEXP * (HID + D)
        braw = sb("braw", [1, HID + D])
        bhi = sb("bhi", [1, HID + D], F32R)
        blo = sb("blo", [1, HID + D], F32R)
        twos = sb("twos", [2, P], F32R)
        rows = sb("xrows", [P, RING, D])
        idx_st = sb("xidx", [P, RING], I32)
        xt = [sb(f"xt{n}", [P, 2, KD * P], F32R) for n in "hl"]
        act_h = sb("act_h", [P, 2, HID])
        ht = [sb(f"ht{n}", [P, 2, HID], F32R) for n in "hl"]
        y = sb("y", [P, 2, D])
        px = ctx.enter_context(nc.psum_tensor("epx", [P, 2, 512], F32))
        ph = ctx.enter_context(nc.psum_tensor("eph", [P, 2, 512], F32))
        pg = ctx.enter_context(nc.psum_tensor("epg", [P, 2, 512], F32))
        py = ctx.enter_context(nc.psum_tensor("epy", [P, 2, 512], F32))
        block = ctx.enter_context(nc.Block())
        raw_in = [s(f"e_raw{k}") for k in range(2)]
        whi, wlo, b_in, b_hi, b_lo, b_out, w_ok, y_ok = (
            s(f"e_{n}") for n in ("whi", "wlo", "bin", "bhi", "blo", "bout", "wok", "yok"))
        idx_ok, tx, xhi, xlo, h_ok, g_ok, tg, hhi, hlo, y_mm = (
            s(f"e_{n}") for n in ("idx", "tx", "xhi", "xlo", "h", "g", "tg", "hhi", "hlo", "ymm"))
        got = [s(f"e_got{q}") for q in range(RING)]
        y_out = [s(f"e_yout{k}") for k in range(2)]
        NWT = 2 * NEXP
        ROUNDS = XTILES // RING

        def skewed(eng, *stages):
            lag = max(n for _, n in stages)
            for t in range(RING):
                for f, n in stages:
                    if t >= n:
                        f(t - n, (t - n) % RING)
            with eng.Fori(1, ROUNDS) as i:
                for q in range(RING):
                    for f, n in stages:
                        f(i * RING + (q - n), (q - n) % RING)
            for t in range(XTILES, XTILES + lag):
                for f, n in stages:
                    if t - n < XTILES:
                        f(t - n, (t - n) % RING)

        @block.sync
        def _(sp):
            for n in range(NWT):
                e, second = divmod(n, 2)
                if n >= 2:
                    sp.wait_ge(wlo, n - 1)
                src = (A.w2 if second else A.w1)[e, :, :].rearrange("(c p) n -> p c n", p=P)
                sp.dma_start(raw[:, n % 2, :].rearrange("p (c n) -> p c n", c=KH if second else KD), src).then_inc(raw_in[n % 2], 16)
            for e in range(NEXP):
                if e:
                    sp.wait_ge(b_lo, e)
                sp.dma_start(braw[0:1, 0:HID], A.b1[e:e + 1, :]).then_inc(b_in, 16)
                sp.dma_start(braw[0:1, HID:], A.b2[e:e + 1, :]).then_inc(b_in, 16)
                sp.wait_ge(b_lo, e + 1)
                for r, t in enumerate((bhi, blo)):
                    sp.dma_start(b1[r:r + 1, e * HID:(e + 1) * HID].bitcast(F32), t[0:1, 0:HID].bitcast(F32)).then_inc(b_out, 16)
                    sp.dma_start(b2[r:r + 1, e * D:(e + 1) * D].bitcast(F32), t[0:1, HID:].bitcast(F32)).then_inc(b_out, 16)
                sp.wait_ge(b_out, 64 * (e + 1))

            def store(t, k):
                sp.wait_ge(y_ok, t + 3)
                sp.dma_start(A.y_dram[bass.ds(t * P, P), :], y[:, k, :]).then_inc(y_out[k], 16)
            pairs(XTILES, sp, store)
            for k in range(2):
                sp.wait_ge(y_out[k], 16 * (XTILES // 2))

        @block.gpsimd
        def _(pool):
            with pool.Fori(0, ROUNDS) as i:
                for q in range(RING):
                    t = i * RING + q
                    T.gate_pool.wait(pool, idx_ok, t + 1)
                    T.gate_pool.wait(pool, tx, t + 1)
                    nc.gpsimd.indirect_dma_start(
                        out=rows[:, q, :], out_offset=None, in_=A.x2_dram[:, :],
                        in_offset=bass.IndirectOffsetOnAxis(ap=idx_st[:, q:q + 1], axis=0)).then_inc(got[q], 16)

        @block.scalar
        def _(act):
            nc.scalar.copy(idx_st[:, :], T.tokens[:, 0:RING]).then_inc(idx_ok, RING)
            for n in range(NWT):
                e, second = divmod(n, 2)
                act.wait_ge(raw_in[n % 2], 16 * (n // 2 + 1))
                nc.scalar.activation((w2 if second else w1)[0][:, e * KD * HID:(e + 1) * KD * HID],
                                     raw[:, n % 2, :], ACT.Copy).then_inc(whi, 1)

            def split_x(t, q):
                act.wait_ge(tx, t + (RING + 1))
                act.wait_ge(h_ok, t + 1)
                nc.scalar.activation(xt[0][:, q % 2, :], px[:, q % 2, 0:KD * P], ACT.Copy).then_inc(xhi, 1)
                nc.scalar.copy(idx_st[:, q:q + 1], T.tokens[:, bass.ds(t + RING, 1)]).then_inc(idx_ok, 1)

            def gelu(t, q):
                act.wait_ge(h_ok, t + 3)
                act.wait_ge(tg, t + 1)
                nc.scalar.activation(act_h[:, q % 2, :], ph[:, q % 2, :], ACT.Gelu).then_inc(g_ok, 1)

            def split_h(t, q):
                act.wait_ge(tg, t + 3)
                act.wait_ge(y_mm, t + 1)
                nc.scalar.activation(ht[0][:, q % 2, :], pg[:, q % 2, :], ACT.Copy).then_inc(hhi, 1)
            skewed(act, (split_x, 0), (gelu, 0), (split_h, 1))

        @block.vector
        def _(dve):
            nc.vector.tensor_scalar(twos[:, :], T.ident[0:2, :], 0.0, 1.0, ALU.mult, ALU.add).then_inc(w_ok, 1)
            dve.sem_inc(tx, RING)
            for sem in (h_ok, tg, y_mm, xlo, g_ok, hlo, y_ok):
                dve.sem_inc(sem, 2)
            for n in range(NWT):
                e, second = divmod(n, 2)
                w = w2 if second else w1
                cols = slice(e * KD * HID, (e + 1) * KD * HID)
                dve.wait_ge(whi, n + 1)
                nc.vector.tensor_tensor(w[1][:, cols], raw[:, n % 2, :], w[0][:, cols].bitcast(F32),
                                        ALU.subtract).then_inc(wlo, 1)
            for e in range(NEXP):
                dve.wait_ge(b_in, 32 * (e + 1))
                if e:
                    dve.wait_ge(b_out, 64 * e)
                nc.vector.tensor_copy(bhi[:, :], braw[:, :]).then_inc(b_hi, 1)
                dve.wait_ge(b_hi, e + 1)
                nc.vector.tensor_tensor(blo[:, :], braw[:, :], bhi[:, :].bitcast(F32), ALU.subtract).then_inc(b_lo, 1)

            def low_x(t, q):
                dve.wait_ge(xhi, t + 1)
                nc.vector.tensor_tensor(xt[1][:, q % 2, :], px[:, q % 2, 0:KD * P],
                                        xt[0][:, q % 2, :].bitcast(F32), ALU.subtract).then_inc(xlo, 1)

            def low_h(t, q):
                dve.wait_ge(hhi, t + 1)
                nc.vector.tensor_tensor(ht[1][:, q % 2, :], pg[:, q % 2, :],
                                        ht[0][:, q % 2, :].bitcast(F32), ALU.subtract).then_inc(hlo, 1)

            def out(t, q):
                dve.wait_ge(y_mm, t + 3)
                if behind(t, 2):
                    dve.wait_ge(y_out[q % 2], (t - q % 2) * 8)
                nc.vector.tensor_copy(y[:, q % 2, :], py[:, q % 2, 0:D]).then_inc(y_ok, 1)
            skewed(dve, (low_x, 0), (low_h, 1), (out, 2))

        @block.tensor
        def _(pe):
            pe.wait_ge(w_ok, 1)
            pe.wait_ge(wlo, NWT)
            pe.wait_ge(b_out, 64 * NEXP)
            expert = {}

            def load_expert(t):
                _, v = nc.values_load_multi_w_load_instructions(
                    T.xtable[0:1, bass.ds(t, 1)], engines=(mybir.EngineType.PE,), min_val=0, max_val=NEXP - 1,
                    skip_runtime_bounds_check_because="the table's values are clamped when it is made")
                return v[0]

            def turn_x(t, q):
                pe.wait_ge(got[q], got_value(t, q))
                pe.wait_ge(xlo, t + 1)
                for c in range(KD):
                    last = nc.tensor.transpose(px[:, q % 2, c * P:(c + 1) * P], rows[:, q, c * P:(c + 1) * P], T.ident[:, :])
                last.then_inc(tx, 1)

            def got_value(t, q):
                return (t - q) * (16 // RING) + 16

            def hidden(t, q):
                e = load_expert(t)
                pe.wait_ge(xlo, t + 3)
                pe.wait_ge(g_ok, t + 1)
                out, k = ph[:, q % 2, :], q % 2
                nc.tensor.matmul(out, twos[:, :], b1[:, bass.ds(e * HID, HID)], start=True, stop=False)
                for c in range(KD):
                    x_h, x_l = (xt[m][:, k, c * P:(c + 1) * P] for m in range(2))
                    w_h, w_l = (w1[m][:, bass.ds(e * (KD * HID) + c * HID, HID)] for m in range(2))
                    nc.tensor.matmul(out, x_h, w_h, start=False, stop=False)
                    nc.tensor.matmul(out, x_h, w_l, start=False, stop=False)
                    last = nc.tensor.matmul(out, x_l, w_h, start=False, stop=c == KD - 1)
                last.then_inc(h_ok, 1)

            def turn_h(t, q):
                pe.wait_ge(g_ok, t + 3)
                pe.wait_ge(hlo, t + 1)
                for c in range(KH):
                    last = nc.tensor.transpose(pg[:, q % 2, c * P:(c + 1) * P], act_h[:, q % 2, c * P:(c + 1) * P], T.ident[:, :])
                last.then_inc(tg, 1)

            def outputs(t, q):
                e = load_expert(t)
                pe.wait_ge(hlo, t + 3)
                pe.wait_ge(y_ok, t + 1)
                out, k = py[:, q % 2, 0:D], q % 2
                nc.tensor.matmul(out, twos[:, :], b2[:, bass.ds(e * D, D)], start=True, stop=False)
                for c in range(KH):
                    h_h, h_l = (ht[m][:, k, c * P:(c + 1) * P] for m in range(2))
                    w_h, w_l = (w2[m][:, bass.ds(e * (KH * D) + c * D, D)] for m in range(2))
                    nc.tensor.matmul(out, h_h, w_h, start=False, stop=False)
                    nc.tensor.matmul(out, h_h, w_l, start=False, stop=False)
                    last = nc.tensor.matmul(out, h_l, w_h, start=False, stop=c == KH - 1)
                last.then_inc(y_mm, 1)
            skewed(pe, (turn_x, 0), (hidden, 0), (turn_h, 1), (outputs, 2))


def combine(nc, A, T, s):
    ctx = ExitStack()
    with ctx:
        def sb(name, shape, dt=F32):
            return ctx.enter_context(nc.sbuf_tensor(name, shape, dt))
        NG = 7
        idx_st = sb("cidx", [P, 2, NG], I32)
        yy = sb("cy", [P, 2, NG, D])
        x1 = sb("cx1", [P, NG, D])
        block = ctx.enter_context(nc.Block())
        idx_ok, got, x_in, sum_ok, done, out_ok = (
            s(f"c_{n}") for n in ("idx", "got", "xin", "sum", "done", "out"))
        slots = T.slot_of[:, :].rearrange("p (j b) -> p j b", j=2)
        rounds = NBLK // NG

        @block.scalar
        def _(act):
            for i in range(rounds):
                if i:
                    act.wait_ge(got, i * 2 * NG * 16)
                nc.scalar.copy(idx_st[:, :, :], slots[:, :, i * NG:(i + 1) * NG]).then_inc(idx_ok, 1)

        @block.gpsimd
        def _(pool):
            for i in range(rounds):
                pool.wait_ge(idx_ok, i + 1)
                if i:
                    pool.wait_ge(done, i)
                for j in range(2):
                    for q in range(NG):
                        nc.gpsimd.indirect_dma_start(
                            out=yy[:, j, q, :], out_offset=None, in_=A.y_dram[:, :],
                            in_offset=bass.IndirectOffsetOnAxis(ap=idx_st[:, j, q:q + 1], axis=0)).then_inc(got, 16)

        @block.vector
        def _(dve):
            for i in range(rounds):
                dve.wait_ge(got, (i + 1) * 2 * NG * 16)
                dve.wait_ge(x_in, 16 * (i + 1))
                nc.vector.tensor_tensor(x1[:, :, :], x1[:, :, :], yy[:, 0, :, :], ALU.add).then_inc(sum_ok, 1)
                dve.wait_ge(sum_ok, i + 1)
                nc.vector.tensor_tensor(x1[:, :, :], x1[:, :, :], yy[:, 1, :, :], ALU.add).then_inc(done, 1)

        @block.sync
        def _(sp):
            n_out = 0
            for i in range(rounds):
                if i:
                    sp.wait_ge(out_ok, 16 * n_out)
                r = slice(i * NG * P, (i + 1) * NG * P)
                sp.dma_start(x1[:, :, :], A.x1_dram[r, :].rearrange("(b p) f -> p b f", p=P)).then_inc(x_in, 16)
                sp.wait_ge(done, i + 1)
                full = NG if i < rounds - 1 else NG - 1
                sp.dma_start(A.out[i * NG * P:(i * NG + full) * P, :].rearrange("(b p) f -> p b f", p=P),
                             x1[:, 0:full, :]).then_inc(out_ok, 16)
                n_out += 1
            sp.dma_start(A.out[(NBLK - 1) * P:NODES, :], x1[0:TAIL, NG - 1, :]).then_inc(out_ok, 16)
            sp.wait_ge(out_ok, 16 * (n_out + 1))


class Names:
    pass


def gps_layer(nc, args):
    ctx = ExitStack()
    with ctx:
        A, T, W = Names(), Names(), Names()
        (A.x, A.src, A.dst, A.w_in, A.b_in, A.w_out, A.b_out, A.wih_t, A.b_ih, A.whh_t, A.b_hh) = (
            args[n] for n in "x src dst w_in b_in w_out b_out wih_t b_ih whh_t b_hh".split())
        (A.wq, A.bq, A.wk_t, A.bk, A.wv_t, A.bv, A.wfc_t, A.bfc, A.wg, A.bg, A.w1, A.b1, A.w2, A.b2, A.out) = (
            args[n] for n in "wq bq wk_t bk wv_t bv wfc_t bfc wg bg w1 b1 w2 b2 out".split())

        def sb(name, shape, dt=F32):
            return ctx.enter_context(nc.sbuf_tensor(name, shape, dt))

        def s(name):
            return ctx.enter_context(nc.semaphore(name))
        NP = NBLK * P
        T.gate_dve, T.gate_pe, T.gate_pool = (Gate(s(f"passed_{n}")) for n in ("dve", "pe", "pool"))
        A.xn_dram, A.xs_dram, A.x1_dram, A.x2_dram = (
            nc.dram_tensor(f"{n}_rows", [NP, D], F32).ap() for n in ("xn", "xs", "x1", "x2"))
        A.split_dram = nc.dram_tensor("split_rows", [NP, SPLIT], F32).ap()
        A.y_dram = nc.dram_tensor("y_rows", [XTILES * P, D], F32).ap()
        T.ident = sb("ident", [P, P])
        T.ident1 = sb("ident1", [P, P], F16)
        T.ident128 = sb("ident128", [P, P], F16)
        T.upper = sb("upper", [P, P], F16)
        T.colsel = sb("colsel", [P, 192], F16)
        T.ones16 = sb("ones16", [P, 16], F16)
        T.zeros16 = sb("zeros16", [P, 512], F16)
        T.ramp16 = sb("ramp16", [P, ETILES], F16)
        T.ramp32 = sb("ramp32", [P, P])
        T.mean2, T.rstd2, T.tmp2 = (sb(n, [P, NBLK]) for n in ("mean2", "rstd2", "tmp2"))
        T.expert = sb("expert", [P, 2 * NBLK])
        T.slot_of = sb("slot_of", [P, 2 * NBLK], I32)
        T.tokens = sb("tokens", [P, XTILES + RING], I32)
        T.xtable = sb("xtable", [1, XTILES], I32)
        with ExitStack() as blocks:
            def sb2(name, shape, dt=F32):
                return blocks.enter_context(nc.sbuf_tensor(name, shape, dt))
            W.hi = sb2("whi", [P, WCOLS], F32R)
            W.lo = sb2("wlo", [P, WCOLS], F32R)
            W.aux = sb2("waux", [6, GCOLS], F32R)
            with ExitStack() as first:
                T.ramp_i = first.enter_context(nc.sbuf_tensor("ramp_i", [P, ETILES], I32))
                T.gram = first.enter_context(nc.sbuf_tensor("gram", [P, 3, D + 1], F32))
                constants(nc, T, s)
                normalise(nc, A, T, s)
                weights(nc, A, T, W, s)
            with ExitStack() as edges:
                def sb3(name, shape, dt=F32):
                    return edges.enter_context(nc.sbuf_tensor(name, shape, dt))
                acc = sb3("acc", [P, 2 * NBLK * ACOLS])
                aggregate(nc, A, T, acc, s)
                update(nc, A, T, W, acc, s)
                route(nc, A, T, acc, s)
        sort_tokens(nc, A, T, s)
        experts(nc, A, T, s)
        combine(nc, A, T, s)


def kernel(**inputs):
    import numpy as _np
    import concourse.bacc as _bacc
    from concourse import mybir as _mybir
    from concourse.bass_utils import run_bass_kernel_spmd as _run

    names = {
        "x": ("x", 0), "src": ("src", 0), "dst": ("dst", 0),
        "w_in": ("L0_gnn_W_in", 0), "b_in": ("L0_gnn_b_in", 0), "w_out": ("L0_gnn_W_out", 0), "b_out": ("L0_gnn_b_out", 0),
        "wih_t": ("L0_gnn_W_ih", 1), "b_ih": ("L0_gnn_b_ih", 0), "whh_t": ("L0_gnn_W_hh", 1), "b_hh": ("L0_gnn_b_hh", 0),
        "wq": ("L0_mix_Wq", 0), "bq": ("L0_mix_bq", 0), "wk_t": ("L0_mix_Wk", 1), "bk": ("L0_mix_bk", 0),
        "wv_t": ("L0_mix_Wv", 1), "bv": ("L0_mix_bv", 0), "wfc_t": ("L0_mix_Wfc", 1), "bfc": ("L0_mix_bfc", 0),
        "wg": ("L0_ffn_Wg", 0), "bg": ("L0_ffn_bg", 0), "w1": ("L0_ffn_W1", 0), "b1": ("L0_ffn_b1", 0),
        "w2": ("L0_ffn_W2", 0), "b2": ("L0_ffn_b2", 0),
    }
    nc = _bacc.Bacc("TRN2", target_bir_lowering=False, num_devices=1)
    arrays, args = {}, {}
    for name, (given, turned) in names.items():
        a = _np.asarray(inputs[given])
        a = _np.ascontiguousarray(a.T if turned else a)
        arrays[f"in_{name}_dram"] = a
        args[name] = nc.dram_tensor(f"in_{name}_dram", a.shape, _mybir.dt.from_np(a.dtype), kind="ExternalInput").ap()
    args["out"] = nc.dram_tensor("out_0_dram", (NODES, D), _mybir.dt.float32, kind="ExternalOutput").ap()
    gps_layer(nc, args)
    r = _run(nc, [arrays], core_ids=[0])
    return r.results[0]["out_0_dram"]
```

```python
import concourse.bass as bass
from concourse import mybir
from contextlib import ExitStack

F32 = mybir.dt.float32
F32R = mybir.dt.float32r
F16 = mybir.dt.float16
I32 = mybir.dt.int32
U16 = mybir.dt.uint16
ALU = mybir.AluOpType
ACT = mybir.ActivationFunctionType
AX = mybir.AxisListType

P = 128
NODES = 6250
D = 256
NBLK = -(-NODES // P)
TAIL = NODES - (NBLK - 1) * P
EDGES = 100000
EP = 125
EC = EDGES // EP
HEADS = 8
DK = D // HEADS
NEXP = 8
HID = 512
EPS = 1e-5

UNIT = 2
RING = 4


def whole(n, m):
    return -(-n // m) * m


CHUNKS = 2
CC = EC // CHUNKS
ETILES = whole((EP * CC + NBLK * (UNIT * P - 1)) // P, UNIT * RING)
ROUNDS = ETILES // (UNIT * RING)
XTILES = whole((2 * NBLK * P + NEXP * (P - 1)) // P, RING)
LOW = 11
ACOLS = D + 2
SPLIT = ACOLS + D
WCOLS = 20 * D
KD, KH = D // P, HID // P
MASKS = 4
RAWS = 4
GCOLS = 5 * D


class Count:

    def __init__(self, sem):
        self.sem, self.n = sem, 0

    def after(self, eng, ins):
        self.n += 1
        ins.then_inc(self.sem, 1)
        eng.wait_ge(self.sem, self.n)


def constants(nc, T, s):
    with nc.Block() as block:
        @block.gpsimd
        def _(pool):
            c = Count(s("const_chain"))
            for t, v in ((T.ident, 0.0), (T.ident1, 0.0), (T.ident128, 0.0), (T.upper, 1.0),
                         (T.colsel, 0.0), (T.ones16, 1.0), (T.zeros16, 0.0)):
                c.after(pool, nc.gpsimd.memset(t[:, :], v))
            for t, v in ((T.ident, 1.0), (T.ident1, 1.0), (T.ident128, 128.0)):
                c.after(pool, nc.gpsimd.affine_select(
                    out=t[:, :], in_=t[:, :], pattern=[[-1, P]], compare_op=ALU.not_equal,
                    fill=v, base=0, channel_multiplier=1))
            c.after(pool, nc.gpsimd.affine_select(
                out=T.upper[:, :], in_=T.upper[:, :], pattern=[[1, P]], compare_op=ALU.is_gt,
                fill=0.0, base=0, channel_multiplier=-1))
            c.after(pool, nc.gpsimd.memset(T.colsel[:, 63:64], 1.0))
            c.after(pool, nc.gpsimd.iota(T.ramp_i[:, :], pattern=[[1, ETILES]], base=0,
                                         channel_multiplier=0))
            c.after(pool, nc.gpsimd.tensor_copy(T.ramp16[:, :], T.ramp_i[:, :]))
            c.after(pool, nc.gpsimd.tensor_copy(T.ramp32[:, :], T.ramp_i[:, 0:P]))


def rstd_steps(nc, dve, c, st, mean, rstd, tmp):
    me, ve = st[:, :, 1], st[:, :, 2]
    mo, vo = st[:, :, 4], st[:, :, 5]
    c.after(dve, nc.vector.tensor_tensor(mean, me, mo, ALU.add))
    c.after(dve, nc.vector.tensor_tensor(tmp, me, mo, ALU.subtract))
    c.after(dve, nc.vector.tensor_tensor(rstd, ve, vo, ALU.add))
    c.after(dve, nc.vector.tensor_scalar(mean, mean, 0.5, None, ALU.mult))
    c.after(dve, nc.vector.tensor_tensor(tmp, tmp, tmp, ALU.mult))
    c.after(dve, nc.vector.tensor_scalar(rstd, rstd, 1.0 / D, EPS, ALU.mult, ALU.add))
    c.after(dve, nc.vector.scalar_tensor_tensor(out=rstd, in0=tmp, scalar=0.25, in1=rstd,
                                                op0=ALU.mult, op1=ALU.add))


class Gate:

    def __init__(self, passed):
        self.passed = passed

    def wait(self, eng, sem, value):
        eng.wait_ge(sem, value)
        eng.sem_inc(self.passed, 1)


def behind(b, n):
    return not isinstance(b, int) or b >= n


def pairs(n, eng, body, first=0):
    m = (n - first) // 2
    if m:
        with eng.Fori(0, m) as j:
            for k in range(2):
                body(j * 2 + (first + k), k)
    if (n - first) % 2:
        body(n - 1, 0)


def cycle(n, m, eng, body, first=0):
    rounds = (n - first) // m
    with eng.Fori(0, rounds) as j:
        for k in range(m):
            body(j * m + (first + k), k)
    for b in range(first + rounds * m, n):
        body(b, b % m)


def normalise(nc, A, T, V, s):
    ctx = ExitStack()
    with ctx:
        def sb(name, shape, dt=F32):
            return ctx.enter_context(nc.sbuf_tensor(name, shape, dt))
        X = sb("X", [P, NBLK, D])
        XN = X
        st = sb("st", [P, NBLK, 6])
        mean, rstd, tmp = sb("mean", [P, NBLK]), sb("rstd", [P, NBLK]), sb("tmp", [P, NBLK])
        SLOTS = 4
        both = sb("both", [P, SLOTS, SPLIT], F32R)
        xhi, xlo = both[:, :, 0:ACOLS], both[:, :, ACOLS:]
        pg = ctx.enter_context(nc.psum_tensor("pg", [P, 2, 512], F32))
        block = ctx.enter_context(nc.Block())
        NG = 7
        x_in = [s(f"x_in{g}") for g in range(NBLK // NG)]
        tail_clear, tail_in, stats, var_ok, sd_ok, xn_ok = (
            s(n) for n in ("tail_clear", "tail_in", "stats", "var_ok", "sd_ok", "xn_ok"))
        both_out = [s(f"both_out{k}") for k in range(SLOTS)]
        hi_ok, lo_ok, gram_used, chain, mm = (
            s(n) for n in ("hi_ok", "lo_ok", "gram_used", "n_chain", "gram_ok"))

        @block.sync
        def _(sp):
            for g in range(NBLK // NG):
                b0, n = g * NG, NG if g < NBLK // NG - 1 else NG - 1
                sp.dma_start(X[:, b0:b0 + n, :],
                             A.x[b0 * P:(b0 + n) * P, :].rearrange("(b p) f -> p b f", p=P)).then_inc(x_in[g], 16)
            sp.wait_ge(tail_clear, 1)
            sp.dma_start(X[0:TAIL, NBLK - 1, :], A.x[(NBLK - 1) * P:NODES, :]).then_inc(tail_in, 16)

            def store(b, k):
                sp.wait_ge(lo_ok, b + 1)
                sp.dma_start(A.split_dram[bass.ds(b * P, P), :], both[:, k, :].bitcast(F32)).then_inc(both_out[k], 16)
            cycle(NBLK, SLOTS, sp, store)
            for k in range(SLOTS):
                sp.wait_ge(both_out[k], 16 * len(range(k, NBLK, SLOTS)))

        @block.scalar
        def _(act):
            act.wait_ge(var_ok, 1)
            nc.scalar.activation(tmp[:, :], tmp[:, :], ACT.Sqrt).then_inc(sd_ok, 1)

            def high(b, k):
                act.wait_ge(xn_ok, b + 1)
                act.wait_ge(gram_used, b + 1)
                if behind(b, SLOTS):
                    act.wait_ge(both_out[k], (b - k) * (16 // SLOTS))
                nc.scalar.copy(xhi[:, k, 0:D], XN[:, bass.ds(b, 1), :].rearrange("p o f -> p (o f)")).then_inc(hi_ok, 1)
            for b in range(SLOTS):
                high(b, b)
            cycle(NBLK, SLOTS, act, high, first=SLOTS)

        @block.gpsimd
        def _(pool):
            pool.wait_ge(tail_in, 16)
            V.load(pool, A)

        @block.vector
        def _(dve):
            c = Count(chain)
            nc.vector.memset(X[:, NBLK - 1, :], 0.0).then_inc(tail_clear, 1)
            nc.vector.tensor_scalar(xhi[:, :, D:ACOLS], T.ones16[:, 0:2 * SLOTS].rearrange("p (a b) -> p a b", b=2),
                                    1.0, None, ALU.mult).then_inc(gram_used, SLOTS)
            for g in range(NBLK // NG):
                dve.wait_ge(x_in[g], 16)
                if g == NBLK // NG - 1:
                    dve.wait_ge(tail_in, 16)
                for b in range(g * NG, g * NG + NG):
                    nc.vector.bn_stats(st[:, b, :], X[:, b, :]).then_inc(stats, 1)
            dve.wait_ge(stats, NBLK)
            rstd_steps(nc, dve, c, st, mean[:, :], rstd[:, :], tmp[:, :])
            nc.vector.tensor_copy(tmp[:, :], rstd[:, :]).then_inc(var_ok, 1)
            dve.wait_ge(sd_ok, 1)
            c.after(dve, nc.vector.reciprocal(rstd[:, :], tmp[:, :]))
            with dve.Fori(0, NBLK // NG) as g:
                for k in range(NG):
                    b = g * NG + k
                    nc.vector.tensor_scalar(XN[:, bass.ds(b, 1), :], X[:, bass.ds(b, 1), :],
                                            mean[:, bass.ds(b, 1)], rstd[:, bass.ds(b, 1)],
                                            ALU.subtract, ALU.mult).then_inc(xn_ok, 1)

            def low(b, k):
                dve.wait_ge(hi_ok, b + 1)
                nc.vector.tensor_tensor(xlo[:, k, :], XN[:, bass.ds(b, 1), :].rearrange("p o f -> p (o f)"),
                                        xhi[:, k, 0:D].bitcast(F32), ALU.subtract).then_inc(lo_ok, 1)
            cycle(NBLK, SLOTS, dve, low)

            dve.wait_ge(mm, 1)
            c.after(dve, nc.vector.tensor_copy(T.gram[:, 0:2, :], pg[:, :, 0:D + 1]))

        @block.tensor
        def _(pe):
            for f in range(2):
                nc.tensor.matmul(pg[:, f, 0:ACOLS], T.zeros16[:, 0:P], T.zeros16[:, 0:ACOLS], start=True, stop=False)

            def gram(b, k):
                pe.wait_ge(lo_ok, b + 1)
                for f in range(2):
                    hi, lo = xhi[:, k, f * P:(f + 1) * P], xlo[:, k, f * P:(f + 1) * P]
                    nc.tensor.matmul(pg[:, f, 0:ACOLS], hi, xhi[:, k, :], start=False, stop=False)
                    nc.tensor.matmul(pg[:, f, 0:ACOLS], lo, xhi[:, k, :], start=False, stop=False)
                    last = nc.tensor.matmul(pg[:, f, 0:D], hi, xlo[:, k, :], start=False, stop=False)
                last.then_inc(gram_used, 1)
            cycle(NBLK, SLOTS, pe, gram)
            for f in range(2):
                last = nc.tensor.matmul(pg[:, f, 0:ACOLS], T.zeros16[:, 0:P], T.zeros16[:, 0:ACOLS], start=False, stop=True)
            last.then_inc(mm, 1)


def part(w, o, q, n=1):
    start, width, first = ((0, 2 * D, 0), (12 * D, D, 0), (16 * D, 2 * D, 4))[o]
    v = w[:, start + (q - first) * width:start + (q - first + n) * width]
    return v.rearrange("p (q c) -> p q c", q=n) if n > 1 else v


class RawWeights:

    def __init__(self, nc, ctx, s):
        def sb(name, shape, dt=F32):
            return ctx.enter_context(nc.sbuf_tensor(name, shape, dt))
        self.wv = sb("wv", [P, 3, D])
        self.wk = sb("wk", [P, 3, D])
        self.wq = sb("wq", [P, 2, D + 1])
        self.wfc = sb("wfc", [P, 2, D])
        self.win = sb("win", [P, 2, 2, D + 1])
        self.wih = sb("wih", [P, 4, 3 * D])
        self.whh = sb("whh", [P, 2, 3 * D])
        self.row = sb("row", [1, 3, GCOLS])
        self.bfc = sb("bfc", [1, D])
        self.bhh = sb("bhh", [1, 3 * D])
        self.w_in, self.loads = s("w_in"), 0

    def load(self, eng, A):
        def load(dst, src):
            eng.dma_start(dst, src).then_inc(self.w_in, 16)
            self.loads += 1

        def line(v):
            return v.rearrange("(o n) -> o n", o=1)

        def parts(w):
            return w.rearrange("(c p) n -> p c n", p=P)
        for t, w, b in ((self.wv, A.wv_t, A.bv), (self.wk, A.wk_t, A.bk)):
            load(t[:, 0:2, :], parts(w))
            load(t[0:1, 2, :], line(b))
        load(self.wq[:, :, 0:D], parts(A.wq))
        for c in range(2):
            load(self.wq[:, c, D:D + 1], A.bq[c * P:(c + 1) * P].rearrange("(p o) -> p o", o=1))
        load(self.wfc[:, :, :], parts(A.wfc_t))
        for d, (w, b) in enumerate(((A.w_in, A.b_in), (A.w_out, A.b_out))):
            load(self.win[:, d, :, 0:D], parts(w))
            for c in range(2):
                load(self.win[:, d, c, D:D + 1], b[c * P:(c + 1) * P].rearrange("(p o) -> p o", o=1))
        load(self.wih[:, :, :], parts(A.wih_t))
        load(self.whh[:, :, :], parts(A.whh_t))
        load(self.bfc[:, :], line(A.bfc))
        load(self.row[0:1, 0, 0:3 * D], line(A.b_ih))
        load(self.bhh[:, :], line(A.b_hh))
        eng.wait_ge(self.w_in, 16 * self.loads)


def weights(nc, A, T, V, W, s):
    ctx = ExitStack()
    with ctx:
        def sb(name, shape, dt=F32):
            return ctx.enter_context(nc.sbuf_tensor(name, shape, dt))
        G = T.gram
        mark = sb("mark", [1, 2])
        wv, wk, wq, wfc, win, wih, whh, row, bfc, bhh, w_in = (
            V.wv, V.wk, V.wq, V.wfc, V.win, V.wih, V.whh, V.row, V.bfc, V.bhh, V.w_in)
        T1 = sb("T1", [P, 3, D])
        KV = sb("KV", [P, 2, D])
        M1 = sb("M1", [P, 2, D + 1])
        rhi = sb("rhi", [1, 3, GCOLS], F32R)
        rlo = sb("rlo", [1, 3, GCOLS], F32R)
        WF = sb("WF", [P, WCOLS])
        pw = ctx.enter_context(nc.psum_tensor("pw", [P, 4, 512], F32))
        NPIECE = 5
        PIECE = WCOLS // NPIECE
        block = ctx.enter_context(nc.Block())
        mm, ev, rows_ok, aux_in, split_hi, chain = (
            s(n) for n in ("mm", "ev", "rows_ok", "aux_in", "split_hi", "w_chain"))
        @block.sync
        def _(sp):
            sp.wait_ge(rows_ok, 6)
            for d in range(3):
                sp.dma_start(W.aux[2 * d:2 * d + 1, :].bitcast(F32), rhi[0:1, d, :].bitcast(F32)).then_inc(aux_in, 16)
                sp.dma_start(W.aux[2 * d + 1:2 * d + 2, :].bitcast(F32), rlo[0:1, d, :].bitcast(F32)).then_inc(aux_in, 16)
            sp.wait_ge(aux_in, 96)

        @block.scalar
        def _(act):
            act.wait_ge(ev, 13)
            for q in range(NPIECE):
                cols = slice(q * PIECE, (q + 1) * PIECE)
                nc.scalar.activation(W.hi[:, cols], WF[:, cols], ACT.Copy).then_inc(split_hi, 1)

        @block.vector
        def _(dve):
            c = Count(chain)
            dve.wait_ge(w_in, 16 * V.loads)
            c.after(dve, nc.vector.memset(row[0:1, 1:3, :], 0.0))
            c.after(dve, nc.vector.memset(G[0:1, 2, D:D + 1], float(NODES)))
            c.after(dve, nc.vector.memset(KV[:, :, :], 0.0))
            ev_n = [0]

            def evict(after_mm, *copies):
                dve.wait_ge(mm, after_mm)
                for ins in copies:
                    last = ins()
                last.then_inc(ev, 1)
                ev_n[0] += 1
            nc.vector.memset(mark[:, :], 0.0).then_inc(ev, 1)
            evict(1, lambda: nc.vector.tensor_copy(G[0:1, 2, 0:D], pw[0:1, 0, 0:D]))
            evict(2, lambda: nc.vector.tensor_copy(T1[:, 0:2, :], pw[:, 0:2, 0:D]),
                  lambda: nc.vector.tensor_copy(T1[0:1, 2, :], pw[0:1, 2, 0:D]))
            heads = [(h // 4, (h % 4) * DK, h * DK) for h in range(HEADS)]
            evict(3, *[lambda a=a, p=p, q=q: nc.vector.tensor_scalar(
                KV[p:p + DK, a, q:q + DK], pw[p:p + DK, a, q:q + DK], 1.0 / NODES, None, ALU.mult)
                for a, p, q in heads])
            evict(4, lambda: nc.vector.tensor_copy(M1[:, :, :], pw[:, 0:2, 0:D + 1]))
            evict(5, lambda: nc.vector.tensor_copy(part(WF, 2, 4, 2)[:, :, D:2 * D], pw[:, 0:2, 0:D]),
                  lambda: nc.vector.tensor_tensor(row[0:1, 0, 4 * D:5 * D], pw[0:1, 2, 0:D], bfc[0:1, :], ALU.add))
            n = 6
            for d in range(2):
                for j in range(3):
                    evict(n, lambda: nc.vector.tensor_copy(part(WF, j // 2, 2 * d, 2)[:, :, (j % 2) * D:(j % 2 + 1) * D], pw[:, 0:2, 0:D]),
                          lambda: nc.vector.tensor_copy(row[0:1, 1 + d, j * D:(j + 1) * D], pw[0:1, 2, 0:D]))
                    n += 1
            c.after(dve, nc.vector.tensor_copy(part(WF, 0, 4, 2), whh[:, :, 0:2 * D]))
            c.after(dve, nc.vector.tensor_copy(part(WF, 2, 4, 2)[:, :, 0:D], whh[:, :, 2 * D:3 * D]))
            c.after(dve, nc.vector.tensor_tensor(row[0:1, 0, 0:2 * D], row[0:1, 0, 0:2 * D], bhh[0:1, 0:2 * D], ALU.add))
            c.after(dve, nc.vector.tensor_copy(row[0:1, 0, 3 * D:4 * D], bhh[0:1, 2 * D:3 * D]))
            nc.vector.memset(mark[:, :], 0.0).then_inc(ev, 1)
            for d in range(3):
                nc.vector.tensor_copy(rhi[0:1, d, :], row[0:1, d, :]).then_inc(rows_ok, 1)
                dve.wait_ge(rows_ok, 2 * d + 1)
                nc.vector.tensor_tensor(rlo[0:1, d, :], row[0:1, d, :], rhi[0:1, d, :].bitcast(F32),
                                        ALU.subtract).then_inc(rows_ok, 1)
            for q in range(NPIECE):
                dve.wait_ge(split_hi, q + 1)
                cols = slice(q * PIECE, (q + 1) * PIECE)
                nc.vector.tensor_tensor(W.lo[:, cols], WF[:, cols], W.hi[:, cols].bitcast(F32), ALU.subtract)

        @block.tensor
        def _(pe):
            def product(out_parts, lhs, rhs):
                for a, out in enumerate(out_parts):
                    for k, r in enumerate(rhs):
                        last = nc.tensor.matmul(out, lhs[k][a], r, start=k == 0, stop=k == len(rhs) - 1)
                last.then_inc(mm, 1)
            cut = ((0, P), (P, 2 * P), (2 * P, 2 * P + 1))
            three = [pw[:, 0, 0:D], pw[:, 1, 0:D], pw[0:1, 2, 0:D]]
            pe.wait_ge(w_in, 16 * V.loads)
            pe.wait_ge(ev, 1)
            for f in range(2):
                last = nc.tensor.matmul(pw[0:1, 0, f * P:(f + 1) * P], G[:, f, D:D + 1], T.ident[:, :], start=True, stop=True)
            last.then_inc(mm, 1)
            pe.wait_ge(ev, 2)
            kp = (P, P, 1)
            product(three, [[G[0:kp[c], c, a:b] for a, b in cut] for c in range(3)],
                    [wv[0:kp[c], c, :] for c in range(3)])
            pe.wait_ge(ev, 3)
            product(three[:2], [[wk[0:kp[c], c, a:b] for a, b in cut[:2]] for c in range(3)],
                    [T1[0:kp[c], c, :] for c in range(3)])
            pe.wait_ge(ev, 4)
            product([pw[:, 0, 0:D + 1], pw[:, 1, 0:D + 1]],
                    [[KV[:, c, a:b] for a, b in cut[:2]] for c in range(2)], [wq[:, c, :] for c in range(2)])
            pe.wait_ge(ev, 5)
            product(three, [[M1[:, c, a:b] for a, b in cut] for c in range(2)], [wfc[:, c, :] for c in range(2)])
            n = 6
            for d in range(2):
                for j in range(3):
                    pe.wait_ge(ev, n)
                    product(three, [[win[:, d, c, a:b] for a, b in cut] for c in range(2)],
                            [wih[:, 2 * d + c, j * D:(j + 1) * D] for c in range(2)])
                    n += 1


class Sort:

    def __init__(self, nc, ctx, s, name, parts, cols, bins, tiles, counted, merged, per, groups, ring=2, together=1, helped=()):
        def sb(n, shape, dt=F32):
            return ctx.enter_context(nc.sbuf_tensor(f"{name}_{n}", shape, dt))
        self.parts, self.cols, self.bins, self.tiles = parts, cols, bins, tiles
        self.n_count, self.n_merge, self.per, self.n_group = counted, merged, per, groups
        self.ring = ring
        self.together = together
        self.key = sb("key", [P, cols], F16)
        self.mask = sb("mask", [P, MASKS, cols], F16)
        self.colsum = sb("colsum", [P, cols])
        self.before = sb("before", [P, cols])
        self.slot_i = sb("slot_i", [P, cols], I32)
        self.tile_i = sb("tile_i", [P, cols], I32)
        self.tile16 = sb("tile16", [P, cols], F16)
        self.rest16 = sb("rest16", [P, cols], F16)
        self.pos = sb("pos", [P, cols])
        self.parts16 = sb("parts16", [P, cols, 2], F16)
        self.part0, self.part1 = self.parts16[:, :, 0], self.parts16[:, :, 1]
        self.low, self.col = self.colsum, self.before
        self.total_i = sb("total_i", [P, 1], I32)
        self.ntiles = sb("ntiles", [P, 1])
        self.ntiles16 = sb("ntiles16", [P, 1], F16)
        self.base = sb("base", [P, 1])
        self.end = sb("end", [P, 1])
        self.past = sb("past", [P, tiles], F16)
        self.to_slot = sb("to_slot", [P, ring, per, 2, P], F16)
        self.to_tile = sb("to_tile", [P, ring, per, tiles], F16)
        self.pa = ctx.enter_context(nc.psum_tensor(f"{name}_pa", [P, 512], F32))
        self.pt = ctx.enter_context(nc.psum_tensor(f"{name}_pt", [P, 512], F32))
        self.pp = [ctx.enter_context(nc.psum_tensor(f"{name}_pp{k}", [P, 512], F32)) for k in range(2)]
        self.masked, self.used, self.counted, self.tiled, self.based, self.split, self.placed, \
            self.merged, self.pasts, self.tabled, self.chain, self.cleared, self.hots, self.hot_used, self.done, self.slots_ok = (
                s(f"{name}_{n}") for n in ("masked", "used", "counted", "tiled", "based", "split",
                                           "placed", "merged", "pasts", "tabled", "chain", "cleared",
                                           "hots", "hot_used", "done", "slots_ok"))
        self.helpers = {k: s(f"{name}_helped{k}") for k in helped}


class SortDVE:

    def __init__(self, nc, dve, T, R):
        self.nc, self.dve, self.T, self.R, self.c = nc, dve, T, R, Count(R.chain)
        nc.vector.memset(R.pos[:, :], 0.0).then_inc(R.cleared, 1)
        dve.wait_ge(R.cleared, 1)
        for sem, ahead in [(R.used, MASKS), (R.merged, MASKS), (R.hot_used, R.ring)] + [
                (sem, R.ring) for sem in R.helpers.values()]:
            dve.sem_inc(sem, ahead)

    def mask(self, b, k):
        R = self.R
        n = R.parts
        return self.nc.vector.tensor_scalar(R.mask[0:n, k, :], R.key[0:n, :], self.T.ramp32[0:n, bass.ds(b, 1)],
                                            None, ALU.is_equal).then_inc(R.masked, 1)

    def count(self, ch, b, k):
        R = self.R
        self.dve.wait_ge(R.used, b + (ch * R.n_count + 1))
        self.mask(b, k)

    def bases(self, ch, j, table, table_base):
        if j == 0:
            self.column_sums(ch)
        elif j == 1:
            self.bin_tiles(ch)
        elif j == 2:
            self.bin_starts(ch)
        else:
            self.column_starts(ch, table, table_base)

    def column_sums(self, ch):
        nc, dve, R, c = self.nc, self.dve, self.R, self.c
        dve.wait_ge(R.counted, ch + 1)
        c.after(dve, nc.vector.tensor_copy(R.colsum[:, :], R.pa[:, 0:R.cols]))
        zero = R.slot_i[:, :].bitcast(F32)
        c.after(dve, nc.vector.memset(zero, 0.0))
        c.after(dve, nc.vector.tensor_tensor_scan(R.before[:, :], R.colsum[:, :], zero, 0.0, ALU.add, ALU.add))

    def bin_tiles(self, ch):
        nc, dve, R, c = self.nc, self.dve, self.R, self.c
        c.after(dve, nc.vector.tensor_scalar(R.total_i[:, :], R.before[:, R.cols - 1:R.cols],
                                              float(R.together * P - 1), None, ALU.add))
        c.after(dve, nc.vector.tensor_scalar(R.total_i[:, :], R.total_i[:, :], 6 + R.together, None,
                                              ALU.arith_shift_right))
        c.after(dve, nc.vector.tensor_scalar(R.ntiles[:, :], R.total_i[:, :], float(R.together), None, ALU.mult))
        nc.vector.tensor_copy(R.ntiles16[:, :], R.ntiles[:, :]).then_inc(R.tiled, 1)
        c.after(dve, nc.vector.tensor_tensor(R.before[:, :], R.before[:, :], R.colsum[:, :], ALU.subtract))

    def bin_starts(self, ch):
        nc, dve, R, T, c = self.nc, self.dve, self.R, self.T, self.c
        dve.wait_ge(R.based, ch + 1)
        c.after(dve, nc.vector.tensor_scalar(R.base[:, :], R.pa[:, 0:1], float(P), None, ALU.mult))
        c.after(dve, nc.vector.tensor_tensor(R.end[:, :], R.pa[:, 0:1], R.ntiles[:, :], ALU.add))
        nc.vector.tensor_scalar(R.past[:, :], T.ramp16[:, 0:R.tiles], R.end[:, 0:1], None, ALU.is_ge).then_inc(R.pasts, 1)

    def column_starts(self, ch, table, table_base):
        nc, dve, R, c = self.nc, self.dve, self.R, self.c
        c.after(dve, nc.vector.tensor_scalar(R.slot_i[:, :], R.before[:, :], R.base[:, 0:1], None, ALU.add))
        c.after(dve, nc.vector.tensor_scalar(R.tile_i[:, :], R.slot_i[:, :], 7, None, ALU.arith_shift_right))
        c.after(dve, nc.vector.tensor_scalar(R.slot_i[:, :], R.slot_i[:, :], P - 1, None, ALU.bitwise_and))
        c.after(dve, nc.vector.tensor_copy(R.tile16[:, :], R.tile_i[:, :]))
        nc.vector.tensor_copy(R.rest16[:, :], R.slot_i[:, :]).then_inc(R.split, 1)
        self.mask(0, 0)
        dve.wait_ge(R.tabled, ch + 1)
        c.after(dve, nc.vector.tensor_scalar(table, R.pt[0:1, 0:R.tiles], float(R.bins - 1), float(table_base), ALU.min, ALU.add))

    def merge(self, ch, b, k):
        R = self.R
        n, done = R.parts, ch * R.n_merge
        self.dve.wait_ge(R.merged, b + (done + 2))
        self.mask(b + 1, (k + 1) % MASKS)
        self.T.gate_dve.wait(self.dve, R.merged, b + (done + MASKS))
        self.T.gate_dve.wait(self.dve, R.placed, b + (done + 1))
        self.nc.vector.copy_predicated(R.pos[0:n, :], R.mask[0:n, k, :].bitcast(U16),
                                       R.pp[k % 2][0:n, 0:R.cols]).then_inc(R.merged, 1)

    def slots(self, ch):
        nc, dve, R, c = self.nc, self.dve, self.R, self.c
        dve.wait_ge(R.merged, (ch + 1) * R.n_merge + MASKS)
        c.after(dve, nc.vector.tensor_copy(R.slot_i[:, :], R.pos[:, :]))
        c.after(dve, nc.vector.tensor_scalar(R.tile_i[:, :], R.slot_i[:, :], P - 1, None, ALU.bitwise_and))
        c.after(dve, nc.vector.tensor_copy(R.low[:, :], R.tile_i[:, :]))
        c.after(dve, nc.vector.tensor_scalar(R.tile_i[:, :], R.slot_i[:, :], 7, None, ALU.arith_shift_right))
        c.after(dve, nc.vector.tensor_copy(R.col[:, :], R.tile_i[:, :]))
        dve.sem_inc(R.slots_ok, 1)

    def spread(self, ch, g, n, k):
        nc, R, T = self.nc, self.R, self.T
        m = R.parts
        self.dve.wait_ge(R.hot_used, g + (ch * R.n_group + 1))
        for j in range(n):
            e = bass.ds(g * n + j, 1)
            last = nc.vector.scalar_tensor_tensor(
                out=R.to_slot[0:m, k, j, :, :], in0=T.ramp16[0:m, 0:P].unsqueeze(1).to_broadcast([m, 2, P]),
                scalar=R.low[0:m, e],
                in1=R.parts16[0:m, e, :].rearrange("p o q -> p (o q)").unsqueeze(2).to_broadcast([m, 2, P]),
                op0=ALU.is_equal, op1=ALU.mult)
            if not ch and k in R.helpers:
                continue
            last = nc.vector.tensor_scalar(R.to_tile[0:m, k, j, :], T.ramp16[0:m, 0:R.tiles], R.col[0:m, e],
                                           None, ALU.is_equal)
        last.then_inc(R.hots, 1)


class SortPE:

    def __init__(self, nc, pe, T, R):
        self.nc, self.pe, self.T, self.R = nc, pe, T, R

    def empty(self, out, start):
        w = out.shape[-1]
        return self.nc.tensor.matmul(out, self.T.zeros16[:, 0:P], self.T.zeros16[:, 0:w], start=start, stop=not start)

    def open_count(self):
        self.empty(self.R.pa[:, 0:self.R.cols], True)

    def count(self, ch, b, k):
        R, n = self.R, self.R.parts
        self.T.gate_pe.wait(self.pe, R.masked, b + (self.masks(ch) + 1))
        self.nc.tensor.matmul(R.pa[:, 0:R.cols], self.T.colsel[0:n, bass.ds(63 - b, P)],
                              R.mask[0:n, k, :], start=False, stop=False).then_inc(R.used, 1)

    def masks(self, ch):
        return ch * (self.R.n_count + 1 + self.R.n_merge)

    def bases(self, ch, j):
        if j == 0:
            self.empty(self.R.pa[:, 0:self.R.cols], False).then_inc(self.R.counted, 1)
        elif j == 1:
            self.bin_tiles(ch)
        elif j == 2:
            self.bin_starts(ch)
        else:
            self.pe.wait_ge(self.R.split, ch + 1)

    def bin_tiles(self, ch):
        nc, pe, R, T = self.nc, self.pe, self.R, self.T
        pe.wait_ge(R.tiled, ch + 1)
        nc.tensor.matmul(R.pa[:, 0:1], T.upper[:, :], R.ntiles16[:, :], start=True, stop=True).then_inc(R.based, 1)

    def bin_starts(self, ch):
        nc, pe, R, T = self.nc, self.pe, self.R, self.T
        pe.wait_ge(R.pasts, ch + 1)
        nc.tensor.matmul(R.pt[0:1, 0:R.tiles], T.ones16[0:R.bins, 0:1], R.past[0:R.bins, :],
                         start=True, stop=True).then_inc(R.tabled, 1)

    def merge(self, ch, b, k):
        nc, pe, R, T = self.nc, self.pe, self.R, self.T
        n = R.parts
        pe.wait_ge(R.masked, b + (self.masks(ch) + R.n_count + 1))
        pe.wait_ge(R.merged, b + (ch * R.n_merge + MASKS - 1))
        out = R.pp[k % 2][0:n, 0:R.cols]
        nc.tensor.matmul(out, T.ident128[:, bass.ds(b, 1)].to_broadcast([P, n]), R.tile16[:, :], start=True, stop=False)
        nc.tensor.matmul(out, T.ident1[:, bass.ds(b, 1)].to_broadcast([P, n]), R.rest16[:, :], start=False, stop=False)
        nc.tensor.matmul(out, T.upper[0:n, 0:n], R.mask[0:n, k, :], start=False, stop=True).then_inc(R.placed, 1)

    def open_spread(self, ch):
        R = self.R
        self.pe.wait_ge(R.merged, (ch + 1) * R.n_merge + MASKS)
        for q in range(2):
            self.empty(R.pp[q][:, 0:R.tiles], True)

    def spread(self, ch, g, n, k):
        R, m = self.R, self.R.parts
        self.pe.wait_ge(R.hots, g + (ch * R.n_group + 1))
        if not ch and k in R.helpers:
            self.pe.wait_ge(R.helpers[k], g + (2 * R.ring - k))
        for j in range(n):
            for q in range(2):
                last = self.nc.tensor.matmul(R.pp[q][:, 0:R.tiles], R.to_slot[0:m, k, j, q, :],
                                             R.to_tile[0:m, k, j, :], start=False, stop=False)
        last.then_inc(R.hot_used, 1)

    def close_spread(self):
        for q in range(2):
            last = self.empty(self.R.pp[q][:, 0:self.R.tiles], False)
        last.then_inc(self.R.done, 1)


BINS_COUNTED = 7
BINS_MERGED = 2
assert RING * BINS_COUNTED % MASKS == 0 and RING * BINS_MERGED % MASKS == 0
ACT_SLOT = 3
R_RING = 4
COUNT_ROUNDS = -(-NBLK // (BINS_COUNTED * RING))
MERGE_ROUNDS = -(-NBLK // (BINS_MERGED * RING))
SPREAD_ROUNDS = CC // (UNIT * RING)
SORT_ROUNDS = COUNT_ROUNDS + 1 + MERGE_ROUNDS + SPREAD_ROUNDS
assert CC == SPREAD_ROUNDS * UNIT * RING and SORT_ROUNDS < ROUNDS and RING == 4


def beside(eng, first, unit, steps, ch):
    def loop(a, n, step):
        start = first + a

        def one_round(i):
            for q in range(RING):
                u = i * RING + (q - start * RING)
                for g in range(UNIT):
                    step(u, q, g)
                    if unit:
                        unit(i * RING + q, q, g)
        peeled = 1 if unit and not a else 0
        if peeled:
            one_round(start)
        with eng.Fori(start + peeled, start + n) as i:
            one_round(i)
        return a + n

    def share(bins, g):
        return range(g * -(-bins // UNIT), min(bins, (g + 1) * -(-bins // UNIT)))

    def count(u, q, g):
        for j in share(BINS_COUNTED, g):
            steps.count(ch, u * BINS_COUNTED + j, (q * BINS_COUNTED + j) % MASKS)

    def merge(u, q, g):
        for j in share(BINS_MERGED, g):
            steps.merge(ch, u * BINS_MERGED + j, (q * BINS_MERGED + j) % MASKS)
    steps.begin(ch)
    a = loop(0, COUNT_ROUNDS, count)
    for q in range(RING):
        steps.bases(ch, q)
        for g in range(UNIT if unit else 0):
            unit((first + a) * RING + q, q, g)
    a += 1
    a = loop(a, MERGE_ROUNDS, merge)
    steps.slots(ch)
    a = loop(a, SPREAD_ROUNDS, lambda u, q, g: steps.spread(ch, u * UNIT + g, 1, (q * UNIT + g) % R_RING))
    steps.end(ch)
    if unit and a < ROUNDS:
        loop(a, ROUNDS - a, lambda u, q, g: None)


def aggregate(nc, A, T, acc, s):
    ctx = ExitStack()
    with ctx:
        def sb(name, shape, dt=F32):
            return ctx.enter_context(nc.sbuf_tensor(name, shape, dt))
        NCH = 2 * CHUNKS
        UNITS = ROUNDS * RING
        ends = [sb(f"ends{d}", [P, CC], I32) for d in range(2)]
        R = Sort(nc, ctx, s, "e", EP, CC, NBLK, ETILES, BINS_COUNTED * RING * COUNT_ROUNDS,
                 BINS_MERGED * RING * MERGE_ROUNDS, 1, CC, R_RING, UNIT, (ACT_SLOT,))
        table = sb("table", [1, 2, ETILES], I32)
        other = sb("other", [P, 2, ETILES], I32)
        minus = sb("minus", [P, 2, ETILES])
        rows = sb("rows", [P, RING, UNIT, SPLIT], F32R)
        idx_st = sb("idx_st", [P, RING, UNIT], I32)
        apart = sb("apart", [P, 2, UNIT, P])
        hot = sb("hot", [P, 2, UNIT, P], F32R)
        one = sb("g_one", [P, 1])
        ps = ctx.enter_context(nc.psum_tensor("gps", [P, 2, 512], F32))
        block = ctx.enter_context(nc.Block())
        keyed, off_ok = s("g_keyed"), s("g_off")
        ends_in, decoded, idx_ok, apart_ok, hot_ok, pe_done, added, cleared, chain = (
            s(f"g_{n}") for n in ("ends", "decoded", "idx", "apart", "hot", "pe", "added", "cleared", "chain"))
        got = [s(f"g_got{q}") for q in range(RING)]

        @block.sync
        def _(sp):
            for ch in range(NCH):
                if ch:
                    sp.wait_ge(keyed, ch)
                cols = slice((ch % CHUNKS) * CC, (ch % CHUNKS + 1) * CC)
                for t, a in zip(ends, (A.dst, A.src) if ch < CHUNKS else (A.src, A.dst)):
                    sp.dma_start(t[0:EP, :], a.rearrange("(p c) -> p c", p=EP)[:, cols]).then_inc(ends_in, 16)
            sp.wait_ge(ends_in, 32 * NCH)

        @block.gpsimd
        def _(pool):
            half = NBLK * ACOLS
            nc.gpsimd.memset(acc[:, 0:half], 0.0).then_inc(cleared, 1)
            nc.gpsimd.memset(acc[:, half:], 0.0).then_inc(cleared, 1)
            with pool.Fori(0, NCH * ROUNDS) as i:
                for q in range(RING):
                    n = i * RING + q
                    T.gate_pool.wait(pool, idx_ok, n + 1)
                    T.gate_pool.wait(pool, pe_done, n + 1)
                    for g in range(UNIT):
                        nc.gpsimd.indirect_dma_start(
                            out=rows[:, q, g, :].bitcast(F32), out_offset=None, in_=A.split_dram[:, :],
                            in_offset=bass.IndirectOffsetOnAxis(ap=idx_st[:, q, g:g + 1], axis=0)).then_inc(got[q], 16)

        @block.scalar
        def _(act):
            act.wait_ge(cleared, 3)
            act.wait_ge(R.slots_ok, 1)
            off = apart[0:EP, :, :, :].rearrange("p a b c -> p (a b c)")[:, 0:ETILES]
            with act.Fori(0, CC // R_RING) as i:
                g = i * R_RING + ACT_SLOT
                act.wait_ge(R.helpers[ACT_SLOT], i * R_RING + R_RING)
                nc.scalar.activation(off, T.ramp16[0:EP, 0:ETILES], ACT.Square, bias=R.col[0:EP, bass.ds(g, 1)],
                                     scale=-1.0).then_inc(off_ok, 1)
                act.wait_ge(off_ok, i + 1)
                act.wait_ge(R.hot_used, g + 1)
                nc.scalar.activation(R.to_tile[0:EP, ACT_SLOT, 0, :], off, ACT.Relu, bias=one[0:EP, :],
                                     scale=-1.0).then_inc(R.helpers[ACT_SLOT], R_RING)
            act.wait_ge(R.helpers[ACT_SLOT], CC + R_RING)
            act.wait_ge(decoded, 1)
            nc.scalar.copy(idx_st[:, :, :], other[:, 0, 0:RING * UNIT].rearrange("p (a b) -> p a b", a=RING)).then_inc(idx_ok, RING)

            def stage(i, q, src):
                act.wait_ge(got[q], i * (UNIT * 16) + UNIT * 16)
                nc.scalar.copy(idx_st[:, q, :], src).then_inc(idx_ok, 1)

            def one_hot(ch, n, q):
                act.wait_ge(pe_done, n + (RING - 1))
                for g in range(UNIT):
                    t = n * UNIT + (g - ch * ETILES)
                    last = nc.scalar.activation(apart[:, q % 2, g, :], T.ramp32[:, :], ACT.Square,
                                                bias=minus[:, ch % 2, bass.ds(t, 1)])
                last.then_inc(apart_ok, 1)
                act.wait_ge(apart_ok, n + 1)
                nc.scalar.activation(hot[:, q % 2, :, :], apart[:, q % 2, :, :], ACT.Relu, bias=one[:, :],
                                     scale=-1.0).then_inc(hot_ok, 1)

            for ch in range(NCH):
                with act.Fori(ch * ROUNDS, (ch + 1) * ROUNDS - 1) as i:
                    for q in range(RING):
                        n = i * RING + q
                        one_hot(ch, n, q)
                        t = (n + RING) * UNIT - ch * ETILES
                        stage(i, q, other[:, ch % 2, bass.ds(t, UNIT)])
                i = (ch + 1) * ROUNDS - 1
                if ch + 1 < NCH:
                    act.wait_ge(decoded, ch + 2)
                for q in range(RING):
                    one_hot(ch, i * RING + q, q)
                    if ch + 1 < NCH:
                        stage(i, q, other[:, 1 - ch % 2, q * UNIT:(q + 1) * UNIT])

        @block.vector
        def _(dve):
            c = Count(chain)
            nc.vector.memset(one[:, :], 1.0).then_inc(cleared, 1)
            sort = SortDVE(nc, dve, T, R)
            dve.sem_inc(pe_done, RING)
            dve.sem_inc(added, 2)

            class Steps:
                count, merge, slots, spread = sort.count, sort.merge, sort.slots, sort.spread

                @staticmethod
                def begin(ch):
                    dve.wait_ge(ends_in, 32 * (ch + 1))
                    tgt, oth = ends[0][0:EP, :], ends[1][0:EP, :]
                    u, v = R.slot_i[0:EP, :], R.tile_i[0:EP, :]
                    c.after(dve, nc.vector.tensor_scalar(u, tgt, 7, None, ALU.arith_shift_right))
                    c.after(dve, nc.vector.tensor_copy(R.key[0:EP, :], u))
                    c.after(dve, nc.vector.tensor_scalar(u, oth, (1 << LOW) - 1, None, ALU.bitwise_and))
                    c.after(dve, nc.vector.tensor_copy(R.part0[0:EP], u))
                    c.after(dve, nc.vector.tensor_scalar(u, tgt, P - 1, 2, ALU.bitwise_and, ALU.logical_shift_left))
                    c.after(dve, nc.vector.tensor_scalar(v, oth, LOW, None, ALU.arith_shift_right))
                    c.after(dve, nc.vector.tensor_tensor(u, u, v, ALU.bitwise_or))
                    c.after(dve, nc.vector.tensor_scalar(R.part1[0:EP], u, 4.0 * P, None, ALU.add))
                    dve.sem_inc(keyed, 1)

                @staticmethod
                def bases(ch, j):
                    sort.bases(ch, j, table[0:1, ch % 2, :], (ch // CHUNKS) * NBLK)

                @staticmethod
                def end(ch):
                    u, v = minus[:, ch % 2, :].bitcast(I32), other[:, ch % 2, :]
                    dve.wait_ge(R.done, ch + 1)
                    if ch >= 2:
                        dve.wait_ge(idx_ok, (ch - 1) * UNITS + RING)
                        dve.wait_ge(hot_ok, (ch - 1) * UNITS)
                    c.after(dve, nc.vector.tensor_copy(u, R.pp[1][:, 0:ETILES]))
                    c.after(dve, nc.vector.tensor_scalar(v, u, 3, None, ALU.bitwise_and))
                    c.after(dve, nc.vector.scalar_tensor_tensor(
                        out=other[:, ch % 2, :], in0=v, scalar=float(1 << LOW), in1=R.pp[0][:, 0:ETILES],
                        op0=ALU.mult, op1=ALU.add))
                    c.after(dve, nc.vector.tensor_scalar(u, u, 2, None, ALU.arith_shift_right))
                    nc.vector.tensor_scalar(minus[:, ch % 2, :], u, -1.0, float(P), ALU.mult, ALU.add).then_inc(decoded, 1)
                    dve.wait_ge(decoded, ch + 1)

            def adder(ch):
                def add(n, q):
                    _, blk = nc.values_load_multi_w_load_instructions(
                        table[0:1, ch % 2, bass.ds(n * UNIT - ch * ETILES, 1)], engines=(mybir.EngineType.DVE,),
                        min_val=0, max_val=2 * NBLK - 1,
                        skip_runtime_bounds_check_because="the table's values are clamped when it is made")
                    dve.wait_ge(pe_done, n + (RING + 1))
                    dve.wait_ge(added, n + 2)
                    a = acc[:, bass.ds(blk[0] * ACOLS, ACOLS)]
                    nc.vector.tensor_tensor(a, a, ps[:, q % 2, 0:ACOLS], ALU.add).then_inc(added, 1)

                def lagged(n, q, g):
                    if not g and behind(n, ch * UNITS + 1):
                        add(n - 1, (q - 1) % RING)
                return lagged, lambda: add((ch + 1) * UNITS - 1, RING - 1)
            beside(dve, 0, None, Steps, 0)
            dve.wait_ge(cleared, 3)
            for ch in range(NCH - 1):
                lagged, last_add = adder(ch)
                beside(dve, ch * ROUNDS, lagged, Steps, ch + 1)
                last_add()
            lagged, last_add = adder(NCH - 1)
            for q in range(RING):
                lagged((NCH - 1) * UNITS + q, q, 0)
            with dve.Fori((NCH - 1) * ROUNDS + 1, NCH * ROUNDS) as i:
                for q in range(RING):
                    lagged(i * RING + q, q, 0)
            last_add()

        @block.tensor
        def _(pe):
            sort = SortPE(nc, pe, T, R)

            class Steps:
                count, merge, bases, spread = sort.count, sort.merge, sort.bases, sort.spread
                slots = sort.open_spread

                @staticmethod
                def begin(ch):
                    sort.open_count()

                @staticmethod
                def end(ch):
                    sort.close_spread()

            def total(n, q, g):
                if g:
                    return
                pe.wait_ge(hot_ok, n + 1)
                pe.wait_ge(got[q], n * (UNIT * 16 // RING) + (RING - q) * (UNIT * 16 // RING))
                pe.wait_ge(added, n + 1)
                for g in range(UNIT):
                    w = hot[:, q % 2, g, :]
                    nc.tensor.matmul(ps[:, q % 2, 0:ACOLS], w, rows[:, q, g, 0:ACOLS], start=g == 0, stop=False)
                    last = nc.tensor.matmul(ps[:, q % 2, 0:D], w, rows[:, q, g, ACOLS:], start=False, stop=g == UNIT - 1)
                last.then_inc(pe_done, 1)
            beside(pe, 0, None, Steps, 0)
            for ch in range(NCH - 1):
                beside(pe, ch * ROUNDS, total, Steps, ch + 1)
            with pe.Fori((NCH - 1) * ROUNDS, NCH * ROUNDS) as i:
                for q in range(RING):
                    total(i * RING + q, q, 0)


def update(nc, A, T, W, acc, s):
    ctx = ExitStack()
    with ctx:
        def sb(name, shape, dt=F32):
            return ctx.enter_context(nc.sbuf_tensor(name, shape, dt))
        rc = sb("rc", [P, 2 * NBLK])
        aux = sb("auxv", [P, NBLK, 6])
        aux_st = sb("aux_st", [P, 2, 6])
        ag = sb("ag", [P, 2, 2, D])
        xn = sb("uxn", [P, 4, D])
        parts = sb("uparts", [P, 4, SPLIT])
        x0 = sb("ux0", [P, 4, D])
        thi = sb("thi", [P, 2, 7, P], F32R)
        tlo = sb("tlo", [P, 2, 6, P], F32R)
        rz = sb("rz", [P, 2, 2 * D])
        nn = sb("nn", [P, 2, D])
        x1 = sb("ux1", [P, 2, D])
        st2 = sb("st2", [P, NBLK, 6])
        pt = ctx.enter_context(nc.psum_tensor("upt", [P, 2, 512], F32))
        po = ctx.enter_context(nc.psum_tensor("upo", [P, 2, 3, 512], F32))
        acc_v = acc[:, :].rearrange("p (d b c) -> p d b c", d=2, b=NBLK)
        block = ctx.enter_context(nc.Block())
        chain, mean_ok, tr_ok, hi_ok, lo_ok, gates, sig_ok, pre_ok, tanh_ok, x1_ok = (
            s(n) for n in ("u_chain", "u_mean", "u_tr", "u_hi", "u_lo", "u_gates", "u_sig",
                           "u_pre", "u_tanh", "u_x1"))
        rows_in = [s(f"u_rows{k}") for k in range(4)]
        x1_out = [s(f"u_out{k}") for k in range(2)]
        dchain, st_ok = s("u_dchain"), s("u_stats")

        @block.sync
        def _(sp):
            def load(b, k):
                sp.dma_start(parts[:, k, :], A.split_dram[bass.ds(b * P, P), :]).then_inc(rows_in[k], 16)
                n = TAIL if isinstance(b, int) and b == NBLK - 1 else P
                sp.dma_start(x0[0:n, k, :], A.x[bass.ds(b * P, n), :]).then_inc(rows_in[k], 16)

            def store(b, k):
                sp.wait_ge(x1_ok, b + 3)
                sp.dma_start(A.x1_dram[bass.ds(b * P, P), :], x1[:, k % 2, :]).then_inc(x1_out[k % 2], 16)
            for b in range(4):
                load(b, b)
            with sp.Fori(0, (NBLK - 4) // 4) as j:
                for k in range(4):
                    store(j * 4 + k, k)
                    load(j * 4 + (k + 4), k)
            for b in range((NBLK - 4) // 4 * 4, NBLK):
                store(b, b % 4)
                if b + 4 < NBLK:
                    load(b + 4, b % 4)
            sp.wait_ge(x1_out[0], 16 * (NBLK - NBLK // 2))
            sp.wait_ge(x1_out[1], 16 * (NBLK // 2))

        @block.scalar
        def _(act):
            def split(b, k):
                act.wait_ge(tr_ok, b + 3)
                act.wait_ge(gates, b + 1)
                nc.scalar.copy(thi[:, k, 0:4, :].rearrange("p a b -> p (a b)"), pt[:, 0, :])
                nc.scalar.copy(thi[:, k, 4:6, :].rearrange("p a b -> p (a b)"), pt[:, 1, 0:2 * P])
                nc.scalar.copy(thi[0:6, k, 6, :], pt[0:6, 1, 2 * P:3 * P]).then_inc(hi_ok, 1)

            def gate(b, k):
                act.wait_ge(gates, b + 3)
                nc.scalar.activation(rz[:, k, :], po[:, k, 0, :], ACT.Sigmoid).then_inc(sig_ok, 1)
                act.wait_ge(pre_ok, b + 1)
                nc.scalar.activation(nn[:, k, :], nn[:, k, :], ACT.Tanh).then_inc(tanh_ok, 1)
            split(0, 0)
            split(1, 1)

            def step(b, k):
                gate(b, k)
                split(b + 2, k)
            with act.Fori(0, (NBLK - 2) // 2) as j:
                for k in range(2):
                    step(j * 2 + k, k)
            step(NBLK - 3, (NBLK - 3) % 2)
            gate(NBLK - 2, (NBLK - 2) % 2)
            gate(NBLK - 1, (NBLK - 1) % 2)

        @block.vector
        def _(dve):
            c = Count(chain)
            cnt = acc_v[:, :, :, D]
            rcv = rc[:, :].rearrange("p (d b) -> p d b", d=2)
            c.after(dve, nc.vector.tensor_scalar(rcv, cnt, 1.0, None, ALU.max))
            c.after(dve, nc.vector.memset(aux[:, :, 0:2], 1.0))
            for d in range(2):
                for j in range(2):
                    c.after(dve, nc.vector.tensor_scalar(aux[:, :, 2 + 2 * d + j], acc_v[:, d, :, D], 1.0, None, ALU.min))
            c.after(dve, nc.vector.reciprocal(rc[:, :], rc[:, :]))
            for sem in (x1_ok, tr_ok, gates):
                dve.sem_inc(sem, 2)
            dve.sem_inc(lo_ok, 1)

            def means(b, k):
                dve.wait_ge(rows_in[k], (b - k) * 8 + 32)
                nc.vector.tensor_tensor(xn[:, k, :], parts[:, k, 0:D], parts[:, k, ACOLS:], ALU.add).then_inc(mean_ok, 1)
                dve.wait_ge(tr_ok, b + 1)
                for d in range(2):
                    nc.vector.tensor_scalar(ag[:, k % 2, d, :], acc_v[:, d, bass.ds(b, 1), 0:D].rearrange("p o f -> p (o f)"),
                                            rc[:, bass.ds(b + d * NBLK, 1)], None, ALU.mult).then_inc(mean_ok, 1)
                nc.vector.tensor_copy(aux_st[:, k % 2, :], aux[:, bass.ds(b, 1), :].rearrange("p o f -> p (o f)")).then_inc(mean_ok, 1)

            def low(b, k):
                dve.wait_ge(hi_ok, b + 1)
                nc.vector.tensor_tensor(tlo[:, k, 0:4, :].rearrange("p a b -> p (a b)"), pt[:, 0, :],
                                        thi[:, k, 0:4, :].rearrange("p a b -> p (a b)").bitcast(F32), ALU.subtract)
                nc.vector.tensor_tensor(tlo[:, k, 4:6, :].rearrange("p a b -> p (a b)"), pt[:, 1, 0:2 * P],
                                        thi[:, k, 4:6, :].rearrange("p a b -> p (a b)").bitcast(F32),
                                        ALU.subtract).then_inc(lo_ok, 1)

            def before_tanh(b, k):
                n = nn[:, k % 2, :]
                dve.wait_ge(sig_ok, b + 1)
                nc.vector.tensor_tensor(n, rz[:, k % 2, 0:D], po[:, k % 2, 2, 0:D], ALU.mult).then_inc(dchain, 1)
                dve.wait_ge(dchain, b * 4 + 1)
                nc.vector.tensor_tensor(n, n, po[:, k % 2, 1, 0:D], ALU.add).then_inc(pre_ok, 1)

            def after_tanh(b, k):
                n = nn[:, k % 2, :]
                z = rz[:, k % 2, D:2 * D]
                dve.wait_ge(tanh_ok, b + 1)
                nc.vector.tensor_tensor(n, n, xn[:, k, :], ALU.subtract).then_inc(dchain, 1)
                dve.wait_ge(dchain, b * 4 + 2)
                nc.vector.tensor_tensor(n, n, z, ALU.mult)
                nc.vector.tensor_tensor(xn[:, k, :], xn[:, k, :], x0[:, k, :], ALU.add).then_inc(dchain, 1)
                dve.wait_ge(dchain, b * 4 + 3)
                nc.vector.tensor_tensor(n, n, xn[:, k, :], ALU.add).then_inc(dchain, 1)
                dve.wait_ge(dchain, b * 4 + 4)
                if behind(b, 2):
                    dve.wait_ge(x1_out[k % 2], (b - k % 2) * 8)
                y = x1[:, k % 2, :]
                nc.vector.tensor_tensor(y, n, po[:, k % 2, 2, D:2 * D], ALU.add).then_inc(x1_ok, 1)
                T.gate_dve.wait(dve, x1_ok, b + 3)
                nc.vector.tensor_copy(acc_v[:, 0, bass.ds(b, 1), 0:D].rearrange("p o f -> p (o f)"), y)
                nc.vector.bn_stats(st2[:, bass.ds(b, 1), :].rearrange("p o f -> p (o f)"), y).then_inc(st_ok, 1)
            means(0, 0)
            means(1, 1)
            low(0, 0)
            means(2, 2)
            low(1, 1)

            def step(b, k):
                before_tanh(b, k)
                if not isinstance(b, int) or b + 3 < NBLK:
                    means(b + 3, (k + 3) % 4)
                if not isinstance(b, int) or b + 2 < NBLK:
                    low(b + 2, k % 2)
                after_tanh(b, k)
            for b in range(4):
                step(b, b)
            with dve.Fori(1, (NBLK - 3) // 4) as j:
                for k in range(4):
                    step(j * 4 + k, k)
            for b in range((NBLK - 3) // 4 * 4, NBLK):
                step(b, b % 4)
            dve.wait_ge(st_ok, NBLK)
            rstd_steps(nc, dve, c, st2, T.mean2[:, :], T.rstd2[:, :], T.tmp2[:, :])

        @block.tensor
        def _(pe):
            def transposes(b, k):
                pe.wait_ge(mean_ok, b * 4 + 4)
                pe.wait_ge(lo_ok, b + 1)
                for q in range(6):
                    src = (ag[:, k % 2, q // 2, :] if q < 4 else xn[:, k, :])[:, (q % 2) * P:(q % 2 + 1) * P]
                    nc.tensor.transpose(pt[:, q // 4, (q % 4) * P:(q % 4 + 1) * P], src, T.ident[:, :])
                nc.tensor.matmul(pt[0:6, 1, 2 * P:3 * P], aux_st[:, k % 2, :], T.ident[:, :], start=True, stop=True).then_inc(tr_ok, 1)

            def products(b, k):
                pe.wait_ge(lo_ok, b + 2)
                pe.wait_ge(x1_ok, b + 1)
                for o, c0, c1, p0, p1 in ((0, 0, 2 * D, 0, 6), (1, 2 * D, 3 * D, 0, 4), (2, 3 * D, 5 * D, 4, 6)):
                    out = po[:, k, o, 0:c1 - c0]
                    nc.tensor.matmul(out, thi[0:6, k, 6, :], W.aux[:, c0:c1], start=True, stop=False)
                    for q in range(p0, p1):
                        nc.tensor.matmul(out, thi[:, k, q, :], part(W.hi, o, q), start=False, stop=False)
                        nc.tensor.matmul(out, thi[:, k, q, :], part(W.lo, o, q), start=False, stop=False)
                        last = nc.tensor.matmul(out, tlo[:, k, q, :], part(W.hi, o, q), start=False, stop=q == p1 - 1)
                last.then_inc(gates, 1)
            transposes(0, 0)
            transposes(1, 1)

            def step(b, k):
                products(b, k % 2)
                if not isinstance(b, int) or b + 2 < NBLK:
                    transposes(b + 2, (k + 2) % 4)
            with pe.Fori(0, (NBLK - 2) // 4) as j:
                for k in range(4):
                    step(j * 4 + k, k)
            for b in range((NBLK - 2) // 4 * 4, NBLK):
                step(b, b % 4)


def route(nc, A, T, acc, s):
    ctx = ExitStack()
    with ctx:
        def sb(name, shape, dt=F32):
            return ctx.enter_context(nc.sbuf_tensor(name, shape, dt))
        SLOTS = 4
        x2 = sb("x2", [P, SLOTS, D])
        x2t = sb("x2t", [P, 2, 2, P])
        wg = sb("wg", [P, 2, NEXP])
        bg = sb("bg", [1, NEXP])
        one = sb("one", [1, P])
        score = sb("score", [P, NBLK, NEXP])
        other = sb("r_other", [P, NBLK, NEXP])
        best = sb("best", [P, NBLK])
        pt = ctx.enter_context(nc.psum_tensor("rpt", [P, 2, 512], F32))
        bias = sb("r_bias", [P, NEXP])
        pg = ctx.enter_context(nc.psum_tensor("rpg", [P, (NBLK + 1) * NEXP], F32))
        acc_v = acc[:, :].rearrange("p (d b c) -> p d b c", d=2, b=NBLK)
        block = ctx.enter_context(nc.Block())
        w_in, sd_ok, chain, x2_ok, tr_ok, t_ok, sc_ok, one_ok = (
            s(n) for n in ("r_w", "r_sd", "r_chain", "r_x2", "r_tr", "r_t", "r_sc", "r_one"))
        x2_out = [s(f"r_out{k}") for k in range(SLOTS)]

        @block.sync
        def _(sp):
            sp.dma_start(wg[:, :, :], A.wg.rearrange("(c p) n -> p c n", p=P)).then_inc(w_in, 16)
            sp.dma_start(bg[:, :], A.bg.rearrange("(o n) -> o n", o=1)).then_inc(w_in, 16)

            def store(b, k):
                sp.wait_ge(x2_ok, b + 1)
                sp.dma_start(A.x2_dram[bass.ds(b * P, P), :], x2[:, k, :]).then_inc(x2_out[k], 16)
            cycle(NBLK, SLOTS, sp, store)
            for k in range(SLOTS):
                sp.wait_ge(x2_out[k], 16 * len(range(k, NBLK, SLOTS)))

        @block.scalar
        def _(act):
            nc.scalar.activation(T.tmp2[:, :], T.rstd2[:, :], ACT.Sqrt).then_inc(sd_ok, 1)

            def out(b, k):
                act.wait_ge(tr_ok, b + (SLOTS + 1))
                act.wait_ge(sc_ok, b + 1)
                nc.scalar.copy(x2t[:, k, :, :].rearrange("p a b -> p (a b)"), pt[:, k, 0:2 * P]).then_inc(t_ok, 1)
            pairs(NBLK, act, out)

        @block.vector
        def _(dve):
            c = Count(chain)
            nc.vector.memset(one[:, :], 1.0).then_inc(one_ok, 1)
            for sem, ahead in ((tr_ok, SLOTS), (t_ok, 2), (sc_ok, 2)):
                dve.sem_inc(sem, ahead)
            dve.wait_ge(sd_ok, 1)
            c.after(dve, nc.vector.reciprocal(T.rstd2[:, :], T.tmp2[:, :]))

            def norm(b, k):
                if behind(b, SLOTS):
                    dve.wait_ge(x2_out[k], (b - k) * (16 // SLOTS))
                dve.wait_ge(tr_ok, b + 1)
                nc.vector.tensor_scalar(x2[:, k, :], acc_v[:, 0, bass.ds(b, 1), 0:D].rearrange("p o f -> p (o f)"),
                                        T.mean2[:, bass.ds(b, 1)], T.rstd2[:, bass.ds(b, 1)],
                                        ALU.subtract, ALU.mult).then_inc(x2_ok, 1)
            for b in range(SLOTS):
                norm(b, b)
            cycle(NBLK, SLOTS, dve, norm, first=SLOTS)

            dve.wait_ge(sc_ok, NBLK + 2)
            c.after(dve, nc.vector.tensor_copy(score[:, :, :].rearrange("p b e -> p (b e)"), pg[:, 0:NBLK * NEXP]))
            c.after(dve, nc.vector.tensor_copy(bias[:, :], pg[:, NBLK * NEXP:]))
            c.after(dve, nc.vector.tensor_tensor(score[:, :, :], score[:, :, :],
                                                 bias[:, :].unsqueeze(1).to_broadcast([P, NBLK, NEXP]), ALU.add))
            number = T.ramp32[:, 0:NEXP].unsqueeze(1).to_broadcast([P, NBLK, NEXP])

            def each(t):
                return t.unsqueeze(2).to_broadcast([P, NBLK, NEXP])
            for j in range(2):
                found = T.expert[:, j * NBLK:(j + 1) * NBLK]
                c.after(dve, nc.vector.tensor_reduce(best[:, :], score[:, :, :], AX.X, ALU.max))
                c.after(dve, nc.vector.tensor_tensor(other[:, :, :], score[:, :, :], each(best[:, :]), ALU.is_equal))
                c.after(dve, nc.vector.tensor_scalar(other[:, :, :], other[:, :, :], -float(NEXP), float(NEXP),
                                                     ALU.mult, ALU.add))
                c.after(dve, nc.vector.tensor_tensor(other[:, :, :], other[:, :, :], number, ALU.add))
                c.after(dve, nc.vector.tensor_reduce(found, other[:, :, :], AX.X, ALU.min))
                if not j:
                    c.after(dve, nc.vector.tensor_tensor(other[:, :, :], number, each(found), ALU.is_equal))
                    c.after(dve, nc.vector.scalar_tensor_tensor(
                        out=score[:, :, :], in0=other[:, :, :], scalar=-3e38, in1=score[:, :, :],
                        op0=ALU.mult, op1=ALU.add))

        @block.tensor
        def _(pe):
            pe.wait_ge(w_in, 32)
            pe.wait_ge(one_ok, 1)
            nc.tensor.matmul(pg[:, NBLK * NEXP:], one[:, :], bg[:, :], start=True, stop=True)

            def turn(b, k):
                pe.wait_ge(x2_ok, b + 1)
                pe.wait_ge(t_ok, b + 1)
                for q in range(2):
                    last = nc.tensor.transpose(pt[:, k % 2, q * P:(q + 1) * P], x2[:, k, q * P:(q + 1) * P], T.ident[:, :])
                last.then_inc(tr_ok, 1)

            def gate(b, k):
                pe.wait_ge(t_ok, b + 3)
                out = pg[:, bass.ds(b * NEXP, NEXP)]
                for q in range(2):
                    last = nc.tensor.matmul(out, x2t[:, k % 2, q, :], wg[:, q, :], start=q == 0, stop=q == 1)
                last.then_inc(sc_ok, 1)
            turn(0, 0)

            def step(b, k):
                turn(b + 1, (k + 1) % SLOTS)
                gate(b, k)
            cycle(NBLK - 1, SLOTS, pe, step)
            gate(NBLK - 1, (NBLK - 1) % SLOTS)


class ExpertWeights:

    def __init__(self, nc, ctx, s):
        def sb(name, shape, dt=F32):
            return ctx.enter_context(nc.sbuf_tensor(name, shape, dt))
        self.w1 = [sb(f"w1{n}", [P, NEXP * KD * HID], F32R) for n in "hl"]
        self.w2 = [sb(f"w2{n}", [P, NEXP * KH * D], F32R) for n in "hl"]
        self.b1 = sb("b1", [2, NEXP * HID], F32R)
        self.b2 = sb("b2", [2, NEXP * D], F32R)
        self.twos = sb("twos", [2, P], F32R)
        self.raw_in = [s(f"e_raw{k}") for k in range(RAWS)]
        self.b_in, self.whi, self.wlo, self.b_hi, self.b_lo, self.b_out, self.ones_ok = (
            s(f"e_{n}") for n in ("bin", "whi", "wlo", "bhi", "blo", "bout", "ones"))

    def buffers(self, nc, ctx):
        def sb(name, shape, dt=F32):
            return ctx.enter_context(nc.sbuf_tensor(name, shape, dt))
        self.raw = sb("raw", [P, RAWS, KD * HID])
        self.braw = sb("braw", [NEXP, HID + D])
        self.bhi = sb("bhi", [NEXP, HID + D], F32R)
        self.blo = sb("blo", [NEXP, HID + D], F32R)

    def part(self, n, m):
        e, second = divmod(n, 2)
        return (self.w2 if second else self.w1)[m][:, e * KD * HID:(e + 1) * KD * HID]

    def load(self, sp, A):
        sp.dma_start(self.braw[:, 0:HID], A.b1).then_inc(self.b_in, 16)
        sp.dma_start(self.braw[:, HID:], A.b2).then_inc(self.b_in, 16)
        for n in range(2 * NEXP):
            e, second = divmod(n, 2)
            if n >= RAWS:
                sp.wait_ge(self.wlo, n - RAWS + 1)
            src = (A.w2 if second else A.w1)[e, :, :].rearrange("(c p) n -> p c n", p=P)
            sp.dma_start(self.raw[:, n % RAWS, :].rearrange("p (c n) -> p c n", c=KH if second else KD),
                         src).then_inc(self.raw_in[n % RAWS], 16)
            if n == 1:
                sp.wait_ge(self.b_lo, 1)
                for r, t in enumerate((self.bhi, self.blo)):
                    for x in range(NEXP):
                        sp.dma_start(self.b1[r:r + 1, x * HID:(x + 1) * HID].bitcast(F32),
                                     t[x:x + 1, 0:HID].bitcast(F32)).then_inc(self.b_out, 16)
                        sp.dma_start(self.b2[r:r + 1, x * D:(x + 1) * D].bitcast(F32),
                                     t[x:x + 1, HID:].bitcast(F32)).then_inc(self.b_out, 16)
        sp.wait_ge(self.b_out, 16 * 4 * NEXP)

    def high(self, nc, act):
        act.wait_ge(self.b_in, 32)
        nc.scalar.copy(self.bhi[:, :], self.braw[:, :]).then_inc(self.b_hi, 1)
        for n in range(2 * NEXP):
            act.wait_ge(self.raw_in[n % RAWS], 16 * (n // RAWS + 1))
            nc.scalar.copy(self.part(n, 0), self.raw[:, n % RAWS, :]).then_inc(self.whi, 1)

    def low(self, nc, pool, T):
        nc.gpsimd.tensor_scalar(self.twos[:, :], T.ident[0:2, :], 0.0, 1.0, ALU.mult, ALU.add).then_inc(self.ones_ok, 1)
        pool.wait_ge(self.b_hi, 1)
        nc.gpsimd.tensor_tensor(self.blo[:, :], self.braw[:, :], self.bhi[:, :].bitcast(F32),
                                ALU.subtract).then_inc(self.b_lo, 1)
        for n in range(2 * NEXP):
            pool.wait_ge(self.whi, n + 1)
            nc.gpsimd.tensor_tensor(self.part(n, 1), self.raw[:, n % RAWS, :], self.part(n, 0).bitcast(F32),
                                    ALU.subtract).then_inc(self.wlo, 1)


def sort_tokens(nc, A, T, E, s):
    ctx = ExitStack()
    with ctx:
        def sb(name, shape, dt=F32):
            return ctx.enter_context(nc.sbuf_tensor(name, shape, dt))
        token = sb("token", [P, 2 * NBLK], I32)
        high = sb("high", [P, 2 * NBLK], I32)
        low_part = sb("low_part", [P, XTILES])
        PERX = 7
        R = Sort(nc, ctx, s, "x", P, 2 * NBLK, NEXP, XTILES, NEXP, NEXP, PERX, 2 * NBLK // PERX)
        E.buffers(nc, ctx)
        block = ctx.enter_context(nc.Block())
        tok_ok, chain = s("x_tok"), s("x_ch")

        @block.sync
        def _(sp):
            E.load(sp, A)

        @block.scalar
        def _(act):
            E.high(nc, act)

        @block.gpsimd
        def _(pool):
            nc.gpsimd.iota(token[:, :], pattern=[[0, 2], [P, NBLK]], base=0, channel_multiplier=1).then_inc(tok_ok, 1)
            E.low(nc, pool, T)

        @block.vector
        def _(dve):
            c = Count(chain)
            sort = SortDVE(nc, dve, T, R)
            nc.vector.memset(T.tokens[:, XTILES:], 0)
            c.after(dve, nc.vector.tensor_copy(R.key[:, :], T.expert[:, :]))
            cycle(NEXP, MASKS, dve, lambda b, k: sort.count(0, b, k))
            dve.wait_ge(tok_ok, 1)
            c.after(dve, nc.vector.tensor_scalar(high[:, :], token[:, :], LOW, None, ALU.arith_shift_right))
            c.after(dve, nc.vector.tensor_copy(R.part1, high[:, :]))
            c.after(dve, nc.vector.tensor_scalar(token[:, :], token[:, :], (1 << LOW) - 1, None, ALU.bitwise_and))
            c.after(dve, nc.vector.tensor_copy(R.part0, token[:, :]))
            for j in range(4):
                sort.bases(0, j, T.xtable[0:1, 0:XTILES], 0)
            cycle(NEXP, MASKS, dve, lambda b, k: sort.merge(0, b, k))
            sort.slots(0)
            c.after(dve, nc.vector.tensor_copy(T.slot_of[:, :], R.slot_i[:, :]))
            pairs(R.n_group, dve, lambda g, k: sort.spread(0, g, PERX, k))
            dve.wait_ge(R.done, 1)
            c.after(dve, nc.vector.tensor_copy(low_part[:, :], R.pp[0][:, 0:XTILES]))
            c.after(dve, nc.vector.scalar_tensor_tensor(out=T.tokens[:, 0:XTILES], in0=R.pp[1][:, 0:XTILES],
                                                        scalar=float(1 << LOW), in1=low_part[:, :],
                                                        op0=ALU.mult, op1=ALU.add))

        @block.tensor
        def _(pe):
            sort = SortPE(nc, pe, T, R)
            sort.open_count()
            cycle(NEXP, MASKS, pe, lambda b, k: sort.count(0, b, k))
            for j in range(4):
                sort.bases(0, j)
            cycle(NEXP, MASKS, pe, lambda b, k: sort.merge(0, b, k))
            sort.open_spread(0)
            pairs(R.n_group, pe, lambda g, k: sort.spread(0, g, PERX, k))
            sort.close_spread()


def experts(nc, A, T, E, s):
    ctx = ExitStack()
    with ctx:
        def sb(name, shape, dt=F32):
            return ctx.enter_context(nc.sbuf_tensor(name, shape, dt))
        w1, w2, b1, b2, twos = E.w1, E.w2, E.b1, E.b2, E.twos
        rows = sb("xrows", [P, RING, D])
        idx_st = sb("xidx", [P, RING], I32)
        xt = [sb(f"xt{n}", [P, 2, KD * P], F32R) for n in "hl"]
        act_h = sb("act_h", [P, 2, HID])
        ht = [sb(f"ht{n}", [P, 2, HID], F32R) for n in "hl"]
        y = sb("y", [P, 2, D])
        px = ctx.enter_context(nc.psum_tensor("epx", [P, 2, 512], F32))
        ph = ctx.enter_context(nc.psum_tensor("eph", [P, 2, 512], F32))
        pg = ctx.enter_context(nc.psum_tensor("epg", [P, 2, 512], F32))
        py = ctx.enter_context(nc.psum_tensor("epy", [P, 2, 512], F32))
        block = ctx.enter_context(nc.Block())
        y_ok = s("e_yok")
        idx_ok, tx, xhi, xlo, h_ok, g_ok, tg, hhi, hlo, y_mm = (
            s(f"e_{n}") for n in ("idx", "tx", "xhi", "xlo", "h", "g", "tg", "hhi", "hlo", "ymm"))
        got = [s(f"e_got{q}") for q in range(RING)]
        y_out = [s(f"e_yout{k}") for k in range(2)]
        ROUNDS = XTILES // RING

        def skewed(eng, *stages):
            lag = max(n for _, n in stages)
            for t in range(RING):
                for f, n in stages:
                    if t >= n:
                        f(t - n, (t - n) % RING)
            with eng.Fori(1, ROUNDS) as i:
                for q in range(RING):
                    for f, n in stages:
                        f(i * RING + (q - n), (q - n) % RING)
            for t in range(XTILES, XTILES + lag):
                for f, n in stages:
                    if t - n < XTILES:
                        f(t - n, (t - n) % RING)

        @block.sync
        def _(sp):
            def store(t, k):
                sp.wait_ge(y_ok, t + 3)
                sp.dma_start(A.y_dram[bass.ds(t * P, P), :], y[:, k, :]).then_inc(y_out[k], 16)
            pairs(XTILES, sp, store)
            for k in range(2):
                sp.wait_ge(y_out[k], 16 * (XTILES // 2))

        @block.gpsimd
        def _(pool):
            with pool.Fori(0, ROUNDS) as i:
                for q in range(RING):
                    t = i * RING + q
                    T.gate_pool.wait(pool, idx_ok, t + 1)
                    T.gate_pool.wait(pool, tx, t + 1)
                    nc.gpsimd.indirect_dma_start(
                        out=rows[:, q, :], out_offset=None, in_=A.x2_dram[:, :],
                        in_offset=bass.IndirectOffsetOnAxis(ap=idx_st[:, q:q + 1], axis=0)).then_inc(got[q], 16)

        @block.scalar
        def _(act):
            nc.scalar.copy(idx_st[:, :], T.tokens[:, 0:RING]).then_inc(idx_ok, RING)

            def split_x(t, q):
                act.wait_ge(tx, t + (RING + 1))
                act.wait_ge(h_ok, t + 1)
                nc.scalar.copy(xt[0][:, q % 2, :], px[:, q % 2, 0:KD * P]).then_inc(xhi, 1)
                nc.scalar.copy(idx_st[:, q:q + 1], T.tokens[:, bass.ds(t + RING, 1)]).then_inc(idx_ok, 1)

            def gelu(t, q):
                act.wait_ge(h_ok, t + 3)
                act.wait_ge(tg, t + 1)
                nc.scalar.activation(act_h[:, q % 2, :], ph[:, q % 2, :], ACT.Gelu).then_inc(g_ok, 1)

            def split_h(t, q):
                act.wait_ge(tg, t + 3)
                act.wait_ge(y_mm, t + 1)
                nc.scalar.copy(ht[0][:, q % 2, :], pg[:, q % 2, :]).then_inc(hhi, 1)
            skewed(act, (split_x, 0), (gelu, 1), (split_h, 2))

        @block.vector
        def _(dve):
            dve.sem_inc(tx, RING)
            for sem in (h_ok, tg, y_mm, xlo, g_ok, hlo, y_ok):
                dve.sem_inc(sem, 2)
            def low_x(t, q):
                dve.wait_ge(xhi, t + 1)
                nc.vector.tensor_tensor(xt[1][:, q % 2, :], px[:, q % 2, 0:KD * P],
                                        xt[0][:, q % 2, :].bitcast(F32), ALU.subtract).then_inc(xlo, 1)

            def low_h(t, q):
                dve.wait_ge(hhi, t + 1)
                nc.vector.tensor_tensor(ht[1][:, q % 2, :], pg[:, q % 2, :],
                                        ht[0][:, q % 2, :].bitcast(F32), ALU.subtract).then_inc(hlo, 1)

            def out(t, q):
                dve.wait_ge(y_mm, t + 3)
                if behind(t, 2):
                    dve.wait_ge(y_out[q % 2], (t - q % 2) * 8)
                nc.vector.tensor_copy(y[:, q % 2, :], py[:, q % 2, 0:D]).then_inc(y_ok, 1)
            skewed(dve, (low_x, 0), (low_h, 2), (out, 3))

        @block.tensor
        def _(pe):
            def load_expert(t):
                _, v = nc.values_load_multi_w_load_instructions(
                    T.xtable[0:1, bass.ds(t, 1)], engines=(mybir.EngineType.PE,), min_val=0, max_val=NEXP - 1,
                    skip_runtime_bounds_check_because="the table's values are clamped when it is made")
                return v[0]

            def turn_x(t, q):
                pe.wait_ge(got[q], got_value(t, q))
                pe.wait_ge(xlo, t + 1)
                for c in range(KD):
                    last = nc.tensor.transpose(px[:, q % 2, c * P:(c + 1) * P], rows[:, q, c * P:(c + 1) * P], T.ident[:, :])
                last.then_inc(tx, 1)

            def got_value(t, q):
                return (t - q) * (16 // RING) + 16

            def hidden(t, q):
                e = load_expert(t)
                pe.wait_ge(xlo, t + 3)
                pe.wait_ge(g_ok, t + 1)
                out, k = ph[:, q % 2, :], q % 2
                nc.tensor.matmul(out, twos[:, :], b1[:, bass.ds(e * HID, HID)], start=True, stop=False)
                for c in range(KD):
                    x_h, x_l = (xt[m][:, k, c * P:(c + 1) * P] for m in range(2))
                    w_h, w_l = (w1[m][:, bass.ds(e * (KD * HID) + c * HID, HID)] for m in range(2))
                    nc.tensor.matmul(out, x_h, w_h, start=False, stop=False)
                    nc.tensor.matmul(out, x_h, w_l, start=False, stop=False)
                    last = nc.tensor.matmul(out, x_l, w_h, start=False, stop=c == KD - 1)
                last.then_inc(h_ok, 1)

            def turn_h(t, q):
                pe.wait_ge(g_ok, t + 3)
                pe.wait_ge(hlo, t + 1)
                for c in range(KH):
                    last = nc.tensor.transpose(pg[:, q % 2, c * P:(c + 1) * P], act_h[:, q % 2, c * P:(c + 1) * P], T.ident[:, :])
                last.then_inc(tg, 1)

            def outputs(t, q):
                e = load_expert(t)
                pe.wait_ge(hlo, t + 3)
                pe.wait_ge(y_ok, t + 1)
                out, k = py[:, q % 2, 0:D], q % 2
                nc.tensor.matmul(out, twos[:, :], b2[:, bass.ds(e * D, D)], start=True, stop=False)
                for c in range(KH):
                    h_h, h_l = (ht[m][:, k, c * P:(c + 1) * P] for m in range(2))
                    w_h, w_l = (w2[m][:, bass.ds(e * (KH * D) + c * D, D)] for m in range(2))
                    nc.tensor.matmul(out, h_h, w_h, start=False, stop=False)
                    nc.tensor.matmul(out, h_h, w_l, start=False, stop=False)
                    last = nc.tensor.matmul(out, h_l, w_h, start=False, stop=c == KH - 1)
                last.then_inc(y_mm, 1)
            skewed(pe, (turn_x, 0), (hidden, 1), (turn_h, 2), (outputs, 3))


def combine(nc, A, T, s):
    ctx = ExitStack()
    with ctx:
        def sb(name, shape, dt=F32):
            return ctx.enter_context(nc.sbuf_tensor(name, shape, dt))
        NG = 7
        yy = sb("cy", [P, 2, 2, NG, D])
        x1 = sb("cx1", [P, 2, NG, D])
        block = ctx.enter_context(nc.Block())
        sum_ok, done = s("c_sum"), s("c_done")
        got, x_in, out_ok = ([s(f"c_{n}{k}") for k in range(2)] for n in ("got", "xin", "out"))
        rounds = NBLK // NG

        @block.gpsimd
        def _(pool):
            for i in range(rounds):
                if i >= 2:
                    pool.wait_ge(done, i - 1)
                for q in range(NG):
                    for j in range(2):
                        at = j * NBLK + i * NG + q
                        nc.gpsimd.indirect_dma_start(
                            out=yy[:, i % 2, j, q, :], out_offset=None, in_=A.y_dram[:, :],
                            in_offset=bass.IndirectOffsetOnAxis(ap=T.slot_of[:, at:at + 1], axis=0)).then_inc(got[i % 2], 16)

        @block.vector
        def _(dve):
            for i in range(rounds):
                k = i % 2
                dve.wait_ge(x_in[k], 16 * (i // 2 + 1))
                dve.wait_ge(got[k], (i // 2 + 1) * 2 * NG * 16)
                nc.vector.tensor_tensor(x1[:, k, :, :], x1[:, k, :, :], yy[:, k, 0, :, :], ALU.add).then_inc(sum_ok, 1)
                dve.wait_ge(sum_ok, i + 1)
                nc.vector.tensor_tensor(x1[:, k, :, :], x1[:, k, :, :], yy[:, k, 1, :, :], ALU.add).then_inc(done, 1)

        @block.sync
        def _(sp):
            def load(i):
                r = slice(i * NG * P, (i + 1) * NG * P)
                sp.dma_start(x1[:, i % 2, :, :], A.x1_dram[r, :].rearrange("(b p) f -> p b f", p=P)).then_inc(x_in[i % 2], 16)
            load(0)
            load(1)
            for i in range(rounds):
                k = i % 2
                sp.wait_ge(done, i + 1)
                full = NG if i < rounds - 1 else NG - 1
                sp.dma_start(A.out[i * NG * P:(i * NG + full) * P, :].rearrange("(b p) f -> p b f", p=P),
                             x1[:, k, 0:full, :]).then_inc(out_ok[k], 16)
                if i + 2 < rounds:
                    sp.wait_ge(out_ok[k], 16 * (i // 2 + 1))
                    load(i + 2)
            k = (rounds - 1) % 2
            sp.dma_start(A.out[(NBLK - 1) * P:NODES, :], x1[0:TAIL, k, NG - 1, :]).then_inc(out_ok[k], 16)
            for h in range(2):
                sp.wait_ge(out_ok[h], 16 * (len(range(h, rounds, 2)) + (h == k)))


class Names:
    pass


def gps_layer(nc, args):
    ctx = ExitStack()
    with ctx:
        A, T, W = Names(), Names(), Names()
        (A.x, A.src, A.dst, A.w_in, A.b_in, A.w_out, A.b_out, A.wih_t, A.b_ih, A.whh_t, A.b_hh) = (
            args[n] for n in "x src dst w_in b_in w_out b_out wih_t b_ih whh_t b_hh".split())
        (A.wq, A.bq, A.wk_t, A.bk, A.wv_t, A.bv, A.wfc_t, A.bfc, A.wg, A.bg, A.w1, A.b1, A.w2, A.b2, A.out) = (
            args[n] for n in "wq bq wk_t bk wv_t bv wfc_t bfc wg bg w1 b1 w2 b2 out".split())

        def sb(name, shape, dt=F32):
            return ctx.enter_context(nc.sbuf_tensor(name, shape, dt))

        def s(name):
            return ctx.enter_context(nc.semaphore(name))
        NP = NBLK * P
        T.gate_dve, T.gate_pe, T.gate_pool = (Gate(s(f"passed_{n}")) for n in ("dve", "pe", "pool"))
        A.x1_dram, A.x2_dram = (
            nc.dram_tensor(f"{n}_rows", [NP, D], F32).ap() for n in ("x1", "x2"))
        A.split_dram = nc.dram_tensor("split_rows", [NP, SPLIT], F32).ap()
        A.y_dram = nc.dram_tensor("y_rows", [XTILES * P, D], F32).ap()
        T.ident = sb("ident", [P, P])
        T.ident1 = sb("ident1", [P, P], F16)
        T.ident128 = sb("ident128", [P, P], F16)
        T.upper = sb("upper", [P, P], F16)
        T.colsel = sb("colsel", [P, 192], F16)
        T.ones16 = sb("ones16", [P, 16], F16)
        T.zeros16 = sb("zeros16", [P, 512], F16)
        T.ramp16 = sb("ramp16", [P, ETILES], F16)
        T.ramp32 = sb("ramp32", [P, P])
        T.mean2, T.rstd2, T.tmp2 = (sb(n, [P, NBLK]) for n in ("mean2", "rstd2", "tmp2"))
        T.expert = sb("expert", [P, 2 * NBLK])
        T.slot_of = sb("slot_of", [P, 2 * NBLK], I32)
        T.tokens = sb("tokens", [P, XTILES + RING], I32)
        T.xtable = sb("xtable", [1, XTILES], I32)
        with ExitStack() as blocks:
            def sb2(name, shape, dt=F32):
                return blocks.enter_context(nc.sbuf_tensor(name, shape, dt))
            W.hi = sb2("whi", [P, WCOLS], F32R)
            W.lo = sb2("wlo", [P, WCOLS], F32R)
            W.aux = sb2("waux", [6, GCOLS], F32R)
            with ExitStack() as first:
                T.ramp_i = first.enter_context(nc.sbuf_tensor("ramp_i", [P, ETILES], I32))
                T.gram = first.enter_context(nc.sbuf_tensor("gram", [P, 3, D + 1], F32))
                constants(nc, T, s)
                V = RawWeights(nc, first, s)
                normalise(nc, A, T, V, s)
                weights(nc, A, T, V, W, s)
            with ExitStack() as edges:
                def sb3(name, shape, dt=F32):
                    return edges.enter_context(nc.sbuf_tensor(name, shape, dt))
                acc = sb3("acc", [P, 2 * NBLK * ACOLS])
                aggregate(nc, A, T, acc, s)
                update(nc, A, T, W, acc, s)
                route(nc, A, T, acc, s)
        with ExitStack() as second:
            E = ExpertWeights(nc, second, s)
            sort_tokens(nc, A, T, E, s)
            experts(nc, A, T, E, s)
        combine(nc, A, T, s)


def kernel(**inputs):
    import numpy as _np
    import concourse.bacc as _bacc
    from concourse import mybir as _mybir
    from concourse.bass_utils import run_bass_kernel_spmd as _run

    names = {
        "x": ("x", 0), "src": ("src", 0), "dst": ("dst", 0),
        "w_in": ("L0_gnn_W_in", 0), "b_in": ("L0_gnn_b_in", 0), "w_out": ("L0_gnn_W_out", 0), "b_out": ("L0_gnn_b_out", 0),
        "wih_t": ("L0_gnn_W_ih", 1), "b_ih": ("L0_gnn_b_ih", 0), "whh_t": ("L0_gnn_W_hh", 1), "b_hh": ("L0_gnn_b_hh", 0),
        "wq": ("L0_mix_Wq", 0), "bq": ("L0_mix_bq", 0), "wk_t": ("L0_mix_Wk", 1), "bk": ("L0_mix_bk", 0),
        "wv_t": ("L0_mix_Wv", 1), "bv": ("L0_mix_bv", 0), "wfc_t": ("L0_mix_Wfc", 1), "bfc": ("L0_mix_bfc", 0),
        "wg": ("L0_ffn_Wg", 0), "bg": ("L0_ffn_bg", 0), "w1": ("L0_ffn_W1", 0), "b1": ("L0_ffn_b1", 0),
        "w2": ("L0_ffn_W2", 0), "b2": ("L0_ffn_b2", 0),
    }
    nc = _bacc.Bacc("TRN2", target_bir_lowering=False, num_devices=1)
    arrays, args = {}, {}
    for name, (given, turned) in names.items():
        a = _np.asarray(inputs[given])
        a = _np.ascontiguousarray(a.T if turned else a)
        arrays[f"in_{name}_dram"] = a
        args[name] = nc.dram_tensor(f"in_{name}_dram", a.shape, _mybir.dt.from_np(a.dtype), kind="ExternalInput").ap()
    args["out"] = nc.dram_tensor("out_0_dram", (NODES, D), _mybir.dt.float32, kind="ExternalOutput").ap()
    gps_layer(nc, args)
    r = _run(nc, [arrays], core_ids=[0])
    return r.results[0]["out_0_dram"]
```
